# Optimizing a Trainium2 kernel written in Bass

```python
import numpy as np
import jax
import jax.numpy as jnp

def _softmax(x, axis=-1):
    return jax.nn.softmax(x, axis=axis)

def _gelu(x):
    return jax.nn.gelu(x, approximate=True)

def _silu(x):
    return jax.nn.silu(x)

def _sigmoid(x):
    return jax.nn.sigmoid(x)

def _layernorm(x, axis=-1, eps=1e-05):
    m = jnp.mean(x, axis=axis, keepdims=True)
    v = jnp.var(x, axis=axis, keepdims=True)
    return (x - m) / jnp.sqrt(v + eps)

def _scatter_add(tgt, idx, src, axis=0):
    return tgt.at[idx].add(src)

def _segment_sum(src, seg, n):
    return jax.ops.segment_sum(src, seg, n)
kernel_name = 'mk_macaron_d2_jaxref_r8_0bfb4c'

def setup_inputs(seed: int=0):
    np.random.seed(seed)
    _w = jnp.asarray

    def _L0_attn_setup():
        import jax, jax.numpy as jnp
        import numpy as np
        import math
        DIM_MODEL = 128
        DIM_STATE = 128
        DIM_CONV = 4
        EXPAND = 2
        DIM_HEAD = 64
        NGROUPS = 1
        CHUNK = 32
        DIM_INNER = EXPAND * DIM_MODEL
        DIM_SSD = DIM_INNER
        NHEAD = DIM_SSD // DIM_HEAD
        D_IN_PROJ = 2 * DIM_INNER + 2 * NGROUPS * DIM_STATE + NHEAD
        CONV_DIM = DIM_SSD + 2 * NGROUPS * DIM_STATE
        EPS = 1e-05

        def _ssd(x, dt, A, Bm, Cm):
            b, L, h, p = x.shape
            n = Bm.shape[-1]
            c = L // CHUNK
            xc = x.reshape(b, c, CHUNK, h, p)
            dtc = dt.reshape(b, c, CHUNK, h)
            Bc = Bm.reshape(b, c, CHUNK, n)
            Cc = Cm.reshape(b, c, CHUNK, n)
            a = dtc * A
            A_cs = jnp.cumsum(a, axis=2)
            Lmat = jnp.exp(A_cs[:, :, :, None, :] - A_cs[:, :, None, :, :])
            causal = jnp.tril(jnp.ones((CHUNK, CHUNK), bool))
            Lmat = jnp.where(causal[None, None, :, :, None], Lmat, 0.0)
            CB = jnp.einsum('bcin,bcjn->bcij', Cc, Bc)
            scores = CB[..., None] * Lmat * dtc[:, :, None, :, :]
            y = jnp.einsum('bcijh,bcjhp->bcihp', scores, xc)
            decay_end = jnp.exp(A_cs[:, :, -1:, :] - A_cs)
            states = jnp.einsum('bcjh,bcjn,bcjhp->bchpn', dtc * decay_end, Bc, xc)
            chunk_decay = jnp.exp(A_cs[:, :, -1, :])

            def step(carry, inp):
                s, d = inp
                return (carry * d[:, :, None, None] + s, carry)
            init = jnp.zeros((b, h, p, n), x.dtype)
            _, prevs = jax.lax.scan(step, init, (jnp.moveaxis(states, 1, 0), jnp.moveaxis(chunk_decay, 1, 0)))
            prevs = jnp.moveaxis(prevs, 0, 1)
            y = y + jnp.einsum('bcin,bchpn->bcihp', Cc, prevs) * jnp.exp(A_cs)[..., None]
            return y.reshape(b, L, h, p)
        key = jax.random.key(seed)
        ks = jax.random.split(key, 8)
        B, L = (2, 512)
        u = jax.random.normal(ks[0], (B, L, DIM_MODEL), dtype=jnp.float32)
        in_proj_w = jax.random.normal(ks[1], (D_IN_PROJ, DIM_MODEL), dtype=jnp.float32) / np.sqrt(DIM_MODEL)
        conv_w = jax.random.normal(ks[2], (CONV_DIM, DIM_CONV), dtype=jnp.float32) / np.sqrt(DIM_CONV)
        conv_b = jnp.zeros((CONV_DIM,), jnp.float32)
        dt = jnp.exp(jax.random.uniform(ks[3], (NHEAD,)) * (math.log(0.1) - math.log(0.001)) + math.log(0.001))
        dt_bias = dt + jnp.log(-jnp.expm1(-dt))
        A_log = jnp.log(jax.random.uniform(ks[4], (NHEAD,), minval=1.0, maxval=16.0))
        D = jnp.ones((NHEAD,), jnp.float32)
        norm_w = jnp.ones((DIM_SSD,), jnp.float32)
        out_proj_w = jax.random.normal(ks[5], (DIM_MODEL, DIM_INNER), dtype=jnp.float32) / np.sqrt(DIM_INNER)
        return dict(u=u, in_proj_w=in_proj_w, conv_w=conv_w, conv_b=conv_b, dt_bias=dt_bias, A_log=A_log, D=D, norm_w=norm_w, out_proj_w=out_proj_w)
    _L0_attn_in = _L0_attn_setup()

    def _L0_ffn_setup():
        import jax, jax.numpy as jnp
        import numpy as np
        E, K, NG, TG = (64, 8, 8, 4)
        CAP = 128
        SCALE = 2.5

        def _route(x_flat, gate_weight, e_bias):
            T = x_flat.shape[0]
            logits = x_flat.astype(jnp.float32) @ gate_weight.astype(jnp.float32).T
            scores = jax.nn.sigmoid(logits)
            sfc = scores + e_bias[None, :]
            group_scores = jax.lax.top_k(sfc.reshape(T, NG, E // NG), 2)[0].sum(-1)
            _, gidx = jax.lax.top_k(group_scores, TG)
            gmask = jnp.zeros((T, NG), jnp.float32).at[jnp.arange(T)[:, None], gidx].set(1.0)
            smask = jnp.repeat(gmask, E // NG, axis=1)
            tmp = jnp.where(smask > 0, sfc, 0.0)
            _, topk_idx = jax.lax.top_k(tmp, K)
            topk_w = jnp.take_along_axis(scores, topk_idx, axis=1)
            topk_w = topk_w / (topk_w.sum(-1, keepdims=True) + 1e-20)
            return (topk_idx, topk_w * SCALE)

        def _moe_forward(hidden_states, gate_weight, e_bias, w1, w2, w3, shared_gate, shared_up, shared_down):
            B, S, H = hidden_states.shape
            T = B * S
            x = hidden_states.reshape(T, H)
            topk_idx, topk_w = _route(x, gate_weight, e_bias)
            Sk = T * K
            flat_e = topk_idx.reshape(-1)
            order = jnp.argsort(flat_e)
            sorted_e = flat_e[order]
            counts = jax.ops.segment_sum(jnp.ones((Sk,), jnp.int32), flat_e, num_segments=E)
            offsets = jnp.cumsum(counts) - counts
            pos = jnp.arange(Sk) - offsets[sorted_e]
            tok_sorted = x[order // K]
            xe = jnp.zeros((E, CAP, H), x.dtype).at[sorted_e, pos].set(tok_sorted, mode='drop')
            h = jax.nn.silu(jnp.einsum('ech,efh->ecf', xe, w1)) * jnp.einsum('ech,efh->ecf', xe, w3)
            ye = jnp.einsum('ecf,ehf->ech', h, w2)
            pos_c = jnp.minimum(pos, CAP - 1)
            vals = ye[sorted_e, pos_c]
            vals = jnp.where((pos < CAP)[:, None], vals, 0.0)
            flat_w = topk_w.reshape(-1)[order].astype(vals.dtype)
            flat_t = (jnp.arange(Sk) // K)[order]
            out = jax.ops.segment_sum(vals * flat_w[:, None], flat_t, num_segments=T)
            shared = jax.nn.silu(x @ shared_gate.T) * (x @ shared_up.T) @ shared_down.T
            return (out + shared).reshape(B, S, H)
        key = jax.random.key(seed)
        ks = jax.random.split(key, 9)
        B, S, H, F = (1, 256, 128, 64)
        bound = 1.0 / 32.0
        return {'hidden_states': jax.random.normal(ks[0], (B, S, H), jnp.float32), 'gate_weight': jax.random.uniform(ks[1], (E, H), jnp.float32, -bound, bound), 'e_bias': jnp.zeros((E,), jnp.float32), 'w1': jax.random.normal(ks[2], (E, F, H), jnp.float32) * 0.02, 'w2': jax.random.normal(ks[3], (E, H, F), jnp.float32) * 0.02, 'w3': jax.random.normal(ks[4], (E, F, H), jnp.float32) * 0.02, 'shared_gate': jax.random.normal(ks[5], (2 * F, H), jnp.float32) * 0.02, 'shared_up': jax.random.normal(ks[6], (2 * F, H), jnp.float32) * 0.02, 'shared_down': jax.random.normal(ks[7], (H, 2 * F), jnp.float32) * 0.02}
    _L0_ffn_in = _L0_ffn_setup()

    def _L1_attn_setup():
        import jax, jax.numpy as jnp
        import numpy as np
        B, T, D, H = (2, 256, 128, 16)
        HD = D // H
        key = jax.random.key(seed)
        ks = jax.random.split(key, 9)
        s = 1.0 / np.sqrt(D)
        return {'x': jax.random.normal(ks[0], (B, T, D), dtype=jnp.float32), 'Wq': jax.random.uniform(ks[1], (D, D), minval=-s, maxval=s, dtype=jnp.float32), 'bq': jax.random.uniform(ks[2], (D,), minval=-s, maxval=s, dtype=jnp.float32), 'Wk': jax.random.uniform(ks[3], (D, D), minval=-s, maxval=s, dtype=jnp.float32), 'bk': jax.random.uniform(ks[4], (D,), minval=-s, maxval=s, dtype=jnp.float32), 'Wv': jax.random.uniform(ks[5], (D, D), minval=-s, maxval=s, dtype=jnp.float32), 'bv': jax.random.uniform(ks[6], (D,), minval=-s, maxval=s, dtype=jnp.float32), 'Wo': jax.random.uniform(ks[7], (D, D), minval=-s, maxval=s, dtype=jnp.float32), 'bo': jax.random.uniform(ks[8], (D,), minval=-s, maxval=s, dtype=jnp.float32)}
    _L1_attn_in = _L1_attn_setup()

    def _L1_ffn_setup():
        import jax, jax.numpy as jnp
        import numpy as np
        DIM = 128
        HIDDEN = 384
        SCALE = 1.0 / 127.0

        def _dequant(w_int, dtype):
            return w_int.astype(dtype) * jnp.asarray(SCALE, dtype)
        key = jax.random.key(seed)
        k_x, k_g, k_u, k_d = jax.random.split(key, 4)
        x = jax.random.normal(k_x, (4, 256, DIM), dtype=jnp.float32)
        w_gate = jax.random.randint(k_g, (HIDDEN, DIM), -127, 128, dtype=jnp.int32)
        w_up = jax.random.randint(k_u, (HIDDEN, DIM), -127, 128, dtype=jnp.int32)
        w_down = jax.random.randint(k_d, (DIM, HIDDEN), -127, 128, dtype=jnp.int32)
        return {'x': x, 'w_gate': w_gate, 'w_up': w_up, 'w_down': w_down}
    _L1_ffn_in = _L1_ffn_setup()
    _d = {'L0_attn_u': _L0_attn_in['u'], 'L0_attn_in_proj_w': _L0_attn_in['in_proj_w'], 'L0_attn_conv_w': _L0_attn_in['conv_w'], 'L0_attn_conv_b': _L0_attn_in['conv_b'], 'L0_attn_dt_bias': _L0_attn_in['dt_bias'], 'L0_attn_A_log': _L0_attn_in['A_log'], 'L0_attn_D': _L0_attn_in['D'], 'L0_attn_norm_w': _L0_attn_in['norm_w'], 'L0_attn_out_proj_w': _L0_attn_in['out_proj_w'], 'L0_ffn_gate_weight': _L0_ffn_in['gate_weight'], 'L0_ffn_e_bias': _L0_ffn_in['e_bias'], 'L0_ffn_w1': _L0_ffn_in['w1'], 'L0_ffn_w2': _L0_ffn_in['w2'], 'L0_ffn_w3': _L0_ffn_in['w3'], 'L0_ffn_shared_gate': _L0_ffn_in['shared_gate'], 'L0_ffn_shared_up': _L0_ffn_in['shared_up'], 'L0_ffn_shared_down': _L0_ffn_in['shared_down'], 'L1_attn_Wq': _L1_attn_in['Wq'], 'L1_attn_bq': _L1_attn_in['bq'], 'L1_attn_Wk': _L1_attn_in['Wk'], 'L1_attn_bk': _L1_attn_in['bk'], 'L1_attn_Wv': _L1_attn_in['Wv'], 'L1_attn_bv': _L1_attn_in['bv'], 'L1_attn_Wo': _L1_attn_in['Wo'], 'L1_attn_bo': _L1_attn_in['bo'], 'L1_ffn_w_gate': _L1_ffn_in['w_gate'], 'L1_ffn_w_up': _L1_ffn_in['w_up'], 'L1_ffn_w_down': _L1_ffn_in['w_down']}
    _x0 = _d['L0_attn_u']
    _d['L0_attn_u'] = jax.random.normal(jax.random.fold_in(jax.random.key(seed), 1), (8, 512, 128), dtype=_x0.dtype)
    del _x0
    return _d

def reference(L0_attn_u, L0_attn_in_proj_w, L0_attn_conv_w, L0_attn_conv_b, L0_attn_dt_bias, L0_attn_A_log, L0_attn_D, L0_attn_norm_w, L0_attn_out_proj_w, L0_ffn_gate_weight, L0_ffn_e_bias, L0_ffn_w1, L0_ffn_w2, L0_ffn_w3, L0_ffn_shared_gate, L0_ffn_shared_up, L0_ffn_shared_down, L1_attn_Wq, L1_attn_bq, L1_attn_Wk, L1_attn_bk, L1_attn_Wv, L1_attn_bv, L1_attn_Wo, L1_attn_bo, L1_ffn_w_gate, L1_ffn_w_up, L1_ffn_w_down):

    def _L0_attn_ref(u, in_proj_w, conv_w, conv_b, dt_bias, A_log, D, norm_w, out_proj_w):
        import jax, jax.numpy as jnp
        import numpy as np
        import math
        DIM_MODEL = 128
        DIM_STATE = 128
        DIM_CONV = 4
        EXPAND = 2
        DIM_HEAD = 64
        NGROUPS = 1
        CHUNK = 32
        DIM_INNER = EXPAND * DIM_MODEL
        DIM_SSD = DIM_INNER
        NHEAD = DIM_SSD // DIM_HEAD
        D_IN_PROJ = 2 * DIM_INNER + 2 * NGROUPS * DIM_STATE + NHEAD
        CONV_DIM = DIM_SSD + 2 * NGROUPS * DIM_STATE
        EPS = 1e-05

        def _ssd(x, dt, A, Bm, Cm):
            b, L, h, p = x.shape
            n = Bm.shape[-1]
            c = L // CHUNK
            xc = x.reshape(b, c, CHUNK, h, p)
            dtc = dt.reshape(b, c, CHUNK, h)
            Bc = Bm.reshape(b, c, CHUNK, n)
            Cc = Cm.reshape(b, c, CHUNK, n)
            a = dtc * A
            A_cs = jnp.cumsum(a, axis=2)
            Lmat = jnp.exp(A_cs[:, :, :, None, :] - A_cs[:, :, None, :, :])
            causal = jnp.tril(jnp.ones((CHUNK, CHUNK), bool))
            Lmat = jnp.where(causal[None, None, :, :, None], Lmat, 0.0)
            CB = jnp.einsum('bcin,bcjn->bcij', Cc, Bc)
            scores = CB[..., None] * Lmat * dtc[:, :, None, :, :]
            y = jnp.einsum('bcijh,bcjhp->bcihp', scores, xc)
            decay_end = jnp.exp(A_cs[:, :, -1:, :] - A_cs)
            states = jnp.einsum('bcjh,bcjn,bcjhp->bchpn', dtc * decay_end, Bc, xc)
            chunk_decay = jnp.exp(A_cs[:, :, -1, :])

            def step(carry, inp):
                s, d = inp
                return (carry * d[:, :, None, None] + s, carry)
            init = jnp.zeros((b, h, p, n), x.dtype)
            _, prevs = jax.lax.scan(step, init, (jnp.moveaxis(states, 1, 0), jnp.moveaxis(chunk_decay, 1, 0)))
            prevs = jnp.moveaxis(prevs, 0, 1)
            y = y + jnp.einsum('bcin,bchpn->bcihp', Cc, prevs) * jnp.exp(A_cs)[..., None]
            return y.reshape(b, L, h, p)
        b, L, _ = u.shape
        zxbcdt = u @ in_proj_w.T
        z = zxbcdt[..., :DIM_SSD]
        xBC = zxbcdt[..., DIM_SSD:DIM_SSD + CONV_DIM]
        dt_raw = zxbcdt[..., DIM_SSD + CONV_DIM:]
        xp = jnp.pad(xBC, ((0, 0), (DIM_CONV - 1, 0), (0, 0)))
        xconv = conv_b + sum((conv_w[:, k] * xp[:, k:k + L, :] for k in range(DIM_CONV)))
        xBC = jax.nn.silu(xconv)
        x = xBC[..., :DIM_SSD]
        Bm = xBC[..., DIM_SSD:DIM_SSD + DIM_STATE]
        Cm = xBC[..., DIM_SSD + DIM_STATE:]
        dt = jax.nn.softplus(dt_raw + dt_bias)
        A = -jnp.exp(A_log)
        xh = x.reshape(b, L, NHEAD, DIM_HEAD)
        y = _ssd(xh, dt, A, Bm, Cm) + xh * D[:, None]
        y = y.reshape(b, L, DIM_SSD)
        y = y * jax.nn.silu(z)
        y = y * jax.lax.rsqrt(jnp.mean(y * y, axis=-1, keepdims=True) + EPS) * norm_w
        return y @ out_proj_w.T

    def _L0_ffn_ref(hidden_states, gate_weight, e_bias, w1, w2, w3, shared_gate, shared_up, shared_down):
        import jax, jax.numpy as jnp
        import numpy as np
        E, K, NG, TG = (64, 8, 8, 4)
        CAP = 128
        SCALE = 2.5

        def _route(x_flat, gate_weight, e_bias):
            T = x_flat.shape[0]
            logits = x_flat.astype(jnp.float32) @ gate_weight.astype(jnp.float32).T
            scores = jax.nn.sigmoid(logits)
            sfc = scores + e_bias[None, :]
            group_scores = jax.lax.top_k(sfc.reshape(T, NG, E // NG), 2)[0].sum(-1)
            _, gidx = jax.lax.top_k(group_scores, TG)
            gmask = jnp.zeros((T, NG), jnp.float32).at[jnp.arange(T)[:, None], gidx].set(1.0)
            smask = jnp.repeat(gmask, E // NG, axis=1)
            tmp = jnp.where(smask > 0, sfc, 0.0)
            _, topk_idx = jax.lax.top_k(tmp, K)
            topk_w = jnp.take_along_axis(scores, topk_idx, axis=1)
            topk_w = topk_w / (topk_w.sum(-1, keepdims=True) + 1e-20)
            return (topk_idx, topk_w * SCALE)

        def _moe_forward(hidden_states, gate_weight, e_bias, w1, w2, w3, shared_gate, shared_up, shared_down):
            B, S, H = hidden_states.shape
            T = B * S
            x = hidden_states.reshape(T, H)
            topk_idx, topk_w = _route(x, gate_weight, e_bias)
            Sk = T * K
            flat_e = topk_idx.reshape(-1)
            order = jnp.argsort(flat_e)
            sorted_e = flat_e[order]
            counts = jax.ops.segment_sum(jnp.ones((Sk,), jnp.int32), flat_e, num_segments=E)
            offsets = jnp.cumsum(counts) - counts
            pos = jnp.arange(Sk) - offsets[sorted_e]
            tok_sorted = x[order // K]
            xe = jnp.zeros((E, CAP, H), x.dtype).at[sorted_e, pos].set(tok_sorted, mode='drop')
            h = jax.nn.silu(jnp.einsum('ech,efh->ecf', xe, w1)) * jnp.einsum('ech,efh->ecf', xe, w3)
            ye = jnp.einsum('ecf,ehf->ech', h, w2)
            pos_c = jnp.minimum(pos, CAP - 1)
            vals = ye[sorted_e, pos_c]
            vals = jnp.where((pos < CAP)[:, None], vals, 0.0)
            flat_w = topk_w.reshape(-1)[order].astype(vals.dtype)
            flat_t = (jnp.arange(Sk) // K)[order]
            out = jax.ops.segment_sum(vals * flat_w[:, None], flat_t, num_segments=T)
            shared = jax.nn.silu(x @ shared_gate.T) * (x @ shared_up.T) @ shared_down.T
            return (out + shared).reshape(B, S, H)
        return _moe_forward(hidden_states, gate_weight, e_bias, w1, w2, w3, shared_gate, shared_up, shared_down)

    def _L1_attn_ref(x, Wq, bq, Wk, bk, Wv, bv, Wo, bo):
        import jax, jax.numpy as jnp
        import numpy as np
        B, T, D, H = (2, 256, 128, 16)
        HD = D // H
        b, t, d = x.shape

        def split_heads(y):
            return y.reshape(b, t, H, HD).transpose(0, 2, 1, 3)
        Q = split_heads(x @ Wq.T + bq)
        K = split_heads(x @ Wk.T + bk)
        V = split_heads(x @ Wv.T + bv)
        Z = jnp.einsum('bhsp,bhsn->bhspn', V, K)
        Z_cum = jnp.cumsum(Z, axis=2)
        Y = jnp.einsum('bhtn,bhtpn->bhtp', Q, Z_cum)
        Y = Y.transpose(0, 2, 1, 3).reshape(b, t, d)
        return Y @ Wo.T + bo

    def _L1_ffn_ref(x, w_gate, w_up, w_down):
        import jax, jax.numpy as jnp
        import numpy as np
        DIM = 128
        HIDDEN = 384
        SCALE = 1.0 / 127.0

        def _dequant(w_int, dtype):
            return w_int.astype(dtype) * jnp.asarray(SCALE, dtype)
        wg = _dequant(w_gate, x.dtype)
        wu = _dequant(w_up, x.dtype)
        wd = _dequant(w_down, x.dtype)
        gate = jnp.einsum('bsd,hd->bsh', x, wg)
        up = jnp.einsum('bsd,hd->bsh', x, wu)
        h = jax.nn.silu(gate) * up
        return jnp.einsum('bsh,dh->bsd', h, wd)
    x = L0_attn_u
    x = x + 0.5 * _L0_ffn_ref(_layernorm(x, axis=-1), L0_ffn_gate_weight, L0_ffn_e_bias, L0_ffn_w1, L0_ffn_w2, L0_ffn_w3, L0_ffn_shared_gate, L0_ffn_shared_up, L0_ffn_shared_down)
    x = x + _L0_attn_ref(_layernorm(x, axis=-1), L0_attn_in_proj_w, L0_attn_conv_w, L0_attn_conv_b, L0_attn_dt_bias, L0_attn_A_log, L0_attn_D, L0_attn_norm_w, L0_attn_out_proj_w)
    x = x + 0.5 * _L0_ffn_ref(_layernorm(x, axis=-1), L0_ffn_gate_weight, L0_ffn_e_bias, L0_ffn_w1, L0_ffn_w2, L0_ffn_w3, L0_ffn_shared_gate, L0_ffn_shared_up, L0_ffn_shared_down)
    x = x + 0.5 * _L1_ffn_ref(_layernorm(x, axis=-1), L1_ffn_w_gate, L1_ffn_w_up, L1_ffn_w_down)
    x = x + _L1_attn_ref(_layernorm(x, axis=-1), L1_attn_Wq, L1_attn_bq, L1_attn_Wk, L1_attn_bk, L1_attn_Wv, L1_attn_bv, L1_attn_Wo, L1_attn_bo)
    x = x + 0.5 * _L1_ffn_ref(_layernorm(x, axis=-1), L1_ffn_w_gate, L1_ffn_w_up, L1_ffn_w_down)
    return x

_drawn_inputs = setup_inputs


def setup_inputs(seed=0):
    import zlib

    import numpy as np

    out = dict(_drawn_inputs(seed))
    spreads = {'L0_attn_conv_b': (0.0, 0.1),
     'L0_attn_D': (1.0, 0.2),
     'L0_attn_norm_w': (1.0, 0.2),
     'L0_ffn_e_bias': (0.0, 0.8)}
    factors = {'L0_ffn_gate_weight': 8.0,
     'L0_ffn_w1': 8.0,
     'L0_ffn_w2': 8.0,
     'L0_ffn_w3': 8.0,
     'L0_ffn_shared_gate': 6.678,
     'L0_ffn_shared_up': 6.601,
     'L0_ffn_shared_down': 6.55,
     'L1_attn_bq': 6.72,
     'L1_attn_bk': 5.841,
     'L1_attn_bv': 7.017,
     'L1_attn_bo': 64.0}
    for name, (base, spread) in spreads.items():
        noise = np.random.default_rng([zlib.crc32(name.encode()), seed]).standard_normal(out[name].shape)
        drawn = base * np.exp(spread * noise) if base else spread * noise
        out[name] = jnp.asarray(drawn.astype(out[name].dtype))
    for name, factor in factors.items():
        out[name] = (out[name] * factor).astype(out[name].dtype)
    return out
```

```python
from contextlib import ExitStack

import concourse.bass as bass
from concourse import mybir

ALU = mybir.AluOpType
ACT = mybir.ActivationFunctionType
AX_X = mybir.AxisListType.X
F32 = mybir.dt.float32
BF16 = mybir.dt.bfloat16
I32 = mybir.dt.int32
U32 = mybir.dt.uint32

P = 128
SEQS = 8
TILES = 4
NT = SEQS * TILES
T = NT * P
SEQ = TILES * P
EPS = 1e-5

E = 64
CAP = 128
TOPK = 8
GROUPS = 8
TOP_GROUPS = 4
ROW = P + E
HI, LO = 8, 16
EG = P // HI
CHAINS = 2

HIDDEN = 384
HM = HIDDEN // P
QSCALE = 1.0 / 127.0

D_IN = 256
HEADS = 4
HD = D_IN // HEADS
ZDT = D_IN + HEADS
TAPS = 4

AH = 16
AD = P // AH


def pairs(eng, n, peel_first=False):
    if peel_first:
        yield 0, 0, 0
        yield 1, 1, 0
    with eng.Fori(1 if peel_first else 0, n // 2 - 1) as i:
        yield 2 * i, 0, i
        yield 2 * i + 1, 1, i
    yield n - 2, 0, n // 2 - 1
    yield n - 1, 1, n // 2 - 1


def is_last(b, n):
    return isinstance(b, int) and b == n - 1


def reaches(b, n):
    return not isinstance(b, int) or b >= n


def span(first, n):
    return bass.ds(first, n)


class Chain:

    def __init__(self, eng, sem, per_step=0):
        self.eng, self.sem, self.per_step, self.base, self.n = eng, sem, per_step, 0, 0

    def step(self, b):
        if self.n:
            assert self.n == self.per_step, (self.n, self.per_step)
        self.base, self.n = b * self.per_step, 0

    def link(self, ins):
        self.n += 1
        ins.then_inc(self.sem, 1)
        self.eng.wait_ge(self.sem, self.base + self.n)


NORM_LINKS = 2


def moments(dve, chain, x, b, w):
    for k in range(TILES):
        last = dve.bn_stats(w.stats[:, k, :], x[:, span(b * TILES + k, 1), :].rearrange("p a c -> p (a c)"))
    chain.link(last)
    dve.sem_inc(w.passed, 1)
    for k in range(TILES):
        last = dve.bn_aggr(w.mv[:, k, :], w.stats[:, k, :])
    chain.link(last)
    return dve.tensor_scalar(w.var[:, :], w.mv[:, :, 1], EPS, None, ALU.add)


def inverse_roots(pool, c, w, var_ready, rstd_ready):
    for b, p, i in pairs(pool, SEQS):
        pool.wait_ge(var_ready, b + 1)
        pool.tensor_tensor(w[p].rstd[:, :], w[p].var[:, :], c.minus_half[:, :], ALU.pow).then_inc(rstd_ready, 1)


def normalise(dve, x, b, w, rstd_ready):
    dve.wait_ge(rstd_ready, b + 1)
    for k in range(TILES):
        last = dve.tensor_scalar(w.xn[:, k, :], x[:, span(b * TILES + k, 1), :].rearrange("p a c -> p (a c)"),
                                 w.mv[:, k, 0:1], w.rstd[:, k:k + 1], ALU.subtract, ALU.mult)
    return last


class Bag(dict):

    def __getattr__(self, n):
        return self[n]

    def __setattr__(self, n, v):
        self[n] = v


def norm_buffers(sb, sem, name):
    out = []
    passed = sem(f"{name}_passed")
    for p in range(2):
        w = Bag()
        w.passed = passed
        w.stats = sb(f"{name}_stats{p}", [P, TILES, 6], F32)
        w.mv = sb(f"{name}_mv{p}", [P, TILES, 2], F32)
        w.var = sb(f"{name}_var{p}", [P, TILES], F32)
        w.rstd = sb(f"{name}_rstd{p}", [P, TILES], F32)
        w.xn = sb(f"{name}_xn{p}", [P, TILES, P], F32)
        out.append(w)
    return out


def constants(nc, c):
    with nc.semaphore("const_made") as made, nc.semaphore("const_masked") as masked, nc.Block() as block:
        @block.gpsimd
        def _(pool):
            ch = Chain(pool, made)
            ch.link(pool.memset(c.ident[:, :], 0.0))
            ch.link(pool.affine_select(out=c.ident[:, :], in_=c.ident[:, :], compare_op=ALU.not_equal, fill=1.0,
                                       base=0, pattern=[[-1, P]], channel_multiplier=1))
            ch.link(pool.memset(c.ones[:, :], 1.0))
            ch.link(pool.memset(c.ones_bf[:, :], 1.0))
            ch.link(pool.affine_select(out=c.before_bf[:, :], in_=c.ones_bf[:, :], compare_op=ALU.is_gt, fill=0.0,
                                       base=0, pattern=[[1, P]], channel_multiplier=-1))
            ch.link(pool.affine_select(out=c.upto[:, :], in_=c.ones[:, :], compare_op=ALU.is_ge, fill=0.0,
                                       base=0, pattern=[[1, P]], channel_multiplier=-1))
            ch.link(pool.memset(c.earlier_group[:, :, :], 1.0))
            ch.link(pool.affine_select(out=c.earlier_group[:, :, :], in_=c.earlier_group[:, :, :],
                                       compare_op=ALU.is_gt, fill=0.0, base=0,
                                       pattern=[[1, GROUPS], [-1, GROUPS]], channel_multiplier=0))
            ch.link(pool.iota(c.ramp_i[:, :], pattern=[[1, LO]], base=0, channel_multiplier=0))
            ch.link(pool.tensor_copy(c.lo_digit[:, :], c.ramp_i[:, :]))
            ch.link(pool.iota(c.ramp_i[:, :], pattern=[[1, LO]], base=-T // LO, channel_multiplier=0))
            ch.link(pool.tensor_copy(c.hi_digit[:, :], c.ramp_i[:, 0:HI]))
            ch.link(pool.iota(c.part_i[:, :], pattern=[[0, 1]], base=1, channel_multiplier=1))
            ch.link(pool.tensor_copy(c.part1[:, :], c.part_i[:, :]))
            ch.link(pool.iota(c.tile_i[:, :], pattern=[[P, NT]], base=0, channel_multiplier=0))
            ch.link(pool.tensor_copy(c.tile128[:, :], c.tile_i[:, :]))
            ch.link(pool.memset(c.own[:, :], 1.0))
            ch.link(pool.affine_select(out=c.own[:, :], in_=c.own[:, :], compare_op=ALU.is_ge, fill=0.0,
                                       base=0, pattern=[[-HI, EG]], channel_multiplier=1))
            ch.link(pool.affine_select(out=c.own[:, :], in_=c.own[:, :], compare_op=ALU.is_ge, fill=0.0,
                                       base=HI - 1, pattern=[[HI, EG]], channel_multiplier=-1))
            ch.link(pool.iota(c.slot_i[:, :], pattern=[[1, LO]], base=0, channel_multiplier=LO))
            ch.link(pool.memset(c.head_block[:, :], 1.0))
            hb = c.head_block[:, :].rearrange("p (h d) -> p h d", d=AD)
            ch.link(pool.affine_select(out=hb, in_=hb, compare_op=ALU.is_ge, fill=0.0,
                                       base=0, pattern=[[-AD, AH], [0, AD]], channel_multiplier=1))
            ch.link(pool.affine_select(out=hb, in_=hb, compare_op=ALU.is_ge, fill=0.0,
                                       base=AD - 1, pattern=[[AD, AH], [0, AD]], channel_multiplier=-1))

        @block.vector
        def _(dve):
            dve.memset(c.zero_bf[:, :], 0.0)
            dve.memset(c.minus_half[:, :], -0.5)
            dve.memset(c.eps[:, :], EPS)
            dve.wait_ge(made, 20)
            dve.tensor_scalar(c.slot_m[:, :], c.slot_i[:, :], CAP - 1, None, ALU.bitwise_and).then_inc(masked, 1)
            dve.wait_ge(masked, 1)
            dve.tensor_scalar(c.empty_row[:, :], c.slot_m[:, :], float(T + 1), None, ALU.add)


def ffn_layer(nc, name, sb_, x, c, weights, blocks, gate_scale, out_scale, moe=None):
    with ExitStack() as ctx:
        def sb(n, shape, dt):
            return ctx.enter_context(nc.sbuf_tensor(f"{name}_{n}", shape, dt))

        def sem(n):
            return ctx.enter_context(nc.semaphore(f"{name}_{n}"))

        def bank(n):
            return ctx.enter_context(nc.psum_tensor(f"{name}_{n}", [P, 512], F32))

        w = norm_buffers(sb, sem, "norm")
        xT = [sb(f"xT{p}", [P, SEQ], F32) for p in range(2)]
        sil = [sb(f"sil{p}", [P, SEQ], F32) for p in range(2)]
        h = sb("h", [P, blocks, SEQ], F32)
        turned = bank("turned")
        gate = [bank(f"gate{p}") for p in range(2)]
        up = [bank(f"up{p}") for p in range(2)]
        down = bank("down")
        chain_sem, normed, turned_up, xT_ready = sem("chain"), sem("normed"), sem("turned_up"), sem("xT_ready")
        gate_ready, up_ready, sil_ready, h_ready, down_ready = (
            sem("gate_ready"), sem("up_ready"), sem("sil_ready"), sem("h_ready"), sem("down_ready"))
        var_ready, rstd_ready, table_written = (
            sem("var_ready"), sem("rstd_ready"), [sem(f"table_written{p}") for p in range(2)])
        logits_ready, logits_kept = sem("logits_ready"), sem("logits_kept")
        if moe:
            logits = bank("logits")
        block = ctx.enter_context(nc.Block())
        wg, wu, wd = weights

        @block.gpsimd
        def _(pool):
            inverse_roots(pool, c, w, var_ready, rstd_ready)

        @block.vector
        def _(dve):
            chain = Chain(dve, chain_sem, NORM_LINKS)
            dve.sem_inc(h_ready, 2)
            moments(dve, chain, x, 0, w[0]).then_inc(var_ready, 1)
            normalise(dve, x, 0, w[0], rstd_ready).then_inc(normed, 1)
            for b, p, i in pairs(dve, SEQS):
                if not is_last(b, SEQS):
                    chain.step(b + 1)
                    moments(dve, chain, x, b + 1, w[1 - p]).then_inc(var_ready, 1)
                for m in range(blocks):
                    dve.wait_ge(sil_ready, b * blocks + m + 1)
                    dve.wait_ge(up_ready, b * blocks + m + 1)
                    q = (blocks * p + m) % 2
                    dve.scalar_tensor_tensor(out=h[:, m, :], in0=up[q][:, :], scalar=gate_scale, in1=sil[q][:, :],
                                             op0=ALU.mult, op1=ALU.mult).then_inc(h_ready, 1)
                    if m == 0 and not is_last(b, SEQS):
                        if moe:
                            dve.wait_ge(table_written[1 - p], i * 16 + 16)
                        normalise(dve, x, b + 1, w[1 - p], rstd_ready).then_inc(normed, 1)
                dve.wait_ge(down_ready, b + 1)
                xs = x[:, span(b * TILES, TILES), :].rearrange("p a c -> p (a c)")
                dve.scalar_tensor_tensor(out=xs, in0=down[:, :], scalar=out_scale, in1=xs,
                                         op0=ALU.mult, op1=ALU.add)

        @block.tensor
        def _(pe):
            def turn(b, p):
                pe.wait_ge(normed, b + 1)
                for k in range(TILES):
                    last = pe.transpose(turned[:, k * P:(k + 1) * P], w[p].xn[:, k, :], c.ident[:, :])
                last.then_inc(turned_up, 1)

            turn(0, 0)
            for b, p, i in pairs(pe, SEQS):
                pe.wait_ge(xT_ready, b + 1)
                if moe:
                    pe.wait_ge(logits_kept, b + 1)
                    for k in range(TILES):
                        last = pe.matmul(logits[:, k * E:(k + 1) * E], xT[p][:, k * P:(k + 1) * P], moe.gate[:, :],
                                         start=True, stop=True)
                    last.then_inc(logits_ready, 1)
                for m in range(blocks):
                    q = (blocks * p + m) % 2
                    pe.wait_ge(h_ready, b * blocks + m + 1)
                    pe.matmul(gate[q][:, :], wg[:, m * P:(m + 1) * P], xT[p][:, :],
                              start=True, stop=True).then_inc(gate_ready, 1)
                    pe.matmul(up[q][:, :], wu[:, m * P:(m + 1) * P], xT[p][:, :],
                              start=True, stop=True).then_inc(up_ready, 1)
                if not is_last(b, SEQS):
                    turn(b + 1, 1 - p)
                pe.wait_ge(h_ready, b * blocks + blocks + 2)
                for k in range(TILES):
                    for m in range(blocks):
                        last = pe.matmul(down[:, k * P:(k + 1) * P], h[:, m, k * P:(k + 1) * P], wd[:, m, :],
                                         start=(m == 0), stop=(m == blocks - 1))
                last.then_inc(down_ready, 1)

        @block.scalar
        def _(act):
            def keep(b, p):
                act.wait_ge(turned_up, b + 1)
                act.activation(xT[p][:, :], turned[:, :], ACT.Copy).then_inc(xT_ready, 1)

            if moe:
                act.sem_inc(logits_kept, 1)
            keep(0, 0)
            for b, p, i in pairs(act, SEQS):
                if moe:
                    act.wait_ge(logits_ready, b + 1)
                    act.activation(moe.logits[:, span(b * TILES, TILES), :].rearrange("p a e -> p (a e)"),
                                   logits[:, 0:TILES * E], ACT.Copy).then_inc(logits_kept, 1)
                for m in range(blocks):
                    q = (blocks * p + m) % 2
                    act.wait_ge(gate_ready, b * blocks + m + 1)
                    act.activation(sil[q][:, :], gate[q][:, :], ACT.Silu, scale=gate_scale).then_inc(sil_ready, 1)
                if not is_last(b, SEQS):
                    keep(b + 1, 1 - p)

        if moe:
            @block.sync
            def _(sp):
                sp.sem_inc(table_written[1], 16)
                rows = moe.table[0:T, :].rearrange("(a p) c -> p a c", p=P)
                for b, p, i in pairs(sp, SEQS):
                    sp.wait_ge(normed, b + 1)
                    sp.dma_start(rows[:, span(b * TILES, TILES), 0:P], w[p].xn[:, :, :]).then_inc(table_written[p], 16)
                sp.wait_ge(table_written[0], SEQS // 2 * 16)
                sp.wait_ge(table_written[1], SEQS // 2 * 16 + 16)


def route(nc, name, c, moe):
    with ExitStack() as ctx:
        def sb(n, shape, dt):
            return ctx.enter_context(nc.sbuf_tensor(f"{name}_{n}", shape, dt))

        def sem(n):
            return ctx.enter_context(nc.semaphore(f"{name}_{n}"))

        def bank(n):
            return ctx.enter_context(nc.psum_tensor(f"{name}_{n}", [P, 512], F32))

        score = sb("score", [P, NT, E], F32)
        choice = sb("choice", [P, NT, E], F32)
        left = sb("left", [P, NT, E], F32)
        pick = sb("pick", [P, NT, E], BF16)
        ahead = sb("ahead", [P, NT, E], BF16)
        hi8 = sb("hi8", [P, NT, GROUPS, 4], F32)
        lo8 = sb("lo8", [P, NT, GROUPS, 4], F32)
        hi4 = sb("hi4", [P, NT, GROUPS, 2], F32)
        lo4 = sb("lo4", [P, NT, GROUPS, 2], F32)
        lo4b = sb("lo4b", [P, NT, GROUPS, 2], F32)
        g1, g2, g3 = (sb(f"g{k}", [P, NT, GROUPS], F32) for k in range(3))
        beats = sb("beats", [P, NT, GROUPS, GROUPS], F32)
        ties = sb("ties", [P, NT, GROUPS, GROUPS], F32)
        top = sb("top", [P, NT, TOPK], F32)
        total = sb("total", [P, NT], F32)
        inv = sb("inv", [P, NT], F32)
        inv2 = sb("inv2", [P, NT], F32)
        place = sb("place", [P, NT, E], I32)
        hi = sb("hi", [P, NT, E], I32)
        lo = sb("lo", [P, NT, E], I32)
        is_hi = [sb(f"is_hi{p}", [P, E, HI], BF16) for p in range(2)]
        is_lo = [sb(f"is_lo{p}", [P, E, LO], BF16) for p in range(2)]
        part_lo = [sb(f"part_lo{p}", [P, E, LO], BF16) for p in range(2)]
        tile_lo = [sb(f"tile_lo{p}", [P, E, LO], BF16) for p in range(2)]
        found = sb("found", [P, E // EG, LO], F32)
        empty = sb("empty", [P, E // EG, LO], F32)
        own_part = sb("own_part", [P, LO, EG], F32)
        by_expert = sb("by_expert", [E, CAP], F32)

        counts = [bank(f"counts{k}") for k in range(4)]
        slots = [bank(f"slots{k}") for k in range(4)]
        chain_sem, scored, picked, counted = sem("chain"), sem("scored"), sem("picked"), sem("counted")
        weights_written, low_ready, low_used, rows_found = (
            sem("weights_written"), sem("low_ready"), sem("low_used"), sem("rows_found"))
        rows_written, rows_read, rows_turned = sem("rows_written"), sem("rows_read"), sem("rows_turned")
        weights_ready = sem("weights_ready")
        is_ready = sem("is_ready")
        block = ctx.enter_context(nc.Block())

        def flat(t):
            return t[:, :, :].rearrange("p a e -> p (a e)")

        def over_groups(t):
            return t[:, :, :].rearrange("p a (g e) -> p a g e", g=GROUPS)

        @block.scalar
        def _(act):
            act.activation(flat(score), flat(moe.logits), ACT.Sigmoid).then_inc(scored, 1)
            for j, p, i in pairs(act, NT):
                act.wait_ge(is_ready, j + 1)
                act.activation(flat(part_lo[p]), flat(is_lo[p]), ACT.Copy,
                               scale=c.part1[:, 0:1]).then_inc(low_ready, 1)
                act.activation(flat(tile_lo[p]), flat(is_lo[p]), ACT.Copy,
                               scale=c.tile128[:, span(j, 1)]).then_inc(low_ready, 1)
            act.wait_ge(rows_turned, 1)
            act.activation(moe.rows[:, :], slots[0][:, 0:E], ACT.Copy).then_inc(low_ready, 1)

        @block.vector
        def _(dve):
            ch = Chain(dve, chain_sem)
            dve.wait_ge(scored, 1)
            bias = moe.bias[:, :].rearrange("p (a e) -> p a e", a=1).broadcast_to([P, NT, E])
            ch.link(dve.tensor_tensor(choice[:, :, :], score[:, :, :], bias, ALU.add))
            v = over_groups(choice)
            dve.tensor_tensor(hi8[:, :, :, :], v[:, :, :, 0:4], v[:, :, :, 4:8], ALU.max)
            ch.link(dve.tensor_tensor(lo8[:, :, :, :], v[:, :, :, 0:4], v[:, :, :, 4:8], ALU.min))
            dve.tensor_tensor(hi4[:, :, :, :], hi8[:, :, :, 0:2], hi8[:, :, :, 2:4], ALU.max)
            dve.tensor_tensor(lo4[:, :, :, :], hi8[:, :, :, 0:2], hi8[:, :, :, 2:4], ALU.min)
            ch.link(dve.tensor_tensor(lo4b[:, :, :, :], lo8[:, :, :, 0:2], lo8[:, :, :, 2:4], ALU.max))
            ch.link(dve.tensor_tensor(lo4[:, :, :, :], lo4[:, :, :, :], lo4b[:, :, :, :], ALU.max))
            dve.tensor_tensor(g1[:, :, :], hi4[:, :, :, 0], hi4[:, :, :, 1], ALU.max)
            dve.tensor_tensor(g2[:, :, :], hi4[:, :, :, 0], hi4[:, :, :, 1], ALU.min)
            ch.link(dve.tensor_tensor(g3[:, :, :], lo4[:, :, :, 0], lo4[:, :, :, 1], ALU.max))
            ch.link(dve.tensor_tensor(g2[:, :, :], g2[:, :, :], g3[:, :, :], ALU.max))
            ch.link(dve.tensor_tensor(g1[:, :, :], g1[:, :, :], g2[:, :, :], ALU.add))
            shape = [P, NT, GROUPS, GROUPS]
            other = g1[:, :, :].rearrange("p a (o g) -> p a o g", o=1).broadcast_to(shape)
            self_ = g1[:, :, :].rearrange("p a (g o) -> p a g o", o=1).broadcast_to(shape)
            earlier = c.earlier_group[:, :, :].rearrange("p (o g) h -> p o g h", o=1).broadcast_to(shape)
            dve.tensor_tensor(beats[:, :, :, :], other, self_, ALU.is_gt)
            ch.link(dve.tensor_tensor(ties[:, :, :, :], other, self_, ALU.is_equal))
            ch.link(dve.tensor_tensor(ties[:, :, :, :], ties[:, :, :, :], earlier, ALU.mult))
            ch.link(dve.tensor_tensor(beats[:, :, :, :], beats[:, :, :, :], ties[:, :, :, :], ALU.add))
            ch.link(dve.tensor_reduce(g2[:, :, :], beats[:, :, :, :], AX_X, ALU.add))
            ch.link(dve.tensor_scalar(g3[:, :, :], g2[:, :, :], float(TOP_GROUPS), None, ALU.is_lt))
            kept = g3[:, :, :].rearrange("p a (g o) -> p a g o", o=1).broadcast_to([P, NT, GROUPS, E // GROUPS])
            ch.link(dve.tensor_tensor(v, v, kept, ALU.mult))
            for j in range(NT):
                last = dve.max(top[:, j, :], choice[:, j, :])
            ch.link(last)
            for j in range(NT):
                last = dve.match_replace(left[:, j, :], top[:, j, :], choice[:, j, :], -1e30)
            ch.link(last)
            ch.link(dve.tensor_tensor(flat(pick), flat(left), flat(choice), ALU.not_equal))
            ch.link(dve.memset(ahead[:, 0, :], 0.0))
            for j in range(1, NT):
                ch.link(dve.tensor_tensor(ahead[:, j, :], ahead[:, j - 1, :], pick[:, j - 1, :], ALU.add))
            dve.sem_inc(picked, 1)
            ch.link(dve.tensor_tensor(flat(score), flat(score), flat(pick), ALU.mult))
            ch.link(dve.tensor_reduce(total[:, :], score[:, :, :], AX_X, ALU.add))
            ch.link(dve.tensor_scalar(total[:, :], total[:, :], 1e-20, None, ALU.add))
            ch.link(dve.reciprocal(inv[:, :], total[:, :]))
            ch.link(dve.tensor_scalar(inv2[:, :], inv[:, :], 1.25, None, ALU.mult))
            dve.tensor_tensor(score[:, :, :], score[:, :, :],
                              inv2[:, :].rearrange("p (a o) -> p a o", o=1).broadcast_to([P, NT, E]),
                              ALU.mult).then_inc(weights_ready, 1)
            for k in range(4):
                dve.wait_ge(counted, k + 1)
                s = slice(8 * k, 8 * k + 8)
                last = dve.scalar_tensor_tensor(
                    out=place[:, s, :].rearrange("p a e -> p (a e)"),
                    in0=pick[:, s, :].rearrange("p a e -> p (a e)"), scalar=-float(T),
                    in1=counts[k][:, :], op0=ALU.mult, op1=ALU.add)
            ch.link(last)
            dve.tensor_scalar(flat(hi), flat(place), 4, None, ALU.arith_shift_right)
            ch.link(dve.tensor_scalar(flat(lo), flat(place), LO - 1, None, ALU.bitwise_and))
            for j, p, i in pairs(dve, NT):
                dve.wait_ge(low_used, j + 1)
                dve.tensor_tensor(is_hi[p][:, :, :],
                                  hi[:, span(j, 1), :].rearrange("p a (e o) -> p (a e) o", o=1).broadcast_to([P, E, HI]),
                                  c.hi_digit[:, :].rearrange("p (o h) -> p o h", o=1).broadcast_to([P, E, HI]),
                                  ALU.is_equal)
                dve.tensor_tensor(is_lo[p][:, :, :],
                                  lo[:, span(j, 1), :].rearrange("p a (e o) -> p (a e) o", o=1).broadcast_to([P, E, LO]),
                                  c.lo_digit[:, :].rearrange("p (o h) -> p o h", o=1).broadcast_to([P, E, LO]),
                                  ALU.is_equal).then_inc(is_ready, 1)
            dve.wait_ge(low_used, NT + 2)
            for g in range(E // EG):
                ch.link(dve.tensor_tensor(own_part[:, :, :],
                                          slots[g][:, 0:EG * LO].rearrange("p (e l) -> p l e", l=LO),
                                          c.own[:, :].rearrange("p (o e) -> p o e", o=1).broadcast_to([P, LO, EG]),
                                          ALU.mult))
                ch.link(dve.tensor_reduce(found[:, g, :], own_part[:, :, :], AX_X, ALU.add))
            ch.link(dve.tensor_scalar(flat(empty), flat(found), 0.0, None, ALU.is_equal))
            ch.link(dve.tensor_tensor(empty[:, :, :], empty[:, :, :],
                                      c.empty_row[:, :].rearrange("p (o l) -> p o l", o=1)
                                      .broadcast_to([P, E // EG, LO]), ALU.mult))
            dve.scalar_tensor_tensor(out=flat(found), in0=flat(found), scalar=-1.0, in1=flat(empty),
                                     op0=ALU.add, op1=ALU.add).then_inc(rows_found, 1)

        @block.tensor
        def _(pe):
            pe.wait_ge(picked, 1)
            for k in range(4):
                s = slice(8 * k, 8 * k + 8)
                pe.matmul(counts[k][:, :], c.before_bf[:, :], pick[:, s, :].rearrange("p a e -> p (a e)"),
                          start=True, stop=False)
                pe.matmul(counts[k][:, :], c.ones_bf[:, :], ahead[:, s, :].rearrange("p a e -> p (a e)"),
                          start=False, stop=True).then_inc(counted, 1)
            for g in range(E // EG):
                pe.matmul(slots[g][:, 0:EG * LO], c.zero_bf[:, 0:P], c.zero_bf[:, 0:EG * LO], start=True, stop=False,
                          skip_group_check=True)
            pe.sem_inc(low_used, 2)
            for j, p, i in pairs(pe, NT):
                pe.wait_ge(low_ready, 2 * j + 2)
                for g in range(E // EG):
                    lhs = is_hi[p][:, g * EG:(g + 1) * EG, :].rearrange("p e h -> p (e h)")
                    for rhs in (part_lo, tile_lo):
                        last = pe.matmul(slots[g][:, 0:EG * LO], lhs,
                                         rhs[p][:, g * EG:(g + 1) * EG, :].rearrange("p e l -> p (e l)"),
                                         start=False, stop=is_last(j, NT) and rhs is tile_lo, skip_group_check=True)
                last.then_inc(low_used, 1)
            pe.wait_ge(rows_read, 16)
            pe.transpose(slots[0][:, 0:E], by_expert[:, :], c.ident[0:E, 0:E]).then_inc(rows_turned, 1)

        @block.sync
        def _(sp):
            sp.wait_ge(weights_ready, 1)
            sp.dma_start(moe.table[0:T, :].rearrange("(a p) c -> p a c", p=P)[:, :, P:ROW],
                         score[:, :, :]).then_inc(weights_written, 16)
            sp.wait_ge(rows_found, 1)
            sp.dma_start(moe.row_list.rearrange("(g p l) -> p g l", p=P, l=LO), found[:, :, :]).then_inc(rows_written, 16)
            sp.wait_ge(rows_written, 16)
            sp.dma_start(by_expert[:, :], moe.row_list.rearrange("(e s) -> e s", s=CAP)).then_inc(rows_read, 16)
            sp.wait_ge(weights_written, 16)


def experts(nc, name, c, moe):
    n_pairs = E // 2
    with ExitStack() as ctx:
        def sb(n, shape, dt):
            return ctx.enter_context(nc.sbuf_tensor(f"{name}_{n}", shape, dt))

        def sem(n):
            return ctx.enter_context(nc.semaphore(f"{name}_{n}"))

        def bank(n):
            return ctx.enter_context(nc.psum_tensor(f"{name}_{n}", [P, 512], F32))

        row = [[sb(f"row{p}{k}", [P, 1], U32) for k in range(2)] for p in range(2)]
        row_out = [[sb(f"row_out{p}{k}", [P, 1], U32) for k in range(2)] for p in range(2)]
        xg = [[sb(f"xg{p}{k}", [P, ROW], F32) for k in range(2)] for p in range(2)]
        xgT = [sb(f"xgT{p}", [P, 2 * CAP], F32) for p in range(2)]
        w123 = [sb(f"w123{p}", [P, 3 * P], F32) for p in range(2)]
        sil = [sb(f"sil{p}", [P, CAP], F32) for p in range(2)]
        h = [sb(f"h{p}", [P, CAP], F32) for p in range(2)]
        y = [[sb(f"y{p}{k}", [P, P], F32) for k in range(2)] for p in range(2)]
        turned = [bank(f"turned{p}") for p in range(2)]
        gate_up = [bank(f"gate_up{p}") for p in range(2)]
        down = [[bank(f"down{p}{k}") for k in range(2)] for p in range(2)]
        row_staged, gathered, loaded = (
            sem("row_staged"), moe.gathered, [sem(f"loaded{p}") for p in range(2)])
        turned_up, xgT_ready, gate_ready, sil_ready, h_ready, down_ready, y_ready = (
            sem("turned_up"), sem("xgT_ready"), sem("gate_ready"), sem("sil_ready"), sem("h_ready"),
            sem("down_ready"), sem("y_ready"))
        passed = sem("passed")
        added = moe.added
        block = ctx.enter_context(nc.Block())

        @block.gpsimd
        def _(pool):
            def gather(r, p):
                pool.wait_ge(y_ready, 2 * r + 2)
                for k in range(2):
                    last = pool.tensor_copy(row[p][k][:, :], moe.rows[:, span(2 * r + k, 1)])
                last.then_inc(row_staged, 1)
                pool.wait_ge(row_staged, r + 1)
                pool.sem_inc(passed, 1)
                for k in range(2):
                    pool.indirect_dma_start(xg[p][k][:, :], None, moe.table[:, :],
                                            bass.IndirectOffsetOnAxis(ap=row[p][k][:, :], axis=0)
                                            ).then_inc(gathered[p], 16)

            pool.sem_inc(y_ready, 4)
            gather(0, 0)
            for r, p, i in pairs(pool, n_pairs, peel_first=True):
                if not is_last(r, n_pairs):
                    gather(r + 1, 1 - p)
                for k in range(2):
                    pool.wait_ge(y_ready, 2 * r + k + 5)
                    if reaches(r, 1):
                        pool.wait_ge(added[k], r * 16)
                        pool.sem_inc(passed, 1)
                    pool.indirect_dma_start(moe.sums[k][:, :],
                                            bass.IndirectOffsetOnAxis(ap=row_out[p][k][:, :], axis=0),
                                            y[p][k][:, :], None, compute_op=ALU.add).then_inc(added[k], 16)
            for k in range(CHAINS):
                pool.wait_ge(added[k], n_pairs * 16)

        @block.sync
        def _(sp):
            for r, p, i in pairs(sp, n_pairs):
                sp.wait_ge(y_ready, 2 * r + 2)
                sp.dma_start(w123[p][:, :], moe.w123[span(r, 1), :, :].rearrange("a p c -> (a p) c")
                             ).then_inc(loaded[p], 16)

        @block.tensor
        def _(pe):
            def turn(r, p, i):
                pe.wait_ge(gathered[p], 32 * i + 32)
                for k in range(2):
                    last = pe.transpose(turned[p][:, k * P:(k + 1) * P], xg[p][k][:, 0:P], c.ident[:, :])
                last.then_inc(turned_up, 1)

            turn(0, 0, 0)
            for r, p, i in pairs(pe, n_pairs):
                pe.wait_ge(xgT_ready, r + 1)
                pe.wait_ge(loaded[p], 16 * i + 16)
                for m in range(2):
                    for k in range(2):
                        last = pe.matmul(gate_up[p][k * E:(k + 1) * E, m * CAP:(m + 1) * CAP],
                                         w123[p][:, m * P + k * E:m * P + (k + 1) * E],
                                         xgT[p][:, k * CAP:(k + 1) * CAP], start=True, stop=True)
                last.then_inc(gate_ready, 1)
                if not is_last(r, n_pairs):
                    turn(r + 1, 1 - p, i + p)
                pe.wait_ge(h_ready, r + 1)
                for k in range(2):
                    last = pe.matmul(down[p][k][:, 0:P], h[p][k * E:(k + 1) * E, :],
                                     w123[p][k * E:(k + 1) * E, 2 * P:3 * P], start=True, stop=True)
                last.then_inc(down_ready, 1)

        @block.scalar
        def _(act):
            def keep(r, p):
                act.wait_ge(turned_up, r + 1)
                act.activation(xgT[p][:, :], turned[p][:, 0:2 * P], ACT.Copy).then_inc(xgT_ready, 1)

            keep(0, 0)
            for r, p, i in pairs(act, n_pairs):
                act.wait_ge(gate_ready, r + 1)
                act.activation(sil[p][:, :], gate_up[p][:, 0:CAP], ACT.Silu).then_inc(sil_ready, 1)
                if not is_last(r, n_pairs):
                    keep(r + 1, 1 - p)

        @block.vector
        def _(dve):
            for r, p, i in pairs(dve, n_pairs, peel_first=True):
                dve.wait_ge(sil_ready, r + 1)
                dve.tensor_tensor(h[p][:, :], gate_up[p][:, CAP:2 * CAP], sil[p][:, :], ALU.mult).then_inc(h_ready, 1)
                dve.wait_ge(down_ready, r + 1)
                for k in range(2):
                    if reaches(r, 2):
                        dve.wait_ge(added[k], 16 * (r - 1))
                    dve.tensor_copy(row_out[p][k][:, :], moe.rows[:, span(2 * r + k, 1)])
                    dve.tensor_scalar(y[p][k][:, :], down[p][k][:, 0:P],
                                      xg[p][k][:, span(P + 2 * r + k, 1)], None, ALU.mult).then_inc(y_ready, 1)


def combine(nc, name, x, moe):
    with ExitStack() as ctx:
        part = [[ctx.enter_context(nc.sbuf_tensor(f"{name}_part{p}{k}", [P, TILES, P], F32)) for k in range(CHAINS)]
                for p in range(2)]
        loaded = [ctx.enter_context(nc.semaphore(f"{name}_loaded{p}")) for p in range(2)]
        joined = ctx.enter_context(nc.semaphore(f"{name}_joined"))
        block = ctx.enter_context(nc.Block())

        @block.sync
        def _(sp):
            for b, p, i in pairs(sp, SEQS):
                sp.wait_ge(joined, 2 * b + 2)
                for k in range(CHAINS):
                    sp.dma_start(part[p][k][:, :, :], moe.sums[k][0:T, :].rearrange("(a p) c -> p a c", p=P)
                                 [:, span(b * TILES, TILES), :]).then_inc(loaded[p], 16)

        @block.vector
        def _(dve):
            dve.sem_inc(joined, 4)
            for b, p, i in pairs(dve, SEQS):
                dve.wait_ge(loaded[p], 16 * CHAINS * i + 16 * CHAINS)
                xs = x[:, span(b * TILES, TILES), :]
                for k in range(CHAINS):
                    dve.tensor_tensor(xs, xs, part[p][k][:, :, :], ALU.add).then_inc(joined, 1)
                    dve.wait_ge(joined, 2 * b + k + 5)



DT_LINKS = 15
STEP_LINKS = NORM_LINKS + DT_LINKS
Y_LINKS = 2 + 3 * TILES


def state_space(nc, x, c, d):
    with ExitStack() as ctx:
        def sb(n, shape, dt=F32):
            return ctx.enter_context(nc.sbuf_tensor(f"ssm_{n}", shape, dt))

        def sem(n):
            return ctx.enter_context(nc.semaphore(f"ssm_{n}"))

        def bank(n):
            return ctx.enter_context(nc.psum_tensor(f"ssm_{n}", [P, 512], F32))

        KH = TILES * HEADS
        w = norm_buffers(sb, sem, "norm")
        zdt_w, in_w = sb("zdt_w", [P, ZDT]), sb("in_w", [P, 4 * P])
        tap_w, tap_b = sb("tap_w", [P, TAPS, 4 * P]), sb("tap_b", [P, TAPS, 4 * P])
        out_w, norm_col = sb("out_w", [P, 2, P]), sb("norm_col", [P, 2])
        x_bias, feature_bias = sb("x_bias", [P, D_IN]), sb("feature_bias", [P, 2])
        dt_bias, a_log, a_neg, d_skip = (sb(n, [P, HEADS]) for n in ("dt_bias", "a_log", "a_neg", "d_skip"))
        xT = [sb(f"xT{p}", [P, TAPS - 1 + SEQ]) for p in range(2)]
        zx = [sb(f"zx{p}", [P, TILES, 2 * D_IN]) for p in range(2)]
        features = [[sb(f"features{p}{m}", [P, SEQ]) for m in range(2)] for p in range(2)]
        b_tok = [sb(f"b_tok{p}", [P, TILES, P]) for p in range(2)]
        v, u, s, s2, q, dt, a = (sb(n, [P, KH]) for n in ("v", "u", "s", "s2", "q", "dt", "a"))
        acs, tot, to_end = sb("acs", [P, KH]), sb("tot", [P, KH]), sb("to_end", [P, KH])
        decayed, decay_end, chunk_decay = sb("decayed", [P, KH]), sb("decay_end", [P, KH]), sb("chunk_decay", [P, KH])
        diff = [sb(f"diff{k}", [P, HEADS, P]) for k in range(2)]
        decay = [sb(f"decay{k}", [P, HEADS, P]) for k in range(TILES)]
        cb = [sb(f"cb{k}", [P, P]) for k in range(TILES)]
        score = [sb(f"score{k}", [P, HEADS, P]) for k in range(TILES)]
        xdt, xend, xskip = (sb(n, [P, TILES, D_IN]) for n in ("xdt", "xend", "xskip"))
        state = [sb(f"state{k}", [P, D_IN]) for k in range(TILES + 1)]
        scaled = sb("scaled", [P, D_IN])
        from_state, within, ungated = (sb(n, [P, D_IN]) for n in ("from_state", "within", "ungated"))
        y = [sb(f"y{k}", [P, D_IN]) for k in range(2)]
        square = [sb(f"square{k}", [P, D_IN]) for k in range(TILES)]
        ss, ms, rms = sb("ss", [P, TILES]), sb("ms", [P, TILES]), sb("rms", [P, TILES])
        yT = [sb(f"yT{k}", [P, D_IN]) for k in range(2)]

        turned = bank("turned")
        yT_up = turned[:, 0:D_IN]
        zx_up = [bank(f"zx_up{k}") for k in range(2)]
        small = bank("small")
        dt_up, acs_up, tot_up, cb_up = (small[:, 0:KH], small[:, KH:2 * KH], small[:, 2 * KH:3 * KH],
                                        small[:, P:2 * P])
        rows_up = [bank(f"rows_up{k}") for k in range(2)]
        y_up = bank("y_up")
        mixed = bank("mixed")
        grow_up, out_up = mixed[:, 0:D_IN], mixed[:, D_IN:D_IN + P]

        cleared, loaded, prepared = sem("cleared"), sem("loaded"), sem("prepared")
        chain_sem, var_ready, rstd_ready, normed, turned_up, xT_ready = (
            sem("chain"), sem("var_ready"), sem("rstd_ready"), sem("normed"), sem("turned_up"), sem("xT_ready"))
        zx_multiplied, zx_ready, dt_multiplied = sem("zx_multiplied"), sem("zx_ready"), sem("dt_multiplied")
        feature_multiplied, feature_ready, b_turned, b_ready = (
            sem("feature_multiplied"), sem("feature_ready"), sem("b_turned"), sem("b_ready"))
        v_ready, u_ready, a_ready = sem("v_ready"), sem("u_ready"), sem("a_ready")
        sums_up, sums_ready, decays_ready = sem("sums_up"), sem("sums_ready"), sem("decays_ready")
        rows_ready, diff_ready, decay_ready = sem("rows_ready"), sem("diff_ready"), sem("decay_ready")
        cb_multiplied, cb_ready, score_ready = sem("cb_multiplied"), sem("cb_ready"), sem("score_ready")
        xdt_ready, x_scaled, grown, state_ready, y_multiplied, y_taken = (
            sem("xdt_ready"), sem("x_scaled"), sem("grown"), sem("state_ready"), sem("y_multiplied"),
            sem("y_taken"))
        y_ready, ss_ready, ms_ready, rms_ready = sem("y_ready"), sem("ss_ready"), sem("ms_ready"), sem("rms_ready")
        yT_turned, yT_ready, out_ready, x_done = sem("yT_turned"), sem("yT_ready"), sem("out_ready"), sem("x_done")
        y_chain = sem("y_chain")

        plan = [(zdt_w[:, :], d["in_zdt"]), (in_w[:, :], d["in_xbc"]),
                (tap_b[:, :, :].rearrange("p k c -> p (k c)"),
                 d["conv_w"].rearrange("(o c) -> o c", o=1).broadcast_to([P, TAPS * 4 * P])),
                (out_w[:, :, :], d["out_w"].rearrange("(m p) o -> p m o", p=P)),
                (norm_col[:, :], d["norm_w"]),
                (x_bias[0:1, :], d["conv_b"][0:D_IN].rearrange("(o c) -> o c", o=1)),
                (feature_bias[:, :], d["feature_b"])] + [
            (t[:, :], d[n].rearrange("(o h) -> o h", o=1).broadcast_to([P, HEADS]))
            for t, n in ((dt_bias, "dt_bias"), (a_log, "A_log"), (d_skip, "D"))]

        def heads(t):
            return t.rearrange("p (h e) -> p h e", h=HEADS)

        def per_head(t, k):
            return t[:, k * HEADS:(k + 1) * HEADS].rearrange("p (h o) -> p h o", o=1).broadcast_to([P, HEADS, HD])

        with nc.Block() as block:
            @block.sync
            def _(sp):
                sp.wait_ge(cleared, 1)
                for dst, src in plan:
                    sp.dma_start(dst, src).then_inc(loaded, 16)

            @block.scalar
            def _(act):
                act.wait_ge(loaded, 16 * len(plan))
                act.activation(a_log[:, :], a_log[:, :], ACT.Exp).then_inc(prepared, 1)

            @block.vector
            def _(dve):
                dve.memset(x_bias[:, :], 0.0).then_inc(cleared, 1)
                for p in range(2):
                    dve.memset(xT[p][:, 0:TAPS - 1], 0.0)
                dve.memset(state[0][:, :], 0.0)
                dve.wait_ge(loaded, 16 * len(plan))
                for k in range(TAPS):
                    dve.tensor_tensor(tap_w[:, k, :], in_w[:, :], tap_b[:, k, :], ALU.mult)
                for m in range(2):
                    dve.tensor_scalar(out_w[:, m, :], out_w[:, m, :], norm_col[:, m:m + 1], None, ALU.mult)
                dve.wait_ge(prepared, 1)
                dve.tensor_scalar(a_neg[:, :], a_log[:, :], -1.0, None, ALU.mult)

        block = ctx.enter_context(nc.Block())

        @block.gpsimd
        def _(pool):
            def inverse_root(b, p):
                pool.wait_ge(var_ready, b + 1)
                pool.tensor_tensor(w[p].rstd[:, :], w[p].var[:, :], c.minus_half[:, :], ALU.pow
                                   ).then_inc(rstd_ready, 1)

            inverse_root(0, 0)
            for b, p, i in pairs(pool, SEQS):
                pool.wait_ge(a_ready, b + 1)
                pool.wait_ge(zx_ready, b * TILES + TILES + 2)
                for k in range(TILES):
                    xk = heads(zx[p][:, k, D_IN:])
                    pool.tensor_tensor(heads(xdt[:, k, :]), xk, per_head(dt, k), ALU.mult).then_inc(xdt_ready, 1)
                    pool.tensor_tensor(heads(xskip[:, k, :]), xk,
                                       d_skip[:, :].rearrange("p (h o) -> p h o", o=1).broadcast_to([P, HEADS, HD]),
                                       ALU.mult)
                pool.wait_ge(decays_ready, b + 1)
                pool.wait_ge(xdt_ready, b * TILES + TILES)
                for k in range(TILES):
                    pool.tensor_tensor(heads(xend[:, k, :]), heads(xdt[:, k, :]), per_head(decay_end, k),
                                       ALU.mult).then_inc(x_scaled, 1)
                if not is_last(b, SEQS):
                    inverse_root(b + 1, 1 - p)
                for k in range(TILES):
                    pool.wait_ge(ss_ready, b * TILES + k + 1)
                    pool.tensor_tensor(ms[:, k:k + 1], ss[:, k:k + 1], c.eps[:, :], ALU.add).then_inc(ms_ready, 1)
                    pool.wait_ge(ms_ready, b * TILES + k + 1)
                    pool.tensor_tensor(rms[:, k:k + 1], ms[:, k:k + 1], c.minus_half[:, 0:1], ALU.pow
                                       ).then_inc(rms_ready, 1)

        @block.tensor
        def _(pe):
            def project(b, p):
                pe.wait_ge(normed, b + 1)
                if reaches(b, 1):
                    pe.wait_ge(b_ready, b)
                for k in range(TILES):
                    last = pe.transpose(turned[:, k * P:(k + 1) * P], w[p].xn[:, k, :], c.ident[:, :])
                last.then_inc(turned_up, 1)
                pe.wait_ge(xT_ready, b + 1)
                for k in range(TILES):
                    now = slice(TAPS - 1 + k * P, TAPS - 1 + (k + 1) * P)
                    pe.wait_ge(zx_ready, b * TILES + k + 1)
                    pe.matmul(zx_up[k % 2][:, 0:D_IN], xT[p][:, now], zdt_w[:, 0:D_IN], start=True, stop=True)
                    for j in range(TAPS):
                        pe.matmul(zx_up[k % 2][:, D_IN:], xT[p][:, k * P + j:k * P + j + P],
                                  tap_w[:, j, 0:D_IN], start=(j == 0), stop=False)
                    pe.matmul(zx_up[k % 2][:, D_IN:], c.ones[:, :], x_bias[:, :], start=False, stop=True
                              ).then_inc(zx_multiplied, 1)
                if reaches(b, 1):
                    pe.wait_ge(cb_ready, b * TILES + 1)
                for k in range(TILES):
                    now = slice(TAPS - 1 + k * P, TAPS - 1 + (k + 1) * P)
                    last = pe.matmul(dt_up[:, k * HEADS:(k + 1) * HEADS], xT[p][:, now], zdt_w[:, D_IN:ZDT],
                                     start=True, stop=True)
                last.then_inc(dt_multiplied, 1)
                for m in range(2):
                    if m == 1:
                        pe.wait_ge(feature_ready, 2 * b + 1)
                    for j in range(TAPS):
                        last = pe.matmul(turned[:, :], tap_w[:, j, (2 + m) * P:(3 + m) * P], xT[p][:, j:j + SEQ],
                                         start=(j == 0), stop=(j == TAPS - 1))
                    last.then_inc(feature_multiplied, 1)
                pe.wait_ge(feature_ready, 2 * b + 2)
                for k in range(TILES):
                    last = pe.transpose(turned[:, k * P:(k + 1) * P], features[p][0][:, k * P:(k + 1) * P],
                                        c.ident[:, :])
                last.then_inc(b_turned, 1)

            def turn_and_project(k, n, grown_to):
                pe.wait_ge(y_ready, n + 1)
                for m in range(2):
                    last = pe.transpose(yT_up[:, m * P:(m + 1) * P], y[k % 2][:, m * P:(m + 1) * P], c.ident[:, :])
                last.then_inc(yT_turned, 1)
                pe.wait_ge(yT_ready, n + 1)
                pe.wait_ge(state_ready, grown_to)
                pe.wait_ge(x_done, n + 1)
                pe.matmul(out_up, yT[k % 2][:, 0:P], out_w[:, 0, :], start=True, stop=False)
                pe.matmul(out_up, yT[k % 2][:, P:], out_w[:, 1, :], start=False, stop=True).then_inc(out_ready, 1)

            project(0, 0)
            for b, p, i in pairs(pe, SEQS):
                pe.wait_ge(a_ready, b + 1)
                pe.matmul(acs_up, c.upto[:, :], a[:, :], start=True, stop=True)
                pe.matmul(tot_up, c.ones[:, :], a[:, :], start=True, stop=True).then_inc(sums_up, 1)
                for k in range(TILES):
                    n = b * TILES + k
                    pe.wait_ge(diff_ready, n + 1)
                    for h in range(HEADS):
                        last = pe.matmul(rows_up[k % 2][:, h * P:(h + 1) * P],
                                         a[:, k * HEADS + h:k * HEADS + h + 1].broadcast_to([P, P]), c.upto[:, :],
                                         start=True, stop=True)
                    last.then_inc(rows_ready, 1)
                    if k == 0:
                        pe.wait_ge(feature_ready, 2 * b + 2)
                        pe.wait_ge(sums_ready, b + 1)
                    pe.wait_ge(cb_ready, n + 1)
                    pe.matmul(cb_up, features[p][0][:, k * P:(k + 1) * P], features[p][1][:, k * P:(k + 1) * P],
                              start=True, stop=True).then_inc(cb_multiplied, 1)
                if not is_last(b, SEQS):
                    project(b + 1, 1 - p)
                for k in range(TILES):
                    n = b * TILES + k
                    if k == 0:
                        pe.wait_ge(b_ready, b + 1)
                    else:
                        pe.wait_ge(state_ready, n)
                        pe.wait_ge(x_done, n)
                    pe.wait_ge(x_scaled, n + 1)
                    pe.matmul(grow_up, b_tok[p][:, k, :], xend[:, k, :], start=True, stop=True).then_inc(grown, 1)
                    pe.wait_ge(score_ready, n + 1)
                    pe.wait_ge(y_taken, n + 1)
                    for h in range(HEADS):
                        pe.matmul(y_up[:, h * HD:(h + 1) * HD], score[k][:, h, :], xdt[:, k, h * HD:(h + 1) * HD],
                                  start=True, stop=True)
                    pe.matmul(y_up[:, D_IN:], features[p][1][:, k * P:(k + 1) * P], state[k][:, :],
                              start=True, stop=True).then_inc(y_multiplied, 1)
                    if k == 1 and not is_last(b, SEQS):
                        pe.wait_ge(b_ready, b + 2)
                    if k:
                        turn_and_project(k - 1, n - 1, n + 1)
                turn_and_project(TILES - 1, b * TILES + TILES - 1, b * TILES + TILES)

        @block.scalar
        def _(act):
            def activate(b, p):
                act.wait_ge(turned_up, b + 1)
                act.activation(xT[p][:, TAPS - 1:], turned[:, :], ACT.Copy).then_inc(xT_ready, 1)
                for k in range(TILES):
                    act.wait_ge(zx_multiplied, b * TILES + k + 1)
                    act.activation(zx[p][:, k, :], zx_up[k % 2][:, :], ACT.Silu).then_inc(zx_ready, 1)
                for m in range(2):
                    act.wait_ge(feature_multiplied, 2 * b + m + 1)
                    act.activation(features[p][m][:, :], turned[:, :], ACT.Silu, bias=feature_bias[:, m:m + 1]
                                   ).then_inc(feature_ready, 1)
                act.wait_ge(b_turned, b + 1)
                act.activation(b_tok[p][:, :, :].rearrange("p a c -> p (a c)"), turned[:, :], ACT.Copy
                               ).then_inc(b_ready, 1)

            def exponential(b):
                act.wait_ge(v_ready, b + 1)
                act.activation(u[:, :], q[:, :], ACT.Exp).then_inc(u_ready, 1)

            act.sem_inc(zx_ready, 2)
            act.sem_inc(decay_ready, 2)
            activate(0, 0)
            exponential(0)
            for b, p, i in pairs(act, SEQS):
                act.wait_ge(sums_ready, b + 1)
                act.activation(decayed[:, :], acs[:, :], ACT.Exp)
                act.activation(decay_end[:, :], to_end[:, :], ACT.Exp)
                act.activation(chunk_decay[:, :], tot[:, :], ACT.Exp).then_inc(decays_ready, 1)
                for k in range(TILES):
                    act.wait_ge(diff_ready, b * TILES + k + 3)
                    act.activation(decay[k][:, :, :], diff[k % 2][:, :, :], ACT.Exp).then_inc(decay_ready, 1)
                if not is_last(b, SEQS):
                    activate(b + 1, 1 - p)
                for k in range(TILES):
                    n = b * TILES + k
                    act.wait_ge(y_ready, n + 1)
                    act.activation(square[k][:, :], y[k % 2][:, :], ACT.Square, scale=D_IN ** -0.5,
                                   accum_out=ss[:, k:k + 1]
                                   ).then_inc(ss_ready, 1)
                    act.wait_ge(yT_turned, n + 1)
                    act.activation(yT[k % 2][:, :], yT_up, ACT.Copy).then_inc(yT_ready, 1)
                if not is_last(b, SEQS):
                    exponential(b + 1)

        @block.vector
        def _(dve):
            chain = Chain(dve, chain_sem, STEP_LINKS)

            def time_steps(b):
                link = chain.link

                def spread(t):
                    return t[:, :].rearrange("p (o h) -> p o h", o=1).broadcast_to([P, TILES, HEADS])

                def kh(t):
                    return t.rearrange("p (k h) -> p k h", h=HEADS)

                dve.wait_ge(dt_multiplied, b + 1)
                link(dve.tensor_tensor(kh(v[:, :]), kh(dt_up), spread(dt_bias), ALU.add))
                dve.scalar_tensor_tensor(out=q[:, :], in0=v[:, :], scalar=-1.0, in1=v[:, :],
                                         op0=ALU.mult, op1=ALU.min).then_inc(v_ready, 1)
                dve.wait_ge(u_ready, b + 1)
                link(dve.tensor_scalar(s2[:, :], u[:, :], 2.0, None, ALU.add))
                link(dve.reciprocal(s[:, :], s2[:, :]))
                link(dve.tensor_tensor(s[:, :], s[:, :], u[:, :], ALU.mult))
                link(dve.tensor_tensor(s2[:, :], s[:, :], s[:, :], ALU.mult))
                link(dve.tensor_scalar(q[:, :], s2[:, :], 1.0 / 15.0, None, ALU.mult))
                for n in (13, 11, 9, 7, 5, 3):
                    link(dve.scalar_tensor_tensor(out=q[:, :], in0=q[:, :], scalar=1.0 / n, in1=s2[:, :],
                                                  op0=ALU.add, op1=ALU.mult))
                link(dve.scalar_tensor_tensor(out=q[:, :], in0=q[:, :], scalar=1.0, in1=s[:, :],
                                              op0=ALU.add, op1=ALU.mult))
                link(dve.tensor_scalar(q[:, :], q[:, :], 2.0, None, ALU.mult))
                link(dve.scalar_tensor_tensor(out=dt[:, :], in0=v[:, :], scalar=0.0, in1=q[:, :],
                                              op0=ALU.max, op1=ALU.add))
                dve.tensor_tensor(kh(a[:, :]), kh(dt[:, :]), spread(a_neg), ALU.mult).then_inc(a_ready, 1)

            def finish(k, n):
                dve.wait_ge(out_ready, n + 1)
                dve.wait_ge(rms_ready, n + 1)
                xs = x[:, span(n, 1), :].rearrange("p a c -> p (a c)")
                dve.scalar_tensor_tensor(out=xs, in0=out_up, scalar=rms[:, k:k + 1], in1=xs,
                                         op0=ALU.mult, op1=ALU.add).then_inc(x_done, 1)

            dve.sem_inc(diff_ready, 2)
            dve.sem_inc(cb_ready, 1)
            dve.sem_inc(x_done, 1)
            dve.sem_inc(y_taken, 1)
            moments(dve, chain, x, 0, w[0]).then_inc(var_ready, 1)
            normalise(dve, x, 0, w[0], rstd_ready).then_inc(normed, 1)
            time_steps(0)
            for b, p, i in pairs(dve, SEQS):
                dve.wait_ge(sums_up, b + 1)
                dve.tensor_copy(acs[:, :], acs_up).then_inc(y_chain, 1)
                dve.tensor_copy(tot[:, :], tot_up).then_inc(y_chain, 1)
                dve.wait_ge(y_chain, Y_LINKS * b + 2)
                dve.tensor_tensor(to_end[:, :], tot[:, :], acs[:, :], ALU.subtract).then_inc(sums_ready, 1)
                for k in range(TILES):
                    n = b * TILES + k
                    dve.wait_ge(rows_ready, n + 1)
                    dve.wait_ge(decay_ready, n + 1)
                    for h in range(HEADS):
                        last = dve.tensor_scalar(diff[k % 2][:, h, :], rows_up[k % 2][:, h * P:(h + 1) * P],
                                                 acs[:, k * HEADS + h:k * HEADS + h + 1], 0.0,
                                                 ALU.subtract, ALU.min)
                    last.then_inc(diff_ready, 1)
                    dve.wait_ge(cb_multiplied, n + 1)
                    dve.tensor_tensor(cb[k][:, :], cb_up, c.upto[:, :], ALU.mult).then_inc(cb_ready, 1)
                if not is_last(b, SEQS):
                    chain.step(b + 1)
                    moments(dve, chain, x, b + 1, w[1 - p]).then_inc(var_ready, 1)
                    normalise(dve, x, b + 1, w[1 - p], rstd_ready).then_inc(normed, 1)
                for k in range(TILES):
                    dve.wait_ge(decay_ready, b * TILES + k + 3)
                    dve.wait_ge(cb_ready, b * TILES + k + 2)
                    dve.tensor_tensor(score[k][:, :, :], decay[k][:, :, :],
                                      cb[k][:, :].rearrange("p (o i) -> p o i", o=1).broadcast_to([P, HEADS, P]),
                                      ALU.mult).then_inc(score_ready, 1)
                dve.wait_ge(decays_ready, b + 1)
                for k in range(TILES):
                    n = b * TILES + k
                    done = Y_LINKS * b + 2 + 3 * k
                    dve.tensor_tensor(heads(scaled[:, :]), heads(state[k][:, :]), per_head(chunk_decay, k), ALU.mult
                                      ).then_inc(y_chain, 1)
                    dve.wait_ge(y_chain, done + 1)
                    dve.wait_ge(grown, n + 1)
                    dve.tensor_tensor(state[k + 1][:, :], scaled[:, :], grow_up, ALU.add
                                      ).then_inc(state_ready, 1)
                    dve.wait_ge(y_multiplied, n + 1)
                    dve.tensor_tensor(heads(from_state[:, :]), heads(y_up[:, D_IN:]), per_head(decayed, k), ALU.mult
                                      ).then_inc(y_chain, 1)
                    dve.tensor_tensor(within[:, :], y_up[:, 0:D_IN], xskip[:, k, :], ALU.add).then_inc(y_taken, 1)
                    dve.wait_ge(y_chain, done + 2)
                    dve.wait_ge(y_taken, n + 2)
                    dve.tensor_tensor(ungated[:, :], from_state[:, :], within[:, :], ALU.add).then_inc(y_chain, 1)
                    dve.wait_ge(y_chain, done + 3)
                    dve.tensor_tensor(y[k % 2][:, :], ungated[:, :], zx[p][:, k, 0:D_IN], ALU.mult).then_inc(y_ready, 1)
                    dve.wait_ge(state_ready, n + 1)
                    if k:
                        finish(k - 1, n - 1)
                finish(TILES - 1, b * TILES + TILES - 1)
                if not is_last(b, SEQS):
                    time_steps(b + 1)


def attention(nc, x, c, d):
    with ExitStack() as ctx:
        def sb(n, shape, dt=F32):
            return ctx.enter_context(nc.sbuf_tensor(f"att_{n}", shape, dt))

        def sem(n):
            return ctx.enter_context(nc.semaphore(f"att_{n}"))

        def bank(n):
            return ctx.enter_context(nc.psum_tensor(f"att_{n}", [P, 512], F32))

        w = norm_buffers(sb, sem, "norm")
        qkv_w, qkv_bias, q_bias = sb("qkv_w", [P, 3 * P]), sb("qkv_bias", [P, 3 * P]), sb("q_bias", [P, 1])
        out_w, out_bias = sb("out_w", [P, P]), sb("out_bias", [P, P])
        xT = [sb(f"xT{p}", [P, SEQ]) for p in range(2)]
        qT = [sb(f"qT{p}", [P, SEQ]) for p in range(2)]
        qkv = [sb(f"qkv{p}", [P, TILES, 3 * P]) for p in range(2)]
        vk = [sb(f"vk{k}", [P, AH, AD, AD]) for k in range(2)]
        weighted = sb("weighted", [P, AH, AD, AD])
        inside = sb("inside", [P, P])
        state = [sb(f"state{k}", [P, P]) for k in range(TILES + 1)]
        grown = sb("grown", [P, P])
        y = [sb(f"y{k}", [P, P]) for k in range(2)]
        yT = [sb(f"yT{k}", [P, P]) for k in range(2)]

        turned = bank("turned")
        qkv_up = [bank(f"qkv_up{k}") for k in range(2)]
        sums_up = [bank(f"sums_up{m}") for m in range(2)]
        grow_up, before_up, last_up = bank("grow_up")[:, 0:P], bank("before_up")[:, 0:P], bank("last_up")
        yT_up, out_up = last_up[:, 0:P], last_up[:, P:2 * P]

        cleared, loaded, chain_sem, var_ready, rstd_ready, normed, turned_up, xT_ready = (
            sem("cleared"), sem("loaded"), sem("chain"), sem("var_ready"), sem("rstd_ready"), sem("normed"),
            sem("turned_up"), sem("xT_ready"))
        qkv_multiplied, qkv_ready, q_multiplied, qT_ready = (
            sem("qkv_multiplied"), sem("qkv_ready"), sem("q_multiplied"), sem("qT_ready"))
        vk_ready, summed, weighted_ready, grow_ready, masked, state_ready = (
            sem("vk_ready"), sem("summed"), sem("weighted_ready"), sem("grow_ready"), sem("masked"),
            sem("state_ready"))
        inside_ready, before_ready, y_ready, yT_turned, yT_ready, out_ready, x_done = (
            sem("inside_ready"), sem("before_ready"), sem("y_ready"), sem("yT_turned"), sem("yT_ready"),
            sem("out_ready"), sem("x_done"))

        plan = [(qkv_w[:, :], d["qkv_w"]), (q_bias[:, :], d["qkv_b"][0:P].rearrange("(p o) -> p o", o=1)),
                (qkv_bias[:, :], d["qkv_b"].rearrange("(o c) -> o c", o=1).broadcast_to([P, 3 * P])),
                (out_w[:, :], d["att_out_w"]), (out_bias[0:1, :], d["att_out_b"].rearrange("(o c) -> o c", o=1))]
        with nc.Block() as block:
            @block.sync
            def _(sp):
                sp.wait_ge(cleared, 1)
                for dst, src in plan:
                    sp.dma_start(dst, src).then_inc(loaded, 16)
                sp.wait_ge(loaded, 16 * len(plan))

            @block.vector
            def _(dve):
                dve.memset(out_bias[:, :], 0.0).then_inc(cleared, 1)
                dve.memset(state[0][:, :], 0.0)

        block = ctx.enter_context(nc.Block())

        @block.gpsimd
        def _(pool):
            def inverse_root(b, p):
                pool.wait_ge(var_ready, b + 1)
                pool.tensor_tensor(w[p].rstd[:, :], w[p].var[:, :], c.minus_half[:, :], ALU.pow
                                   ).then_inc(rstd_ready, 1)

            inverse_root(0, 0)
            for b, p, i in pairs(pool, SEQS):
                if not is_last(b, SEQS):
                    inverse_root(b + 1, 1 - p)
                for k in range(TILES):
                    n = b * TILES + k
                    pool.wait_ge(qkv_ready, n + 3)
                    pool.wait_ge(summed, n + 1)
                    shape = [P, AH, AD, AD]
                    keys = qkv[p][:, k, P:2 * P].rearrange("p (h o n) -> p h o n", o=1, n=AD).broadcast_to(shape)
                    values = qkv[p][:, k, 2 * P:].rearrange("p (h v o) -> p h v o", v=AD, o=1).broadcast_to(shape)
                    pool.tensor_tensor(vk[k % 2][:, :, :, :], values, keys, ALU.mult).then_inc(vk_ready, 1)

        @block.tensor
        def _(pe):
            def project(b, p):
                pe.wait_ge(normed, b + 1)
                if reaches(b, 1):
                    pe.wait_ge(qT_ready, b)
                for k in range(TILES):
                    last = pe.transpose(turned[:, k * P:(k + 1) * P], w[p].xn[:, k, :], c.ident[:, :])
                last.then_inc(turned_up, 1)
                pe.wait_ge(xT_ready, b + 1)
                for k in range(TILES):
                    pe.wait_ge(qkv_ready, b * TILES + k + 1)
                    pe.matmul(qkv_up[k % 2][:, 0:3 * P], xT[p][:, k * P:(k + 1) * P], qkv_w[:, :],
                              start=True, stop=True).then_inc(qkv_multiplied, 1)
                pe.matmul(turned[:, :], qkv_w[:, 0:P], xT[p][:, :], start=True, stop=True).then_inc(q_multiplied, 1)

            def turn_and_project(k, n):
                pe.wait_ge(y_ready, n + 1)
                pe.wait_ge(x_done, n + 1)
                pe.transpose(yT_up, y[k % 2][:, :], c.ident[:, :]).then_inc(yT_turned, 1)
                pe.wait_ge(yT_ready, n + 1)
                pe.matmul(out_up, yT[k % 2][:, :], out_w[:, :], start=True, stop=False)
                pe.matmul(out_up, c.ones[:, :], out_bias[:, :], start=False, stop=True).then_inc(out_ready, 1)

            pe.sem_inc(summed, 2)
            project(0, 0)
            for b, p, i in pairs(pe, SEQS):
                if not is_last(b, SEQS):
                    project(b + 1, 1 - p)
                for k in range(TILES):
                    n = b * TILES + k
                    if k == 0:
                        pe.wait_ge(qT_ready, b + 1)
                        pe.wait_ge(qkv_ready, b * TILES + TILES + 2)
                    else:
                        pe.wait_ge(state_ready, n)
                    pe.matmul(grow_up, qkv[p][:, k, P:2 * P], qkv[p][:, k, 2 * P:], start=True, stop=True
                              ).then_inc(grow_ready, 1)
                    if k:
                        pe.wait_ge(y_ready, n)
                    pe.matmul(before_up, qT[p][:, k * P:(k + 1) * P], state[k][:, :], start=True, stop=True
                              ).then_inc(before_ready, 1)
                    pe.wait_ge(vk_ready, n + 1)
                    pe.wait_ge(weighted_ready, 2 * n + 2)
                    flat = vk[k % 2][:, :, :, :].rearrange("p h v n -> p (h v n)")
                    for m in range(2):
                        last = pe.matmul(sums_up[m][:, :], c.upto[:, :], flat[:, m * 512:(m + 1) * 512],
                                         start=True, stop=True)
                    last.then_inc(summed, 1)
                    if k:
                        turn_and_project(k - 1, n - 1)
                turn_and_project(TILES - 1, b * TILES + TILES - 1)

        @block.scalar
        def _(act):
            def keep(b, p):
                act.wait_ge(turned_up, b + 1)
                act.activation(xT[p][:, :], turned[:, :], ACT.Copy).then_inc(xT_ready, 1)
                act.wait_ge(q_multiplied, b + 1)
                act.activation(qT[p][:, :], turned[:, :], ACT.Identity, bias=q_bias[:, 0:1]).then_inc(qT_ready, 1)

            keep(0, 0)
            for b, p, i in pairs(act, SEQS):
                if not is_last(b, SEQS):
                    keep(b + 1, 1 - p)
                for k in range(TILES):
                    act.wait_ge(yT_turned, b * TILES + k + 1)
                    act.activation(yT[k % 2][:, :], yT_up, ACT.Copy).then_inc(yT_ready, 1)

        @block.vector
        def _(dve):
            chain = Chain(dve, chain_sem, NORM_LINKS)

            def add_bias(b, p):
                for k in range(TILES):
                    dve.wait_ge(qkv_multiplied, b * TILES + k + 1)
                    dve.tensor_tensor(qkv[p][:, k, :], qkv_up[k % 2][:, 0:3 * P], qkv_bias[:, :], ALU.add
                                      ).then_inc(qkv_ready, 1)

            def finish(n):
                dve.wait_ge(out_ready, n + 1)
                xs = x[:, span(n, 1), :].rearrange("p a c -> p (a c)")
                dve.tensor_tensor(xs, xs, out_up, ALU.add).then_inc(x_done, 1)

            dve.sem_inc(qkv_ready, 2)
            dve.sem_inc(weighted_ready, 2)
            dve.sem_inc(x_done, 1)
            moments(dve, chain, x, 0, w[0]).then_inc(var_ready, 1)
            normalise(dve, x, 0, w[0], rstd_ready).then_inc(normed, 1)
            add_bias(0, 0)
            for b, p, i in pairs(dve, SEQS):
                if not is_last(b, SEQS):
                    chain.step(b + 1)
                    moments(dve, chain, x, b + 1, w[1 - p]).then_inc(var_ready, 1)
                    normalise(dve, x, b + 1, w[1 - p], rstd_ready).then_inc(normed, 1)
                    add_bias(b + 1, 1 - p)
                for k in range(TILES):
                    n = b * TILES + k
                    dve.wait_ge(grow_ready, n + 1)
                    dve.tensor_tensor(grown[:, :], grow_up, c.head_block[:, :], ALU.mult).then_inc(masked, 1)
                    dve.wait_ge(masked, n + 1)
                    dve.tensor_tensor(state[k + 1][:, :], state[k][:, :], grown[:, :], ALU.add
                                      ).then_inc(state_ready, 1)
                    dve.wait_ge(summed, n + 3)
                    half = [P, AH // 2, AD, AD]
                    for m in range(2):
                        queries = qkv[p][:, k, m * P // 2:(m + 1) * P // 2].rearrange(
                            "p (h o n) -> p h o n", o=1, n=AD).broadcast_to(half)
                        dve.tensor_tensor(weighted[:, m * AH // 2:(m + 1) * AH // 2, :, :],
                                          sums_up[m][:, :].rearrange("p (h v n) -> p h v n", v=AD, n=AD),
                                          queries, ALU.mult).then_inc(weighted_ready, 1)
                    dve.wait_ge(weighted_ready, 2 * n + 4)
                    dve.tensor_reduce(inside[:, :].rearrange("p (h v) -> p h v", v=AD), weighted[:, :, :, :],
                                      AX_X, ALU.add).then_inc(inside_ready, 1)
                    dve.wait_ge(before_ready, n + 1)
                    dve.wait_ge(inside_ready, n + 1)
                    dve.tensor_tensor(y[k % 2][:, :], before_up, inside[:, :], ALU.add).then_inc(y_ready, 1)
                    dve.wait_ge(state_ready, n + 1)
                    if k:
                        finish(n - 1)
                finish(b * TILES + TILES - 1)


def load_once(nc, c, d, x, tables, sums):
    plan = [(x[:, :, :], d["u"].rearrange("(a p) c -> p a c", p=P)),
            (c.gate_w[:, :], d["gate"]), (c.bias[:, :], d["bias"].rearrange("(o e) -> o e", o=1).broadcast_to([P, E])),
            (c.shared_g[:, :], d["shared_gate"]), (c.shared_u[:, :], d["shared_up"]),
            (c.shared_d[:, 0, :], d["shared_down"]),
            (c.q_i[0][:, :], d["ffn_gate"]), (c.q_i[1][:, :], d["ffn_up"]),
            (c.q_i[2][:, :], d["ffn_down"])]
    with nc.semaphore("once_loaded") as loaded, nc.semaphore("once_zero") as zeroed, \
            nc.semaphore("once_cleared") as cleared, nc.Block() as block:
        @block.sync
        def _(sp):
            for dst, src in plan:
                sp.dma_start(dst, src).then_inc(loaded, 16)
            sp.wait_ge(loaded, 16 * len(plan))

        @block.vector
        def _(dve):
            dve.memset(c.zeros[:, :], 0.0).then_inc(zeroed, 1)
            dve.wait_ge(loaded, 16 * len(plan))
            for q, f in zip(c.q_i, c.q_f):
                dve.tensor_copy(f[:, :, :].rearrange("p a c -> p (a c)"), q[:, :])

        @block.scalar
        def _(act):
            act.wait_ge(zeroed, 1)
            n = 0
            for s in sums:
                half = (T + CAP) // P // 3
                for k in range(3):
                    act.dma_start(s[k * half * P:(k + 1) * half * P, :].rearrange("(p a) c -> p (a c)", p=P),
                                  c.zeros[:, 0:half * P]).then_inc(cleared, 16)
                    n += 16
            for t in tables:
                act.dma_start(t[T:T + CAP, :], c.zeros[:, 0:ROW]).then_inc(cleared, 16)
                n += 16
            act.wait_ge(cleared, n)


def clear_semaphores(nc):
    used = sorted(int(n) for n in nc.released_uncleared_semaphores)
    runs = []
    for n in used:
        if runs and runs[-1][1] == n:
            runs[-1][1] = n + 1
        else:
            runs.append([n, n + 1])
    with nc.Block() as block:
        @block.gpsimd
        def _(pool):
            for first, end in runs:
                pool.sem_clear(range(first, end))


def store(nc, x, out):
    with nc.semaphore("out_written") as written, nc.Block() as block:
        @block.sync
        def _(sp):
            sp.dma_start(out.rearrange("(a p) c -> p a c", p=P), x[:, :, :]).then_inc(written, 16)
            sp.wait_ge(written, 16)


def program(nc, d, out, layers):
    with ExitStack() as ctx:
        def sb(n, shape, dt):
            return ctx.enter_context(nc.sbuf_tensor(n, shape, dt))

        c = Bag()
        x = sb("x", [P, NT, P], F32)
        for n, shape, dt in (
                ("minus_half", [P, TILES], F32), ("eps", [P, 1], F32), ("ident", [P, P], F32), ("ones", [P, P], F32), ("upto", [P, P], F32),
                ("ones_bf", [P, P], BF16), ("before_bf", [P, P], BF16), ("zero_bf", [P, EG * LO], BF16),
                ("earlier_group", [P, GROUPS, GROUPS], F32), ("ramp_i", [P, LO], I32),
                ("lo_digit", [P, LO], F32), ("hi_digit", [P, HI], F32), ("part_i", [P, 1], I32),
                ("part1", [P, 1], F32), ("tile_i", [P, NT], I32), ("tile128", [P, NT], F32),
                ("own", [P, EG], F32), ("slot_i", [P, LO], I32), ("slot_m", [P, LO], I32),
                ("empty_row", [P, LO], F32), ("head_block", [P, P], F32),
                ("gate_w", [P, E], F32), ("bias", [P, E], F32), ("shared_g", [P, P], F32),
                ("shared_u", [P, P], F32), ("shared_d", [P, 1, P], F32)):
            c[n] = sb(n, shape, dt)
        c.q_f = [sb(f"q_f{k}", [P, HM, P], F32) for k in range(3)]

        def dram(n, shape, dt=F32):
            return nc.dram_tensor(n, shape, dt, kind="Internal").ap()

        tables = [dram(f"table{k}", (T + CAP, ROW)) for k in range(2)]
        sums = [[dram(f"sums{k}_{j}", (T + CAP, P)) for j in range(CHAINS)] for k in range(2)]
        lists = [dram(f"row_list{k}", (E * CAP,)) for k in range(2)]
        with nc.sbuf_tensor("zeros", [P, (T + CAP) // P // 3 * P], F32) as c.zeros, \
                nc.sbuf_tensor("q_i0", [P, HM * P], I32) as q0, nc.sbuf_tensor("q_i1", [P, HM * P], I32) as q1, \
                nc.sbuf_tensor("q_i2", [P, HM * P], I32) as q2:
            c.q_i = [q0, q1, q2]
            constants(nc, c)
            load_once(nc, c, d, x, tables, [s for pair in sums for s in pair])

        gathered, added = ([[ctx.enter_context(nc.semaphore(f"experts{k}_{n}{p}")) for p in range(2)]
                            for k in range(2)] for n in ("gathered", "added"))

        def moe_layer(k):
            with nc.sbuf_tensor(f"moe{k}_logits", [P, NT, E], F32) as logits, \
                    nc.sbuf_tensor(f"moe{k}_rows", [P, E], U32) as rows:
                moe = Bag()
                moe.gathered, moe.added = gathered[k], added[k]
                moe.logits, moe.rows = logits, rows
                moe.gate, moe.bias, moe.table, moe.sums = c.gate_w, c.bias, tables[k], sums[k]
                moe.row_list, moe.w123 = lists[k], d["w123"]
                ffn_layer(nc, f"shared{k}", sb, x, c, (c.shared_g, c.shared_u, c.shared_d), 1, 1.0, 0.5, moe)
                route(nc, f"route{k}", c, moe)
                experts(nc, f"experts{k}", c, moe)
                combine(nc, f"combine{k}", x, moe)

        def quant_layer(k):
            wg, wu, wd = c.q_f
            ffn_layer(nc, f"ffn{k}", sb, x, c, (wg[:, :, :].rearrange("p a c -> p (a c)"),
                      wu[:, :, :].rearrange("p a c -> p (a c)"), wd), HM, QSCALE, 0.5 * QSCALE)

        for what in layers:
            if what == "moe0":
                moe_layer(0)
            if what == "moe1":
                moe_layer(1)
                clear_semaphores(nc)
            if what == "mamba":
                state_space(nc, x, c, d)
            if what == "ffn0":
                quant_layer(0)
            if what == "attention":
                attention(nc, x, c, d)
            if what == "ffn1":
                quant_layer(1)
        store(nc, x, out)


LAYERS = ("moe0", "mamba", "moe1", "ffn0", "attention", "ffn1")


def kernel(**inputs):
    import numpy as np
    import concourse.bacc as bacc
    from concourse.bass_utils import run_bass_kernel_spmd

    def turned(a):
        return np.ascontiguousarray(np.asarray(a).T)

    w1, w2, w3 = (np.asarray(inputs[f"L0_ffn_{n}"]) for n in ("w1", "w2", "w3"))
    n_pairs = E // 2
    up1, up3 = (w.reshape(n_pairs, P, P).transpose(0, 2, 1) for w in (w1, w3))
    down2 = w2.transpose(0, 2, 1).reshape(n_pairs, P, P)
    arrays = {
        "u": np.ascontiguousarray(np.asarray(inputs["L0_attn_u"]).reshape(T, P)),
        "gate": turned(inputs["L0_ffn_gate_weight"]),
        "bias": np.ascontiguousarray(inputs["L0_ffn_e_bias"]),
        "w123": np.ascontiguousarray(np.concatenate([up1, up3, down2], axis=2)),
        "shared_gate": turned(inputs["L0_ffn_shared_gate"]),
        "shared_up": turned(inputs["L0_ffn_shared_up"]),
        "shared_down": turned(inputs["L0_ffn_shared_down"]),
        "ffn_gate": turned(inputs["L1_ffn_w_gate"]),
        "ffn_up": turned(inputs["L1_ffn_w_up"]),
        "ffn_down": np.ascontiguousarray(
            turned(inputs["L1_ffn_w_down"]).reshape(HM, P, P).transpose(1, 0, 2).reshape(P, HM * P)),
    }
    in_w, conv_b = np.asarray(inputs["L0_attn_in_proj_w"]), np.asarray(inputs["L0_attn_conv_b"])
    arrays |= {
        "in_zdt": turned(np.concatenate([in_w[:D_IN], in_w[D_IN + 4 * P:]])),
        "in_xbc": turned(in_w[D_IN:D_IN + 4 * P]),
        "conv_w": turned(inputs["L0_attn_conv_w"]).reshape(-1),
        "conv_b": np.ascontiguousarray(conv_b),
        "feature_b": turned(conv_b[D_IN:].reshape(2, P)),
        "dt_bias": np.ascontiguousarray(inputs["L0_attn_dt_bias"]),
        "A_log": np.ascontiguousarray(inputs["L0_attn_A_log"]),
        "D": np.ascontiguousarray(inputs["L0_attn_D"]),
        "norm_w": turned(np.asarray(inputs["L0_attn_norm_w"]).reshape(2, P)),
        "out_w": turned(inputs["L0_attn_out_proj_w"]),
        "qkv_w": turned(np.concatenate([np.asarray(inputs[f"L1_attn_W{n}"]) for n in "qkv"])),
        "qkv_b": np.concatenate([np.asarray(inputs[f"L1_attn_b{n}"]) for n in "qkv"]),
        "att_out_w": turned(inputs["L1_attn_Wo"]),
        "att_out_b": np.ascontiguousarray(inputs["L1_attn_bo"]),
    }
    nc = bacc.Bacc("TRN2", target_bir_lowering=False, num_devices=1)
    d = {n: nc.dram_tensor(f"in_{n}", a.shape, mybir.dt.from_np(a.dtype), kind="ExternalInput").ap()
         for n, a in arrays.items()}
    out = nc.dram_tensor("out", (T, P), F32, kind="ExternalOutput").ap()
    program(nc, d, out, LAYERS)
    r = run_bass_kernel_spmd(nc, [{f"in_{n}": a for n, a in arrays.items()}], core_ids=[0])
    return r.results[0]["out"].reshape(SEQS, SEQ, P)
```

```python
from contextlib import ExitStack

import concourse.bass as bass
from concourse import mybir

ALU = mybir.AluOpType
ACT = mybir.ActivationFunctionType
AX_X = mybir.AxisListType.X
F32 = mybir.dt.float32
BF16 = mybir.dt.bfloat16
I32 = mybir.dt.int32
U32 = mybir.dt.uint32

P = 128
SEQS = 8
TILES = 4
NT = SEQS * TILES
T = NT * P
SEQ = TILES * P
EPS = 1e-5

E = 64
CAP = 128
TOPK = 8
GROUPS = 8
TOP_GROUPS = 4
ROW = P + E
HI, LO = 8, 16
EG = P // HI
CHAINS = 2

HIDDEN = 384
HM = HIDDEN // P
QSCALE = 1.0 / 127.0

D_IN = 256
HEADS = 4
HD = D_IN // HEADS
ZDT = D_IN + HEADS
TAPS = 4

AH = 16
AD = P // AH


def pairs(eng, n, peel_first=False, by=2):
    if peel_first:
        for p in range(by):
            yield p, p, 0
    with eng.Fori(1 if peel_first else 0, n // by - 1) as i:
        for p in range(by):
            yield i * by + p, p, i
    for p in range(by):
        yield n - by + p, p, n // by - 1


def is_last(b, n):
    return isinstance(b, int) and b == n - 1


def reaches(b, n):
    return not isinstance(b, int) or b >= n


def span(first, n):
    return bass.ds(first, n)


class Chain:

    def __init__(self, eng, sem, per_step=0):
        self.eng, self.sem, self.per_step, self.base, self.n = eng, sem, per_step, 0, 0

    def step(self, b):
        if self.n:
            assert self.n == self.per_step, (self.n, self.per_step)
        self.base, self.n = b * self.per_step, 0

    def link(self, ins):
        self.n += 1
        ins.then_inc(self.sem, 1)
        self.eng.wait_ge(self.sem, self.base + self.n)


NORM_LINKS = 2


def moments(dve, chain, x, b, w):
    for k in range(TILES):
        last = dve.bn_stats(w.stats[:, k, :], x[:, span(b * TILES + k, 1), :].rearrange("p a c -> p (a c)"))
    chain.link(last)
    dve.sem_inc(w.passed, 1)
    for k in range(TILES):
        last = dve.bn_aggr(w.mv[:, k, :], w.stats[:, k, :])
    chain.link(last)
    return dve.tensor_scalar(w.var[:, :], w.mv[:, :, 1], EPS, None, ALU.add)


def inverse_roots(pool, c, w, var_ready, rstd_ready):
    for b, p, i in pairs(pool, SEQS):
        pool.wait_ge(var_ready, b + 1)
        pool.tensor_tensor(w[p].rstd[:, :], w[p].var[:, :], c.minus_half[:, :], ALU.pow).then_inc(rstd_ready, 1)


def normalise(dve, x, b, w, rstd_ready):
    dve.wait_ge(rstd_ready, b + 1)
    for k in range(TILES):
        last = dve.tensor_scalar(w.xn[:, k, :], x[:, span(b * TILES + k, 1), :].rearrange("p a c -> p (a c)"),
                                 w.mv[:, k, 0:1], w.rstd[:, k:k + 1], ALU.subtract, ALU.mult)
    return last


class Bag(dict):

    def __getattr__(self, n):
        return self[n]

    def __setattr__(self, n, v):
        self[n] = v


def norm_buffers(sb, sem, name):
    out = []
    passed = sem(f"{name}_passed")
    for p in range(2):
        w = Bag()
        w.passed = passed
        w.stats = sb(f"{name}_stats{p}", [P, TILES, 6], F32)
        w.mv = sb(f"{name}_mv{p}", [P, TILES, 2], F32)
        w.var = sb(f"{name}_var{p}", [P, TILES], F32)
        w.rstd = sb(f"{name}_rstd{p}", [P, TILES], F32)
        w.xn = sb(f"{name}_xn{p}", [P, TILES, P], F32)
        out.append(w)
    return out


def ffn_layer(nc, name, sb_, x, c, weights, blocks, gate_scale, out_scale, moe=None):
    with ExitStack() as ctx:
        def sb(n, shape, dt):
            return ctx.enter_context(nc.sbuf_tensor(f"{name}_{n}", shape, dt))

        def sem(n):
            return ctx.enter_context(nc.semaphore(f"{name}_{n}"))

        def bank(n):
            return ctx.enter_context(nc.psum_tensor(f"{name}_{n}", [P, 512], F32))

        w = norm_buffers(sb, sem, "norm")
        xT = [sb(f"xT{p}", [P, SEQ], F32) for p in range(2)]
        sil = [sb(f"sil{p}", [P, SEQ], F32) for p in range(2)]
        h = sb("h", [P, blocks, SEQ], F32)
        turned = bank("turned")
        gate = [bank(f"gate{p}") for p in range(2)]
        up = [bank(f"up{p}") for p in range(2)]
        down = bank("down")
        chain_sem, normed, turned_up, xT_ready = sem("chain"), sem("normed"), sem("turned_up"), sem("xT_ready")
        gate_ready, up_ready, sil_ready, h_ready, down_ready = (
            sem("gate_ready"), sem("up_ready"), sem("sil_ready"), sem("h_ready"), sem("down_ready"))
        var_ready, rstd_ready, table_written = (
            sem("var_ready"), sem("rstd_ready"), [sem(f"table_written{p}") for p in range(2)])
        logits_ready, logits_kept = sem("logits_ready"), sem("logits_kept")
        if moe:
            logits = bank("logits")
        block = ctx.enter_context(nc.Block())
        wg, wu, wd = weights

        @block.gpsimd
        def _(pool):
            inverse_roots(pool, c, w, var_ready, rstd_ready)

        @block.vector
        def _(dve):
            chain = Chain(dve, chain_sem, NORM_LINKS)
            dve.sem_inc(h_ready, 2)
            moments(dve, chain, x, 0, w[0]).then_inc(var_ready, 1)
            normalise(dve, x, 0, w[0], rstd_ready).then_inc(normed, 1)
            for b, p, i in pairs(dve, SEQS):
                if not is_last(b, SEQS):
                    chain.step(b + 1)
                    moments(dve, chain, x, b + 1, w[1 - p]).then_inc(var_ready, 1)
                for m in range(blocks):
                    dve.wait_ge(sil_ready, b * blocks + m + 1)
                    dve.wait_ge(up_ready, b * blocks + m + 1)
                    q = (blocks * p + m) % 2
                    dve.scalar_tensor_tensor(out=h[:, m, :], in0=up[q][:, :], scalar=gate_scale, in1=sil[q][:, :],
                                             op0=ALU.mult, op1=ALU.mult).then_inc(h_ready, 1)
                    if m == 0 and not is_last(b, SEQS):
                        if moe:
                            dve.wait_ge(table_written[1 - p], i * 16 + 16)
                        normalise(dve, x, b + 1, w[1 - p], rstd_ready).then_inc(normed, 1)
                dve.wait_ge(down_ready, b + 1)
                xs = x[:, span(b * TILES, TILES), :].rearrange("p a c -> p (a c)")
                dve.scalar_tensor_tensor(out=xs, in0=down[:, :], scalar=out_scale, in1=xs,
                                         op0=ALU.mult, op1=ALU.add)

        @block.tensor
        def _(pe):
            def turn(b, p):
                pe.wait_ge(normed, b + 1)
                for k in range(TILES):
                    last = pe.transpose(turned[:, k * P:(k + 1) * P], w[p].xn[:, k, :], c.ident[:, :])
                last.then_inc(turned_up, 1)

            turn(0, 0)
            for b, p, i in pairs(pe, SEQS):
                pe.wait_ge(xT_ready, b + 1)
                if moe:
                    pe.wait_ge(logits_kept, b + 1)
                    for k in range(TILES):
                        last = pe.matmul(logits[:, k * E:(k + 1) * E], xT[p][:, k * P:(k + 1) * P], moe.gate[:, :],
                                         start=True, stop=True)
                    last.then_inc(logits_ready, 1)
                for m in range(blocks):
                    q = (blocks * p + m) % 2
                    pe.wait_ge(h_ready, b * blocks + m + 1)
                    pe.matmul(gate[q][:, :], wg[:, m * P:(m + 1) * P], xT[p][:, :],
                              start=True, stop=True).then_inc(gate_ready, 1)
                    pe.matmul(up[q][:, :], wu[:, m * P:(m + 1) * P], xT[p][:, :],
                              start=True, stop=True).then_inc(up_ready, 1)
                if not is_last(b, SEQS):
                    turn(b + 1, 1 - p)
                pe.wait_ge(h_ready, b * blocks + blocks + 2)
                for k in range(TILES):
                    for m in range(blocks):
                        last = pe.matmul(down[:, k * P:(k + 1) * P], h[:, m, k * P:(k + 1) * P], wd[:, m, :],
                                         start=(m == 0), stop=(m == blocks - 1))
                last.then_inc(down_ready, 1)

        @block.scalar
        def _(act):
            def keep(b, p):
                act.wait_ge(turned_up, b + 1)
                act.activation(xT[p][:, :], turned[:, :], ACT.Copy).then_inc(xT_ready, 1)

            if moe:
                act.sem_inc(logits_kept, 1)
            keep(0, 0)
            for b, p, i in pairs(act, SEQS):
                if moe:
                    act.wait_ge(logits_ready, b + 1)
                    act.activation(moe.logits[:, span(b * TILES, TILES), :].rearrange("p a e -> p (a e)"),
                                   logits[:, 0:TILES * E], ACT.Copy).then_inc(logits_kept, 1)
                for m in range(blocks):
                    q = (blocks * p + m) % 2
                    act.wait_ge(gate_ready, b * blocks + m + 1)
                    act.activation(sil[q][:, :], gate[q][:, :], ACT.Silu, scale=gate_scale).then_inc(sil_ready, 1)
                if not is_last(b, SEQS):
                    keep(b + 1, 1 - p)

        if moe:
            @block.sync
            def _(sp):
                sp.sem_inc(table_written[1], 16)
                rows = moe.table[0:T, :].rearrange("(a p) c -> p a c", p=P)
                for b, p, i in pairs(sp, SEQS):
                    sp.wait_ge(normed, b + 1)
                    sp.dma_start(rows[:, span(b * TILES, TILES), 0:P], w[p].xn[:, :, :]).then_inc(table_written[p], 16)
                sp.wait_ge(table_written[0], SEQS // 2 * 16)
                sp.wait_ge(table_written[1], SEQS // 2 * 16 + 16)


def route(nc, name, c, moe):
    with ExitStack() as ctx:
        def sb(n, shape, dt):
            return ctx.enter_context(nc.sbuf_tensor(f"{name}_{n}", shape, dt))

        def sem(n):
            return ctx.enter_context(nc.semaphore(f"{name}_{n}"))

        def bank(n):
            return ctx.enter_context(nc.psum_tensor(f"{name}_{n}", [P, 512], F32))

        score = sb("score", [P, NT, E], F32)
        choice = sb("choice", [P, NT, E], F32)
        left = sb("left", [P, NT, E], F32)
        pick = sb("pick", [P, NT, E], BF16)
        ahead = sb("ahead", [P, NT, E], BF16)
        hi8 = sb("hi8", [P, NT, GROUPS, 4], F32)
        lo8 = sb("lo8", [P, NT, GROUPS, 4], F32)
        hi4 = sb("hi4", [P, NT, GROUPS, 2], F32)
        lo4 = sb("lo4", [P, NT, GROUPS, 2], F32)
        lo4b = sb("lo4b", [P, NT, GROUPS, 2], F32)
        g1, g2, g3 = (sb(f"g{k}", [P, NT, GROUPS], F32) for k in range(3))
        beats = sb("beats", [P, NT, GROUPS, GROUPS], F32)
        ties = sb("ties", [P, NT, GROUPS, GROUPS], F32)
        top = sb("top", [P, NT, TOPK], F32)
        total = sb("total", [P, NT], F32)
        inv = sb("inv", [P, NT], F32)
        inv2 = sb("inv2", [P, NT], F32)
        place = sb("place", [P, NT, E], I32)
        hi = sb("hi", [P, NT, E], I32)
        lo = sb("lo", [P, NT, E], I32)
        hi_bf, lo_bf = sb("hi_bf", [P, NT, E], BF16), sb("lo_bf", [P, NT, E], BF16)
        is_hi = [sb(f"is_hi{p}", [P, E, HI], BF16) for p in range(2)]
        is_lo = [sb(f"is_lo{p}", [P, E, LO], BF16) for p in range(2)]
        part_hi = [sb(f"part_hi{p}", [P, E, HI], BF16) for p in range(2)]
        tile_hi = [sb(f"tile_hi{p}", [P, E, HI], BF16) for p in range(2)]
        found = sb("found", [P, E // EG, LO], F32)
        empty = sb("empty", [P, E // EG, LO], F32)
        own_part = sb("own_part", [P, LO, EG], F32)
        by_expert = sb("by_expert", [E, CAP], F32)

        counts = [bank(f"counts{k}") for k in range(4)]
        slots = [bank(f"slots{k}") for k in range(4)]
        chain_sem, scored, picked, counted = sem("chain"), sem("scored"), sem("picked"), sem("counted")
        weights_written, weighted_ready, used, rows_found = (
            sem("weights_written"), sem("weighted_ready"), sem("used"), sem("rows_found"))
        rows_written, rows_read, rows_turned = sem("rows_written"), sem("rows_read"), sem("rows_turned")
        weights_ready = sem("weights_ready")
        digits, hi_ready, lo_ready = sem("digits"), sem("hi_ready"), sem("lo_ready")
        block = ctx.enter_context(nc.Block())

        def flat(t):
            return t[:, :, :].rearrange("p a e -> p (a e)")

        def over_groups(t):
            return t[:, :, :].rearrange("p a (g e) -> p a g e", g=GROUPS)

        @block.scalar
        def _(act):
            act.activation(flat(score), flat(moe.logits), ACT.Sigmoid).then_inc(scored, 1)
            act.wait_ge(digits, 1)
            act.activation(flat(hi_bf), flat(hi), ACT.Copy).then_inc(digits, 1)
            for j, p, i in pairs(act, NT):
                act.wait_ge(hi_ready, j + 1)
                act.activation(flat(part_hi[p]), flat(is_hi[p]), ACT.Copy,
                               scale=c.part1[:, 0:1]).then_inc(weighted_ready, 1)
                act.activation(flat(tile_hi[p]), flat(is_hi[p]), ACT.Copy,
                               scale=c.tile128[:, span(j, 1)]).then_inc(weighted_ready, 1)
            act.wait_ge(rows_turned, 1)
            act.activation(moe.rows[:, :], slots[0][:, 0:E], ACT.Copy).then_inc(weighted_ready, 1)

        @block.vector
        def _(dve):
            ch = Chain(dve, chain_sem)
            dve.wait_ge(scored, 1)
            bias = moe.bias[:, :].rearrange("p (a e) -> p a e", a=1).broadcast_to([P, NT, E])
            ch.link(dve.tensor_tensor(choice[:, :, :], score[:, :, :], bias, ALU.add))
            v = over_groups(choice)
            dve.tensor_tensor(hi8[:, :, :, :], v[:, :, :, 0:4], v[:, :, :, 4:8], ALU.max)
            ch.link(dve.tensor_tensor(lo8[:, :, :, :], v[:, :, :, 0:4], v[:, :, :, 4:8], ALU.min))
            dve.tensor_tensor(hi4[:, :, :, :], hi8[:, :, :, 0:2], hi8[:, :, :, 2:4], ALU.max)
            dve.tensor_tensor(lo4[:, :, :, :], hi8[:, :, :, 0:2], hi8[:, :, :, 2:4], ALU.min)
            ch.link(dve.tensor_tensor(lo4b[:, :, :, :], lo8[:, :, :, 0:2], lo8[:, :, :, 2:4], ALU.max))
            ch.link(dve.tensor_tensor(lo4[:, :, :, :], lo4[:, :, :, :], lo4b[:, :, :, :], ALU.max))
            dve.tensor_tensor(g1[:, :, :], hi4[:, :, :, 0], hi4[:, :, :, 1], ALU.max)
            dve.tensor_tensor(g2[:, :, :], hi4[:, :, :, 0], hi4[:, :, :, 1], ALU.min)
            ch.link(dve.tensor_tensor(g3[:, :, :], lo4[:, :, :, 0], lo4[:, :, :, 1], ALU.max))
            ch.link(dve.tensor_tensor(g2[:, :, :], g2[:, :, :], g3[:, :, :], ALU.max))
            ch.link(dve.tensor_tensor(g1[:, :, :], g1[:, :, :], g2[:, :, :], ALU.add))
            shape = [P, NT, GROUPS, GROUPS]
            other = g1[:, :, :].rearrange("p a (o g) -> p a o g", o=1).broadcast_to(shape)
            self_ = g1[:, :, :].rearrange("p a (g o) -> p a g o", o=1).broadcast_to(shape)
            earlier = c.earlier_group[:, :, :].rearrange("p (o g) h -> p o g h", o=1).broadcast_to(shape)
            dve.tensor_tensor(beats[:, :, :, :], other, self_, ALU.is_gt)
            ch.link(dve.tensor_tensor(ties[:, :, :, :], other, self_, ALU.is_equal))
            ch.link(dve.tensor_tensor(ties[:, :, :, :], ties[:, :, :, :], earlier, ALU.mult))
            ch.link(dve.tensor_tensor(beats[:, :, :, :], beats[:, :, :, :], ties[:, :, :, :], ALU.add))
            ch.link(dve.tensor_reduce(g2[:, :, :], beats[:, :, :, :], AX_X, ALU.add))
            ch.link(dve.tensor_scalar(g3[:, :, :], g2[:, :, :], float(TOP_GROUPS), None, ALU.is_lt))
            kept = g3[:, :, :].rearrange("p a (g o) -> p a g o", o=1).broadcast_to([P, NT, GROUPS, E // GROUPS])
            ch.link(dve.tensor_tensor(v, v, kept, ALU.mult))
            for j in range(NT):
                last = dve.max(top[:, j, :], choice[:, j, :])
            ch.link(last)
            for j in range(NT):
                last = dve.match_replace(left[:, j, :], top[:, j, :], choice[:, j, :], -1e30)
            ch.link(last)
            ch.link(dve.tensor_tensor(flat(pick), flat(left), flat(choice), ALU.not_equal))
            ch.link(dve.memset(ahead[:, 0, :], 0.0))
            for j in range(1, NT):
                ch.link(dve.tensor_tensor(ahead[:, j, :], ahead[:, j - 1, :], pick[:, j - 1, :], ALU.add))
            dve.sem_inc(picked, 1)
            ch.link(dve.tensor_tensor(flat(score), flat(score), flat(pick), ALU.mult))
            ch.link(dve.tensor_reduce(total[:, :], score[:, :, :], AX_X, ALU.add))
            ch.link(dve.tensor_scalar(total[:, :], total[:, :], 1e-20, None, ALU.add))
            ch.link(dve.reciprocal(inv[:, :], total[:, :]))
            ch.link(dve.tensor_scalar(inv2[:, :], inv[:, :], 1.25, None, ALU.mult))
            dve.tensor_tensor(score[:, :, :], score[:, :, :],
                              inv2[:, :].rearrange("p (a o) -> p a o", o=1).broadcast_to([P, NT, E]),
                              ALU.mult).then_inc(weights_ready, 1)
            for k in range(4):
                dve.wait_ge(counted, k + 1)
                s = slice(8 * k, 8 * k + 8)
                last = dve.scalar_tensor_tensor(
                    out=place[:, s, :].rearrange("p a e -> p (a e)"),
                    in0=pick[:, s, :].rearrange("p a e -> p (a e)"), scalar=-float(T),
                    in1=counts[k][:, :], op0=ALU.mult, op1=ALU.add)
            ch.link(last)
            dve.tensor_scalar(flat(hi), flat(place), 4, None, ALU.arith_shift_right).then_inc(digits, 1)
            ch.link(dve.tensor_scalar(flat(lo), flat(place), LO - 1, None, ALU.bitwise_and))
            ch.link(dve.tensor_copy(flat(lo_bf), flat(lo)))
            dve.wait_ge(digits, 2)
            for j, p, i in pairs(dve, NT):
                dve.wait_ge(used, j + 1)
                dve.tensor_tensor(is_hi[p][:, :, :],
                                  hi_bf[:, span(j, 1), :].rearrange("p a (e o) -> p (a e) o", o=1).broadcast_to([P, E, HI]),
                                  c.hi_digit[:, :].rearrange("p (o h) -> p o h", o=1).broadcast_to([P, E, HI]),
                                  ALU.is_equal).then_inc(hi_ready, 1)
                dve.tensor_tensor(is_lo[p][:, :, :],
                                  lo_bf[:, span(j, 1), :].rearrange("p a (e o) -> p (a e) o", o=1).broadcast_to([P, E, LO]),
                                  c.lo_digit[:, :].rearrange("p (o h) -> p o h", o=1).broadcast_to([P, E, LO]),
                                  ALU.is_equal).then_inc(lo_ready, 1)
            dve.wait_ge(used, NT + 2)
            for g in range(E // EG):
                ch.link(dve.tensor_tensor(own_part[:, :, :],
                                          slots[g][:, 0:EG * LO].rearrange("p (e l) -> p l e", l=LO),
                                          c.own[:, :].rearrange("p (o e) -> p o e", o=1).broadcast_to([P, LO, EG]),
                                          ALU.mult))
                ch.link(dve.tensor_reduce(found[:, g, :], own_part[:, :, :], AX_X, ALU.add))
            ch.link(dve.tensor_scalar(flat(empty), flat(found), 0.0, None, ALU.is_equal))
            ch.link(dve.tensor_tensor(empty[:, :, :], empty[:, :, :],
                                      c.empty_row[:, :].rearrange("p (o l) -> p o l", o=1)
                                      .broadcast_to([P, E // EG, LO]), ALU.mult))
            dve.scalar_tensor_tensor(out=flat(found), in0=flat(found), scalar=-1.0, in1=flat(empty),
                                     op0=ALU.add, op1=ALU.add).then_inc(rows_found, 1)

        @block.tensor
        def _(pe):
            pe.wait_ge(picked, 1)
            for k in range(4):
                s = slice(8 * k, 8 * k + 8)
                pe.matmul(counts[k][:, :], c.before_bf[:, :], pick[:, s, :].rearrange("p a e -> p (a e)"),
                          start=True, stop=False)
                pe.matmul(counts[k][:, :], c.ones_bf[:, :], ahead[:, s, :].rearrange("p a e -> p (a e)"),
                          start=False, stop=True).then_inc(counted, 1)
            for g in range(E // EG):
                pe.matmul(slots[g][:, 0:EG * LO], c.zero_bf[:, 0:P], c.zero_bf[:, 0:EG * LO], start=True, stop=False,
                          skip_group_check=True)
            pe.sem_inc(used, 2)
            for j, p, i in pairs(pe, NT):
                pe.wait_ge(weighted_ready, 2 * j + 2)
                pe.wait_ge(lo_ready, j + 1)
                for g in range(E // EG):
                    rhs = is_lo[p][:, g * EG:(g + 1) * EG, :].rearrange("p e l -> p (e l)")
                    for lhs in (part_hi, tile_hi):
                        last = pe.matmul(slots[g][:, 0:EG * LO],
                                         lhs[p][:, g * EG:(g + 1) * EG, :].rearrange("p e h -> p (e h)"), rhs,
                                         start=False, stop=is_last(j, NT) and lhs is tile_hi, skip_group_check=True)
                last.then_inc(used, 1)
            pe.wait_ge(rows_read, 16)
            pe.transpose(slots[0][:, 0:E], by_expert[:, :], c.ident[0:E, 0:E]).then_inc(rows_turned, 1)

        @block.sync
        def _(sp):
            sp.wait_ge(weights_ready, 1)
            sp.dma_start(moe.table[0:T, :].rearrange("(a p) c -> p a c", p=P)[:, :, P:ROW],
                         score[:, :, :]).then_inc(weights_written, 16)
            sp.wait_ge(rows_found, 1)
            sp.dma_start(moe.row_list.rearrange("(g p l) -> p g l", p=P, l=LO), found[:, :, :]).then_inc(rows_written, 16)
            sp.wait_ge(rows_written, 16)
            sp.dma_start(by_expert[:, :], moe.row_list.rearrange("(e s) -> e s", s=CAP)).then_inc(rows_read, 16)
            sp.wait_ge(weights_written, 16)


def experts(nc, name, c, moe):
    n_pairs = E // 2
    ring = 4
    ahead = 2
    with ExitStack() as ctx:
        def sb(n, shape, dt):
            return ctx.enter_context(nc.sbuf_tensor(f"{name}_{n}", shape, dt))

        def sem(n):
            return ctx.enter_context(nc.semaphore(f"{name}_{n}"))

        def bank(n):
            return ctx.enter_context(nc.psum_tensor(f"{name}_{n}", [P, 512], F32))

        row = [[sb(f"row{p}{k}", [P, 1], U32) for k in range(2)] for p in range(ring)]
        row_out = [[sb(f"row_out{p}{k}", [P, 1], U32) for k in range(2)] for p in range(2)]
        xg = [[sb(f"xg{p}{k}", [P, ROW], F32) for k in range(2)] for p in range(ring)]
        xgT = [sb(f"xgT{p}", [P, 2 * CAP], F32) for p in range(2)]
        w123 = [sb(f"w123{p}", [P, 3 * P], F32) for p in range(ring)]
        sil = [sb(f"sil{p}", [P, CAP], F32) for p in range(2)]
        h = [sb(f"h{p}", [P, CAP], F32) for p in range(2)]
        y = [[sb(f"y{p}{k}", [P, P], F32) for k in range(2)] for p in range(2)]
        turned = [bank(f"turned{p}") for p in range(2)]
        gate_up = [bank(f"gate_up{p}") for p in range(2)]
        down = [[bank(f"down{p}{k}") for k in range(2)] for p in range(2)]
        row_staged, gathered, loaded = (
            sem("row_staged"), moe.gathered, [sem(f"loaded{p}") for p in range(ring)])
        turned_up, xgT_ready, gate_ready, sil_ready, h_ready, down_ready, y_ready = (
            sem("turned_up"), sem("xgT_ready"), sem("gate_ready"), sem("sil_ready"), sem("h_ready"),
            sem("down_ready"), sem("y_ready"))
        passed = sem("passed")
        added = moe.added
        block = ctx.enter_context(nc.Block())

        @block.gpsimd
        def _(pool):
            def gather(r, p):
                if reaches(r, ring):
                    pool.wait_ge(y_ready, 2 * (r - ring + 1))
                for k in range(2):
                    last = pool.tensor_copy(row[p][k][:, :], moe.rows[:, span(2 * r + k, 1)])
                last.then_inc(row_staged, 1)
                pool.wait_ge(row_staged, r + 1)
                pool.sem_inc(passed, 1)
                for k in range(2):
                    pool.indirect_dma_start(xg[p][k][:, :], None, moe.table[:, :],
                                            bass.IndirectOffsetOnAxis(ap=row[p][k][:, :], axis=0)
                                            ).then_inc(gathered[p], 16)

            pool.wait_ge(moe.cleared, moe.zeros_done)
            for r in range(ahead):
                gather(r, r)
            for r, p, i in pairs(pool, n_pairs, peel_first=True, by=ring):
                if not isinstance(r, int) or r + ahead < n_pairs:
                    gather(r + ahead, (p + ahead) % ring)
                for k in range(2):
                    pool.wait_ge(y_ready, 2 * r + k + 1)
                    if reaches(r, 1):
                        pool.wait_ge(added[k], r * 16)
                        pool.sem_inc(passed, 1)
                    pool.indirect_dma_start(moe.sums[k][:, :],
                                            bass.IndirectOffsetOnAxis(ap=row_out[p % 2][k][:, :], axis=0),
                                            y[p % 2][k][:, :], None, compute_op=ALU.add).then_inc(added[k], 16)
            for k in range(CHAINS):
                pool.wait_ge(added[k], n_pairs * 16)

        @block.sync
        def _(sp):
            for r, p, i in pairs(sp, n_pairs, peel_first=True, by=ring):
                if reaches(r, ring):
                    sp.wait_ge(y_ready, 2 * (r - ring + 1))
                sp.dma_start(w123[p][:, :], moe.w123[span(r, 1), :, :].rearrange("a p c -> (a p) c")
                             ).then_inc(loaded[p], 16)

        @block.tensor
        def _(pe):
            def turn(r, p, i):
                pe.wait_ge(gathered[p], 32 * i + 32)
                for k in range(2):
                    last = pe.transpose(turned[p % 2][:, k * P:(k + 1) * P], xg[p][k][:, 0:P], c.ident[:, :])
                last.then_inc(turned_up, 1)

            turn(0, 0, 0)
            for r, p, i in pairs(pe, n_pairs, by=ring):
                pe.wait_ge(xgT_ready, r + 1)
                pe.wait_ge(loaded[p], 16 * i + 16)
                for m in range(2):
                    for k in range(2):
                        last = pe.matmul(gate_up[p % 2][k * E:(k + 1) * E, m * CAP:(m + 1) * CAP],
                                         w123[p][:, m * P + k * E:m * P + (k + 1) * E],
                                         xgT[p % 2][:, k * CAP:(k + 1) * CAP], start=True, stop=True)
                last.then_inc(gate_ready, 1)
                if not is_last(r, n_pairs):
                    turn(r + 1, (p + 1) % ring, i + (p + 1) // ring)
                pe.wait_ge(h_ready, r + 1)
                for k in range(2):
                    last = pe.matmul(down[p % 2][k][:, 0:P], h[p % 2][k * E:(k + 1) * E, :],
                                     w123[p][k * E:(k + 1) * E, 2 * P:3 * P], start=True, stop=True)
                last.then_inc(down_ready, 1)

        @block.scalar
        def _(act):
            def keep(r, p):
                act.wait_ge(turned_up, r + 1)
                act.activation(xgT[p][:, :], turned[p][:, 0:2 * P], ACT.Copy).then_inc(xgT_ready, 1)

            keep(0, 0)
            for r, p, i in pairs(act, n_pairs):
                act.wait_ge(gate_ready, r + 1)
                act.activation(sil[p][:, :], gate_up[p][:, 0:CAP], ACT.Silu).then_inc(sil_ready, 1)
                if not is_last(r, n_pairs):
                    keep(r + 1, 1 - p)

        @block.vector
        def _(dve):
            for r, p, i in pairs(dve, n_pairs, peel_first=True, by=ring):
                dve.wait_ge(sil_ready, r + 1)
                dve.tensor_tensor(h[p % 2][:, :], gate_up[p % 2][:, CAP:2 * CAP], sil[p % 2][:, :],
                                  ALU.mult).then_inc(h_ready, 1)
                dve.wait_ge(down_ready, r + 1)
                for k in range(2):
                    if reaches(r, 2):
                        dve.wait_ge(added[k], 16 * (r - 1))
                    dve.tensor_copy(row_out[p % 2][k][:, :], moe.rows[:, span(2 * r + k, 1)])
                    dve.tensor_scalar(y[p % 2][k][:, :], down[p % 2][k][:, 0:P],
                                      xg[p][k][:, span(P + 2 * r + k, 1)], None, ALU.mult).then_inc(y_ready, 1)


def combine(nc, name, x, moe):
    with ExitStack() as ctx:
        part = [[ctx.enter_context(nc.sbuf_tensor(f"{name}_part{p}{k}", [P, TILES, P], F32)) for k in range(CHAINS)]
                for p in range(2)]
        loaded = [ctx.enter_context(nc.semaphore(f"{name}_loaded{p}")) for p in range(2)]
        joined = ctx.enter_context(nc.semaphore(f"{name}_joined"))
        block = ctx.enter_context(nc.Block())

        @block.sync
        def _(sp):
            for b, p, i in pairs(sp, SEQS):
                sp.wait_ge(joined, 2 * b + 2)
                for k in range(CHAINS):
                    sp.dma_start(part[p][k][:, :, :], moe.sums[k][0:T, :].rearrange("(a p) c -> p a c", p=P)
                                 [:, span(b * TILES, TILES), :]).then_inc(loaded[p], 16)

        @block.vector
        def _(dve):
            dve.sem_inc(joined, 4)
            for b, p, i in pairs(dve, SEQS):
                dve.wait_ge(loaded[p], 16 * CHAINS * i + 16 * CHAINS)
                xs = x[:, span(b * TILES, TILES), :]
                for k in range(CHAINS):
                    dve.tensor_tensor(xs, xs, part[p][k][:, :, :], ALU.add).then_inc(joined, 1)
                    dve.wait_ge(joined, 2 * b + k + 5)



DT_LINKS = 15
Y_LINKS = 2 + 3 * TILES


def state_space(nc, x, c, d):
    with ExitStack() as ctx:
        def sb(n, shape, dt=F32):
            return ctx.enter_context(nc.sbuf_tensor(f"ssm_{n}", shape, dt))

        def sem(n):
            return ctx.enter_context(nc.semaphore(f"ssm_{n}"))

        def bank(n):
            return ctx.enter_context(nc.psum_tensor(f"ssm_{n}", [P, 512], F32))

        KH = TILES * HEADS
        w = norm_buffers(sb, sem, "norm")
        zdt_w, in_w = sb("zdt_w", [P, ZDT]), sb("in_w", [P, 4 * P])
        tap_w, tap_b = sb("tap_w", [P, TAPS, 4 * P]), sb("tap_b", [P, TAPS, 4 * P])
        out_w, norm_col = sb("out_w", [P, 2, P]), sb("norm_col", [P, 2])
        x_bias, feature_bias = sb("x_bias", [P, D_IN]), sb("feature_bias", [P, 2])
        dt_bias, a_log, a_neg, d_skip = (sb(n, [P, HEADS]) for n in ("dt_bias", "a_log", "a_neg", "d_skip"))
        xT = [sb(f"xT{p}", [P, TAPS - 1 + SEQ]) for p in range(2)]
        zx = [sb(f"zx{p}", [P, TILES, 2 * D_IN]) for p in range(2)]
        features = [[sb(f"features{p}{m}", [P, SEQ]) for m in range(2)] for p in range(2)]
        b_tok = [sb(f"b_tok{p}", [P, TILES, P]) for p in range(2)]
        v, u, s, s2, q, a = (sb(n, [P, KH]) for n in ("v", "u", "s", "s2", "q", "a"))
        dt = [sb(f"dt{p}", [P, KH]) for p in range(2)]
        acs, tot, to_end = sb("acs", [P, KH]), sb("tot", [P, KH]), sb("to_end", [P, KH])
        decayed, decay_end, chunk_decay = sb("decayed", [P, KH]), sb("decay_end", [P, KH]), sb("chunk_decay", [P, KH])
        diff = [sb(f"diff{k}", [P, HEADS, P]) for k in range(2)]
        decay = [sb(f"decay{k}", [P, HEADS, P]) for k in range(TILES)]
        cb = [sb(f"cb{k}", [P, P]) for k in range(TILES)]
        score = [sb(f"score{k}", [P, HEADS, P]) for k in range(TILES)]
        xdt, xend, xskip = (sb(n, [P, TILES, D_IN]) for n in ("xdt", "xend", "xskip"))
        state = [sb(f"state{k}", [P, D_IN]) for k in range(TILES + 1)]
        scaled = sb("scaled", [P, D_IN])
        from_state, within, ungated = (sb(n, [P, D_IN]) for n in ("from_state", "within", "ungated"))
        y = [sb(f"y{k}", [P, D_IN]) for k in range(2)]
        square = [sb(f"square{k}", [P, D_IN]) for k in range(TILES)]
        ss, ms, rms = sb("ss", [P, TILES]), sb("ms", [P, TILES]), sb("rms", [P, TILES])
        yT = [sb(f"yT{k}", [P, D_IN]) for k in range(2)]

        turned = bank("turned")
        yT_up = turned[:, 0:D_IN]
        zx_up = [bank(f"zx_up{k}") for k in range(2)]
        small = bank("small")
        dt_up, acs_up, tot_up, cb_up = (small[:, 0:KH], small[:, KH:2 * KH], small[:, 2 * KH:3 * KH],
                                        small[:, P:2 * P])
        rows_up = [bank(f"rows_up{k}") for k in range(2)]
        y_up = bank("y_up")
        mixed = bank("mixed")
        grow_up, out_up = mixed[:, 0:D_IN], mixed[:, D_IN:D_IN + P]

        cleared, loaded, prepared = sem("cleared"), sem("loaded"), sem("prepared")
        chain_sem, var_ready, rstd_ready, normed, turned_up, xT_ready = (
            sem("chain"), sem("var_ready"), sem("rstd_ready"), sem("normed"), sem("turned_up"), sem("xT_ready"))
        zx_multiplied, zx_ready, dt_multiplied = sem("zx_multiplied"), sem("zx_ready"), sem("dt_multiplied")
        feature_multiplied, feature_ready, b_turned, b_ready = (
            sem("feature_multiplied"), sem("feature_ready"), sem("b_turned"), sem("b_ready"))
        v_ready, u_ready, a_ready = sem("v_ready"), sem("u_ready"), sem("a_ready")
        sums_up, sums_ready, decays_ready = sem("sums_up"), sem("sums_ready"), sem("decays_ready")
        rows_ready, diff_ready, decay_ready = sem("rows_ready"), sem("diff_ready"), sem("decay_ready")
        cb_multiplied, cb_ready, score_ready = sem("cb_multiplied"), sem("cb_ready"), sem("score_ready")
        xdt_ready, x_scaled, grown, state_ready, y_multiplied, y_taken = (
            sem("xdt_ready"), sem("x_scaled"), sem("grown"), sem("state_ready"), sem("y_multiplied"),
            sem("y_taken"))
        y_ready, ss_ready, ms_ready, rms_ready = sem("y_ready"), sem("ss_ready"), sem("ms_ready"), sem("rms_ready")
        yT_turned, yT_ready, out_ready, x_done = sem("yT_turned"), sem("yT_ready"), sem("out_ready"), sem("x_done")
        y_chain, dt_chain = sem("y_chain"), sem("dt_chain")

        plan = [(zdt_w[:, :], d["in_zdt"]), (in_w[:, :], d["in_xbc"]),
                (tap_b[:, :, :].rearrange("p k c -> p (k c)"),
                 d["conv_w"].rearrange("(o c) -> o c", o=1).broadcast_to([P, TAPS * 4 * P])),
                (out_w[:, :, :], d["out_w"].rearrange("(m p) o -> p m o", p=P)),
                (norm_col[:, :], d["norm_w"]),
                (x_bias[0:1, :], d["conv_b"][0:D_IN].rearrange("(o c) -> o c", o=1)),
                (feature_bias[:, :], d["feature_b"])] + [
            (t[:, :], d[n].rearrange("(o h) -> o h", o=1).broadcast_to([P, HEADS]))
            for t, n in ((dt_bias, "dt_bias"), (a_log, "A_log"), (d_skip, "D"))]

        def heads(t):
            return t.rearrange("p (h e) -> p h e", h=HEADS)

        def per_head(t, k):
            return t[:, k * HEADS:(k + 1) * HEADS].rearrange("p (h o) -> p h o", o=1).broadcast_to([P, HEADS, HD])

        with nc.Block() as block:
            @block.sync
            def _(sp):
                sp.wait_ge(cleared, 1)
                for dst, src in plan:
                    sp.dma_start(dst, src).then_inc(loaded, 16)

            @block.scalar
            def _(act):
                act.wait_ge(loaded, 16 * len(plan))
                act.activation(a_log[:, :], a_log[:, :], ACT.Exp).then_inc(prepared, 1)

            @block.vector
            def _(dve):
                dve.memset(x_bias[:, :], 0.0).then_inc(cleared, 1)
                for p in range(2):
                    dve.memset(xT[p][:, 0:TAPS - 1], 0.0)
                dve.memset(state[0][:, :], 0.0)
                dve.wait_ge(loaded, 16 * len(plan))
                for k in range(TAPS):
                    dve.tensor_tensor(tap_w[:, k, :], in_w[:, :], tap_b[:, k, :], ALU.mult)
                for m in range(2):
                    dve.tensor_scalar(out_w[:, m, :], out_w[:, m, :], norm_col[:, m:m + 1], None, ALU.mult)
                dve.wait_ge(prepared, 1)
                dve.tensor_scalar(a_neg[:, :], a_log[:, :], -1.0, None, ALU.mult)

        def later(b, n):
            return not isinstance(b, int) or b + n < SEQS

        block = ctx.enter_context(nc.Block())

        @block.gpsimd
        def _(pool):
            def inverse_root(b, p):
                pool.wait_ge(var_ready, b + 1)
                pool.tensor_tensor(w[p].rstd[:, :], w[p].var[:, :], c.minus_half[:, :], ALU.pow
                                   ).then_inc(rstd_ready, 1)

            inverse_root(0, 0)
            inverse_root(1, 1)
            for b, p, i in pairs(pool, SEQS):
                pool.wait_ge(a_ready, b + 1)
                pool.wait_ge(zx_ready, b * TILES + TILES + 2)
                for k in range(TILES):
                    xk = heads(zx[p][:, k, D_IN:])
                    pool.tensor_tensor(heads(xdt[:, k, :]), xk, per_head(dt[p], k), ALU.mult).then_inc(xdt_ready, 1)
                    pool.tensor_tensor(heads(xskip[:, k, :]), xk,
                                       d_skip[:, :].rearrange("p (h o) -> p h o", o=1).broadcast_to([P, HEADS, HD]),
                                       ALU.mult)
                pool.wait_ge(decays_ready, b + 1)
                pool.wait_ge(xdt_ready, b * TILES + TILES)
                for k in range(TILES):
                    pool.tensor_tensor(heads(xend[:, k, :]), heads(xdt[:, k, :]), per_head(decay_end, k),
                                       ALU.mult).then_inc(x_scaled, 1)
                for k in range(TILES):
                    if k == 2 and later(b, 2):
                        inverse_root(b + 2, p)
                    pool.wait_ge(ss_ready, b * TILES + k + 1)
                    pool.tensor_tensor(ms[:, k:k + 1], ss[:, k:k + 1], c.eps[:, :], ALU.add).then_inc(ms_ready, 1)
                    pool.wait_ge(ms_ready, b * TILES + k + 1)
                    pool.tensor_tensor(rms[:, k:k + 1], ms[:, k:k + 1], c.minus_half[:, 0:1], ALU.pow
                                       ).then_inc(rms_ready, 1)

        @block.tensor
        def _(pe):
            def turn(b, p):
                pe.wait_ge(normed, b + 1)
                if reaches(b, 1):
                    pe.wait_ge(b_ready, b)
                for k in range(TILES):
                    last = pe.transpose(turned[:, k * P:(k + 1) * P], w[p].xn[:, k, :], c.ident[:, :])
                last.then_inc(turned_up, 1)

            def project_features(b, p):
                pe.wait_ge(xT_ready, b + 1)
                if reaches(b, 1):
                    pe.wait_ge(cb_ready, b * TILES + 1)
                for k in range(TILES):
                    now = slice(TAPS - 1 + k * P, TAPS - 1 + (k + 1) * P)
                    last = pe.matmul(dt_up[:, k * HEADS:(k + 1) * HEADS], xT[p][:, now], zdt_w[:, D_IN:ZDT],
                                     start=True, stop=True)
                last.then_inc(dt_multiplied, 1)
                for m in range(2):
                    if m == 1:
                        pe.wait_ge(feature_ready, 2 * b + 1)
                    for j in range(TAPS):
                        last = pe.matmul(turned[:, :], tap_w[:, j, (2 + m) * P:(3 + m) * P], xT[p][:, j:j + SEQ],
                                         start=(j == 0), stop=(j == TAPS - 1))
                    last.then_inc(feature_multiplied, 1)
                pe.wait_ge(feature_ready, 2 * b + 2)
                for k in range(TILES):
                    last = pe.transpose(turned[:, k * P:(k + 1) * P], features[p][0][:, k * P:(k + 1) * P],
                                        c.ident[:, :])
                last.then_inc(b_turned, 1)

            def project_tokens(b, p, k):
                now = slice(TAPS - 1 + k * P, TAPS - 1 + (k + 1) * P)
                pe.wait_ge(zx_ready, b * TILES + k + 1)
                pe.matmul(zx_up[k % 2][:, 0:D_IN], xT[p][:, now], zdt_w[:, 0:D_IN], start=True, stop=True)
                for j in range(TAPS):
                    pe.matmul(zx_up[k % 2][:, D_IN:], xT[p][:, k * P + j:k * P + j + P],
                              tap_w[:, j, 0:D_IN], start=(j == 0), stop=False)
                pe.matmul(zx_up[k % 2][:, D_IN:], c.ones[:, :], x_bias[:, :], start=False, stop=True
                          ).then_inc(zx_multiplied, 1)

            def turn_and_project(k, n, grown_to):
                pe.wait_ge(y_ready, n + 1)
                for m in range(2):
                    last = pe.transpose(yT_up[:, m * P:(m + 1) * P], y[k % 2][:, m * P:(m + 1) * P], c.ident[:, :])
                last.then_inc(yT_turned, 1)
                pe.wait_ge(yT_ready, n + 1)
                pe.wait_ge(state_ready, grown_to)
                pe.wait_ge(x_done, n + 1)
                pe.matmul(out_up, yT[k % 2][:, 0:P], out_w[:, 0, :], start=True, stop=False)
                pe.matmul(out_up, yT[k % 2][:, P:], out_w[:, 1, :], start=False, stop=True).then_inc(out_ready, 1)

            turn(0, 0)
            project_features(0, 0)
            for k in range(TILES):
                project_tokens(0, 0, k)
            for b, p, i in pairs(pe, SEQS):
                pe.wait_ge(a_ready, b + 1)
                pe.matmul(acs_up, c.upto[:, :], a[:, :], start=True, stop=True)
                pe.matmul(tot_up, c.ones[:, :], a[:, :], start=True, stop=True).then_inc(sums_up, 1)
                for k in range(TILES):
                    n = b * TILES + k
                    pe.wait_ge(diff_ready, n + 1)
                    for h in range(HEADS):
                        last = pe.matmul(rows_up[k % 2][:, h * P:(h + 1) * P],
                                         a[:, k * HEADS + h:k * HEADS + h + 1].broadcast_to([P, P]), c.upto[:, :],
                                         start=True, stop=True)
                    last.then_inc(rows_ready, 1)
                    if k == 0:
                        pe.wait_ge(feature_ready, 2 * b + 2)
                        pe.wait_ge(sums_ready, b + 1)
                    pe.wait_ge(cb_ready, n + 1)
                    pe.matmul(cb_up, features[p][0][:, k * P:(k + 1) * P], features[p][1][:, k * P:(k + 1) * P],
                              start=True, stop=True).then_inc(cb_multiplied, 1)
                if later(b, 1):
                    turn(b + 1, 1 - p)
                    project_features(b + 1, 1 - p)
                for k in range(TILES):
                    n = b * TILES + k
                    if k == 0:
                        pe.wait_ge(b_ready, b + 1)
                    else:
                        pe.wait_ge(state_ready, n)
                        pe.wait_ge(x_done, n)
                    pe.wait_ge(x_scaled, n + 1)
                    pe.matmul(grow_up, b_tok[p][:, k, :], xend[:, k, :], start=True, stop=True).then_inc(grown, 1)
                    pe.wait_ge(score_ready, n + 1)
                    pe.wait_ge(y_taken, n + 1)
                    for h in range(HEADS):
                        pe.matmul(y_up[:, h * HD:(h + 1) * HD], score[k][:, h, :], xdt[:, k, h * HD:(h + 1) * HD],
                                  start=True, stop=True)
                    pe.matmul(y_up[:, D_IN:], features[p][1][:, k * P:(k + 1) * P], state[k][:, :],
                              start=True, stop=True).then_inc(y_multiplied, 1)
                    if k == 1 and not is_last(b, SEQS):
                        pe.wait_ge(b_ready, b + 2)
                    if k:
                        turn_and_project(k - 1, n - 1, n + 1)
                    if later(b, 1):
                        project_tokens(b + 1, 1 - p, k)
                turn_and_project(TILES - 1, b * TILES + TILES - 1, b * TILES + TILES)

        @block.scalar
        def _(act):
            def keep(b, p):
                act.wait_ge(turned_up, b + 1)
                act.activation(xT[p][:, TAPS - 1:], turned[:, :], ACT.Copy).then_inc(xT_ready, 1)

            def activate_features(b, p):
                for m in range(2):
                    act.wait_ge(feature_multiplied, 2 * b + m + 1)
                    act.activation(features[p][m][:, :], turned[:, :], ACT.Silu, bias=feature_bias[:, m:m + 1]
                                   ).then_inc(feature_ready, 1)
                act.wait_ge(b_turned, b + 1)
                act.activation(b_tok[p][:, :, :].rearrange("p a c -> p (a c)"), turned[:, :], ACT.Copy
                               ).then_inc(b_ready, 1)

            def activate_tokens(b, p, k):
                act.wait_ge(zx_multiplied, b * TILES + k + 1)
                act.activation(zx[p][:, k, :], zx_up[k % 2][:, :], ACT.Silu).then_inc(zx_ready, 1)

            def exponential(b):
                act.wait_ge(v_ready, b + 1)
                act.activation(u[:, :], q[:, :], ACT.Exp).then_inc(u_ready, 1)

            act.sem_inc(zx_ready, 2)
            act.sem_inc(decay_ready, 2)
            keep(0, 0)
            exponential(0)
            activate_features(0, 0)
            for k in range(TILES):
                activate_tokens(0, 0, k)
            for b, p, i in pairs(act, SEQS):
                act.wait_ge(sums_ready, b + 1)
                act.activation(decayed[:, :], acs[:, :], ACT.Exp)
                act.activation(decay_end[:, :], to_end[:, :], ACT.Exp)
                act.activation(chunk_decay[:, :], tot[:, :], ACT.Exp).then_inc(decays_ready, 1)
                for k in range(TILES):
                    act.wait_ge(diff_ready, b * TILES + k + 3)
                    act.activation(decay[k][:, :, :], diff[k % 2][:, :, :], ACT.Exp).then_inc(decay_ready, 1)
                if later(b, 1):
                    keep(b + 1, 1 - p)
                    exponential(b + 1)
                    activate_features(b + 1, 1 - p)
                for k in range(TILES):
                    n = b * TILES + k
                    act.wait_ge(y_ready, n + 1)
                    act.activation(square[k][:, :], y[k % 2][:, :], ACT.Square, scale=D_IN ** -0.5,
                                   accum_out=ss[:, k:k + 1]
                                   ).then_inc(ss_ready, 1)
                    act.wait_ge(yT_turned, n + 1)
                    act.activation(yT[k % 2][:, :], yT_up, ACT.Copy).then_inc(yT_ready, 1)
                    if later(b, 1):
                        activate_tokens(b + 1, 1 - p, k)

        @block.vector
        def _(dve):
            chain = Chain(dve, chain_sem, NORM_LINKS)
            dt_links = Chain(dve, dt_chain, DT_LINKS)
            link = dt_links.link

            def spread(t):
                return t[:, :].rearrange("p (o h) -> p o h", o=1).broadcast_to([P, TILES, HEADS])

            def kh(t):
                return t.rearrange("p (k h) -> p k h", h=HEADS)

            def start_time_steps(b):
                dt_links.step(b)
                dve.wait_ge(dt_multiplied, b + 1)
                link(dve.tensor_tensor(kh(v[:, :]), kh(dt_up), spread(dt_bias), ALU.add))
                dve.scalar_tensor_tensor(out=q[:, :], in0=v[:, :], scalar=-1.0, in1=v[:, :],
                                         op0=ALU.mult, op1=ALU.min).then_inc(v_ready, 1)

            def time_steps(b, p):
                dve.wait_ge(u_ready, b + 1)
                link(dve.tensor_scalar(s2[:, :], u[:, :], 2.0, None, ALU.add))
                link(dve.reciprocal(s[:, :], s2[:, :]))
                link(dve.tensor_tensor(s[:, :], s[:, :], u[:, :], ALU.mult))
                link(dve.tensor_tensor(s2[:, :], s[:, :], s[:, :], ALU.mult))
                link(dve.tensor_scalar(q[:, :], s2[:, :], 1.0 / 15.0, None, ALU.mult))
                for n in (13, 11, 9, 7, 5, 3):
                    link(dve.scalar_tensor_tensor(out=q[:, :], in0=q[:, :], scalar=1.0 / n, in1=s2[:, :],
                                                  op0=ALU.add, op1=ALU.mult))
                link(dve.scalar_tensor_tensor(out=q[:, :], in0=q[:, :], scalar=1.0, in1=s[:, :],
                                              op0=ALU.add, op1=ALU.mult))
                link(dve.tensor_scalar(q[:, :], q[:, :], 2.0, None, ALU.mult))
                link(dve.scalar_tensor_tensor(out=dt[p][:, :], in0=v[:, :], scalar=0.0, in1=q[:, :],
                                              op0=ALU.max, op1=ALU.add))
                dve.tensor_tensor(kh(a[:, :]), kh(dt[p][:, :]), spread(a_neg), ALU.mult).then_inc(a_ready, 1)

            def finish(k, n):
                dve.wait_ge(out_ready, n + 1)
                dve.wait_ge(rms_ready, n + 1)
                xs = x[:, span(n, 1), :].rearrange("p a c -> p (a c)")
                dve.scalar_tensor_tensor(out=xs, in0=out_up, scalar=rms[:, k:k + 1], in1=xs,
                                         op0=ALU.mult, op1=ALU.add).then_inc(x_done, 1)

            dve.sem_inc(diff_ready, 2)
            dve.sem_inc(cb_ready, 1)
            dve.sem_inc(x_done, 1)
            dve.sem_inc(y_taken, 1)
            for b in range(2):
                chain.step(b)
                moments(dve, chain, x, b, w[b]).then_inc(var_ready, 1)
                normalise(dve, x, b, w[b], rstd_ready).then_inc(normed, 1)
            start_time_steps(0)
            time_steps(0, 0)
            for b, p, i in pairs(dve, SEQS):
                dve.wait_ge(sums_up, b + 1)
                dve.tensor_copy(acs[:, :], acs_up).then_inc(y_chain, 1)
                dve.tensor_copy(tot[:, :], tot_up).then_inc(y_chain, 1)
                dve.wait_ge(y_chain, Y_LINKS * b + 2)
                dve.tensor_tensor(to_end[:, :], tot[:, :], acs[:, :], ALU.subtract).then_inc(sums_ready, 1)
                for k in range(TILES):
                    n = b * TILES + k
                    dve.wait_ge(rows_ready, n + 1)
                    dve.wait_ge(decay_ready, n + 1)
                    for h in range(HEADS):
                        last = dve.tensor_scalar(diff[k % 2][:, h, :], rows_up[k % 2][:, h * P:(h + 1) * P],
                                                 acs[:, k * HEADS + h:k * HEADS + h + 1], 0.0,
                                                 ALU.subtract, ALU.min)
                    last.then_inc(diff_ready, 1)
                    dve.wait_ge(cb_multiplied, n + 1)
                    dve.tensor_tensor(cb[k][:, :], cb_up, c.upto[:, :], ALU.mult).then_inc(cb_ready, 1)
                if later(b, 1):
                    start_time_steps(b + 1)
                for k in range(TILES):
                    dve.wait_ge(decay_ready, b * TILES + k + 3)
                    dve.wait_ge(cb_ready, b * TILES + k + 2)
                    dve.tensor_tensor(score[k][:, :, :], decay[k][:, :, :],
                                      cb[k][:, :].rearrange("p (o i) -> p o i", o=1).broadcast_to([P, HEADS, P]),
                                      ALU.mult).then_inc(score_ready, 1)
                if later(b, 1):
                    time_steps(b + 1, 1 - p)
                dve.wait_ge(decays_ready, b + 1)
                for k in range(TILES):
                    n = b * TILES + k
                    done = Y_LINKS * b + 2 + 3 * k
                    dve.tensor_tensor(heads(scaled[:, :]), heads(state[k][:, :]), per_head(chunk_decay, k), ALU.mult
                                      ).then_inc(y_chain, 1)
                    dve.wait_ge(y_chain, done + 1)
                    dve.wait_ge(grown, n + 1)
                    dve.tensor_tensor(state[k + 1][:, :], scaled[:, :], grow_up, ALU.add
                                      ).then_inc(state_ready, 1)
                    dve.wait_ge(y_multiplied, n + 1)
                    dve.tensor_tensor(heads(from_state[:, :]), heads(y_up[:, D_IN:]), per_head(decayed, k), ALU.mult
                                      ).then_inc(y_chain, 1)
                    dve.tensor_tensor(within[:, :], y_up[:, 0:D_IN], xskip[:, k, :], ALU.add).then_inc(y_taken, 1)
                    dve.wait_ge(y_chain, done + 2)
                    dve.wait_ge(y_taken, n + 2)
                    dve.tensor_tensor(ungated[:, :], from_state[:, :], within[:, :], ALU.add).then_inc(y_chain, 1)
                    dve.wait_ge(y_chain, done + 3)
                    dve.tensor_tensor(y[k % 2][:, :], ungated[:, :], zx[p][:, k, 0:D_IN], ALU.mult).then_inc(y_ready, 1)
                    dve.wait_ge(state_ready, n + 1)
                    if k:
                        finish(k - 1, n - 1)
                    if k == 1 and later(b, 2):
                        chain.step(b + 2)
                        moments(dve, chain, x, b + 2, w[p]).then_inc(var_ready, 1)
                    if k == 2 and later(b, 2):
                        normalise(dve, x, b + 2, w[p], rstd_ready).then_inc(normed, 1)
                finish(TILES - 1, b * TILES + TILES - 1)


def attention(nc, x, c, d):
    with ExitStack() as ctx:
        def sb(n, shape, dt=F32):
            return ctx.enter_context(nc.sbuf_tensor(f"att_{n}", shape, dt))

        def sem(n):
            return ctx.enter_context(nc.semaphore(f"att_{n}"))

        def bank(n):
            return ctx.enter_context(nc.psum_tensor(f"att_{n}", [P, 512], F32))

        w = norm_buffers(sb, sem, "norm")
        qkv_w, qkv_bias, q_bias = sb("qkv_w", [P, 3 * P]), sb("qkv_bias", [P, 3 * P]), sb("q_bias", [P, 1])
        out_w, out_bias = sb("out_w", [P, P]), sb("out_bias", [P, P])
        xT = [sb(f"xT{p}", [P, SEQ]) for p in range(2)]
        qT = [sb(f"qT{p}", [P, SEQ]) for p in range(2)]
        qkv = [sb(f"qkv{p}", [P, TILES, 3 * P]) for p in range(2)]
        vk = [sb(f"vk{k}", [P, AH, AD, AD]) for k in range(2)]
        weighted = sb("weighted", [P, AH, AD, AD])
        inside = sb("inside", [P, P])
        state = [sb(f"state{k}", [P, P]) for k in range(TILES + 1)]
        grown = sb("grown", [P, P])
        y = [sb(f"y{k}", [P, P]) for k in range(2)]
        yT = [sb(f"yT{k}", [P, P]) for k in range(2)]

        turned = bank("turned")
        qkv_up = [bank(f"qkv_up{k}") for k in range(2)]
        sums_up = [bank(f"sums_up{m}") for m in range(2)]
        grow_up, before_up, last_up = bank("grow_up")[:, 0:P], bank("before_up")[:, 0:P], bank("last_up")
        yT_up, out_up = last_up[:, 0:P], last_up[:, P:2 * P]

        cleared, loaded, chain_sem, var_ready, rstd_ready, normed, turned_up, xT_ready = (
            sem("cleared"), sem("loaded"), sem("chain"), sem("var_ready"), sem("rstd_ready"), sem("normed"),
            sem("turned_up"), sem("xT_ready"))
        qkv_multiplied, qkv_ready, q_multiplied, qT_ready = (
            sem("qkv_multiplied"), sem("qkv_ready"), sem("q_multiplied"), sem("qT_ready"))
        vk_ready, summed, weighted_ready, grow_ready, masked, state_ready = (
            sem("vk_ready"), sem("summed"), sem("weighted_ready"), sem("grow_ready"), sem("masked"),
            sem("state_ready"))
        inside_ready, before_ready, y_ready, yT_turned, yT_ready, out_ready, x_done = (
            sem("inside_ready"), sem("before_ready"), sem("y_ready"), sem("yT_turned"), sem("yT_ready"),
            sem("out_ready"), sem("x_done"))

        plan = [(qkv_w[:, :], d["qkv_w"]), (q_bias[:, :], d["qkv_b"][0:P].rearrange("(p o) -> p o", o=1)),
                (qkv_bias[:, :], d["qkv_b"].rearrange("(o c) -> o c", o=1).broadcast_to([P, 3 * P])),
                (out_w[:, :], d["att_out_w"]), (out_bias[0:1, :], d["att_out_b"].rearrange("(o c) -> o c", o=1))]
        with nc.Block() as block:
            @block.sync
            def _(sp):
                sp.wait_ge(cleared, 1)
                for dst, src in plan:
                    sp.dma_start(dst, src).then_inc(loaded, 16)
                sp.wait_ge(loaded, 16 * len(plan))

            @block.vector
            def _(dve):
                dve.memset(out_bias[:, :], 0.0).then_inc(cleared, 1)
                dve.memset(state[0][:, :], 0.0)

        block = ctx.enter_context(nc.Block())

        @block.gpsimd
        def _(pool):
            def inverse_root(b, p):
                pool.wait_ge(var_ready, b + 1)
                pool.tensor_tensor(w[p].rstd[:, :], w[p].var[:, :], c.minus_half[:, :], ALU.pow
                                   ).then_inc(rstd_ready, 1)

            inverse_root(0, 0)
            for b, p, i in pairs(pool, SEQS):
                if not is_last(b, SEQS):
                    inverse_root(b + 1, 1 - p)
                for k in range(TILES):
                    n = b * TILES + k
                    pool.wait_ge(qkv_ready, n + 3)
                    pool.wait_ge(summed, n + 1)
                    shape = [P, AH, AD, AD]
                    keys = qkv[p][:, k, P:2 * P].rearrange("p (h o n) -> p h o n", o=1, n=AD).broadcast_to(shape)
                    values = qkv[p][:, k, 2 * P:].rearrange("p (h v o) -> p h v o", v=AD, o=1).broadcast_to(shape)
                    pool.tensor_tensor(vk[k % 2][:, :, :, :], values, keys, ALU.mult).then_inc(vk_ready, 1)

        @block.tensor
        def _(pe):
            def project(b, p):
                pe.wait_ge(normed, b + 1)
                if reaches(b, 1):
                    pe.wait_ge(qT_ready, b)
                for k in range(TILES):
                    last = pe.transpose(turned[:, k * P:(k + 1) * P], w[p].xn[:, k, :], c.ident[:, :])
                last.then_inc(turned_up, 1)
                pe.wait_ge(xT_ready, b + 1)
                for k in range(TILES):
                    pe.wait_ge(qkv_ready, b * TILES + k + 1)
                    pe.matmul(qkv_up[k % 2][:, 0:3 * P], xT[p][:, k * P:(k + 1) * P], qkv_w[:, :],
                              start=True, stop=True).then_inc(qkv_multiplied, 1)
                pe.matmul(turned[:, :], qkv_w[:, 0:P], xT[p][:, :], start=True, stop=True).then_inc(q_multiplied, 1)

            def turn_and_project(k, n):
                pe.wait_ge(y_ready, n + 1)
                pe.wait_ge(x_done, n + 1)
                pe.transpose(yT_up, y[k % 2][:, :], c.ident[:, :]).then_inc(yT_turned, 1)
                pe.wait_ge(yT_ready, n + 1)
                pe.matmul(out_up, yT[k % 2][:, :], out_w[:, :], start=True, stop=False)
                pe.matmul(out_up, c.ones[:, :], out_bias[:, :], start=False, stop=True).then_inc(out_ready, 1)

            pe.sem_inc(summed, 2)
            project(0, 0)
            for b, p, i in pairs(pe, SEQS):
                if not is_last(b, SEQS):
                    project(b + 1, 1 - p)
                for k in range(TILES):
                    n = b * TILES + k
                    pe.wait_ge(vk_ready, n + 1)
                    pe.wait_ge(weighted_ready, 2 * n + 2)
                    flat = vk[k % 2][:, :, :, :].rearrange("p h v n -> p (h v n)")
                    for m in range(2):
                        last = pe.matmul(sums_up[m][:, :], c.upto[:, :], flat[:, m * 512:(m + 1) * 512],
                                         start=True, stop=True)
                    last.then_inc(summed, 1)
                    if k == 0:
                        pe.wait_ge(qT_ready, b + 1)
                        pe.wait_ge(qkv_ready, b * TILES + TILES + 2)
                    else:
                        pe.wait_ge(state_ready, n)
                    pe.matmul(grow_up, qkv[p][:, k, P:2 * P], qkv[p][:, k, 2 * P:], start=True, stop=True
                              ).then_inc(grow_ready, 1)
                    if k:
                        pe.wait_ge(y_ready, n)
                    pe.matmul(before_up, qT[p][:, k * P:(k + 1) * P], state[k][:, :], start=True, stop=True
                              ).then_inc(before_ready, 1)
                    if k:
                        turn_and_project(k - 1, n - 1)
                turn_and_project(TILES - 1, b * TILES + TILES - 1)

        @block.scalar
        def _(act):
            def keep(b, p):
                act.wait_ge(turned_up, b + 1)
                act.activation(xT[p][:, :], turned[:, :], ACT.Copy).then_inc(xT_ready, 1)
                act.wait_ge(q_multiplied, b + 1)
                act.activation(qT[p][:, :], turned[:, :], ACT.Identity, bias=q_bias[:, 0:1]).then_inc(qT_ready, 1)

            keep(0, 0)
            for b, p, i in pairs(act, SEQS):
                if not is_last(b, SEQS):
                    keep(b + 1, 1 - p)
                for k in range(TILES):
                    act.wait_ge(yT_turned, b * TILES + k + 1)
                    act.activation(yT[k % 2][:, :], yT_up, ACT.Copy).then_inc(yT_ready, 1)

        @block.vector
        def _(dve):
            chain = Chain(dve, chain_sem, NORM_LINKS)

            def add_bias(b, p):
                for k in range(TILES):
                    dve.wait_ge(qkv_multiplied, b * TILES + k + 1)
                    dve.tensor_tensor(qkv[p][:, k, :], qkv_up[k % 2][:, 0:3 * P], qkv_bias[:, :], ALU.add
                                      ).then_inc(qkv_ready, 1)

            def finish(n):
                dve.wait_ge(out_ready, n + 1)
                xs = x[:, span(n, 1), :].rearrange("p a c -> p (a c)")
                dve.tensor_tensor(xs, xs, out_up, ALU.add).then_inc(x_done, 1)

            dve.sem_inc(qkv_ready, 2)
            dve.sem_inc(weighted_ready, 2)
            dve.sem_inc(x_done, 1)
            moments(dve, chain, x, 0, w[0]).then_inc(var_ready, 1)
            normalise(dve, x, 0, w[0], rstd_ready).then_inc(normed, 1)
            add_bias(0, 0)
            for b, p, i in pairs(dve, SEQS):
                if not is_last(b, SEQS):
                    chain.step(b + 1)
                    moments(dve, chain, x, b + 1, w[1 - p]).then_inc(var_ready, 1)
                    normalise(dve, x, b + 1, w[1 - p], rstd_ready).then_inc(normed, 1)
                    add_bias(b + 1, 1 - p)
                for k in range(TILES):
                    n = b * TILES + k
                    dve.wait_ge(summed, n + 3)
                    half = [P, AH // 2, AD, AD]
                    for m in range(2):
                        queries = qkv[p][:, k, m * P // 2:(m + 1) * P // 2].rearrange(
                            "p (h o n) -> p h o n", o=1, n=AD).broadcast_to(half)
                        dve.tensor_tensor(weighted[:, m * AH // 2:(m + 1) * AH // 2, :, :],
                                          sums_up[m][:, :].rearrange("p (h v n) -> p h v n", v=AD, n=AD),
                                          queries, ALU.mult).then_inc(weighted_ready, 1)
                    dve.wait_ge(weighted_ready, 2 * n + 4)
                    dve.tensor_reduce(inside[:, :].rearrange("p (h v) -> p h v", v=AD), weighted[:, :, :, :],
                                      AX_X, ALU.add).then_inc(inside_ready, 1)
                    dve.wait_ge(grow_ready, n + 1)
                    dve.tensor_tensor(grown[:, :], grow_up, c.head_block[:, :], ALU.mult).then_inc(masked, 1)
                    dve.wait_ge(masked, n + 1)
                    dve.tensor_tensor(state[k + 1][:, :], state[k][:, :], grown[:, :], ALU.add
                                      ).then_inc(state_ready, 1)
                    dve.wait_ge(before_ready, n + 1)
                    dve.wait_ge(inside_ready, n + 1)
                    dve.tensor_tensor(y[k % 2][:, :], before_up, inside[:, :], ALU.add).then_inc(y_ready, 1)
                    dve.wait_ge(state_ready, n + 1)
                    if k:
                        finish(n - 1)
                finish(b * TILES + TILES - 1)


def start(nc, c, d, x, tables, sums, cleared, ints_loaded):
    first = [(x[:, :, :], d["u"].rearrange("(a p) c -> p a c", p=P)),
             (c.gate_w[:, :], d["gate"]), (c.bias[:, :], d["bias"].rearrange("(o e) -> o e", o=1).broadcast_to([P, E])),
             (c.shared_g[:, :], d["shared_gate"]), (c.shared_u[:, :], d["shared_up"]),
             (c.shared_d[:, 0, :], d["shared_down"])]
    ints = [(c.q_i[0][:, :], d["ffn_gate"]), (c.q_i[1][:, :], d["ffn_up"]), (c.q_i[2][:, :], d["ffn_down"])]
    third = (T + CAP) // P // 3
    zeros = [(t[T:T + CAP, :], c.zeros[:, 0:ROW]) for t in tables] + [
        (s[k * third * P:(k + 1) * third * P, :].rearrange("(p a) c -> p (a c)", p=P), c.zeros[:, 0:third * P])
        for s in sums for k in range(3)]
    with nc.semaphore("start_loaded") as loaded, nc.semaphore("start_zeroed") as zeroed, \
            nc.semaphore("const_made") as made, nc.semaphore("const_masked") as masked, nc.Block() as block:
        @block.sync
        def _(sp):
            for dst, src in first:
                sp.dma_start(dst, src).then_inc(loaded, 16)
            sp.wait_ge(loaded, 16 * len(first))

        @block.scalar
        def _(act):
            act.wait_ge(zeroed, 1)
            act.wait_ge(loaded, 16 * len(first))
            for dst, src in ints:
                act.dma_start(dst, src).then_inc(ints_loaded, 16)
            for dst, src in zeros:
                act.dma_start(dst, src).then_inc(cleared, 16)

        @block.gpsimd
        def _(pool):
            ch = Chain(pool, made)
            ch.link(pool.memset(c.ident[:, :], 0.0))
            ch.link(pool.affine_select(out=c.ident[:, :], in_=c.ident[:, :], compare_op=ALU.not_equal, fill=1.0,
                                       base=0, pattern=[[-1, P]], channel_multiplier=1))
            ch.link(pool.memset(c.ones[:, :], 1.0))
            ch.link(pool.memset(c.ones_bf[:, :], 1.0))
            ch.link(pool.affine_select(out=c.before_bf[:, :], in_=c.ones_bf[:, :], compare_op=ALU.is_gt, fill=0.0,
                                       base=0, pattern=[[1, P]], channel_multiplier=-1))
            ch.link(pool.affine_select(out=c.upto[:, :], in_=c.ones[:, :], compare_op=ALU.is_ge, fill=0.0,
                                       base=0, pattern=[[1, P]], channel_multiplier=-1))
            ch.link(pool.memset(c.earlier_group[:, :, :], 1.0))
            ch.link(pool.affine_select(out=c.earlier_group[:, :, :], in_=c.earlier_group[:, :, :],
                                       compare_op=ALU.is_gt, fill=0.0, base=0,
                                       pattern=[[1, GROUPS], [-1, GROUPS]], channel_multiplier=0))
            ch.link(pool.iota(c.ramp_i[:, :], pattern=[[1, LO]], base=0, channel_multiplier=0))
            ch.link(pool.tensor_copy(c.lo_digit[:, :], c.ramp_i[:, :]))
            ch.link(pool.iota(c.ramp_i[:, :], pattern=[[1, LO]], base=-T // LO, channel_multiplier=0))
            ch.link(pool.tensor_copy(c.hi_digit[:, :], c.ramp_i[:, 0:HI]))
            ch.link(pool.iota(c.part_i[:, :], pattern=[[0, 1]], base=1, channel_multiplier=1))
            ch.link(pool.tensor_copy(c.part1[:, :], c.part_i[:, :]))
            ch.link(pool.iota(c.tile_i[:, :], pattern=[[P, NT]], base=0, channel_multiplier=0))
            ch.link(pool.tensor_copy(c.tile128[:, :], c.tile_i[:, :]))
            ch.link(pool.memset(c.own[:, :], 1.0))
            ch.link(pool.affine_select(out=c.own[:, :], in_=c.own[:, :], compare_op=ALU.is_ge, fill=0.0,
                                       base=0, pattern=[[-HI, EG]], channel_multiplier=1))
            ch.link(pool.affine_select(out=c.own[:, :], in_=c.own[:, :], compare_op=ALU.is_ge, fill=0.0,
                                       base=HI - 1, pattern=[[HI, EG]], channel_multiplier=-1))
            ch.link(pool.iota(c.slot_i[:, :], pattern=[[1, LO]], base=0, channel_multiplier=LO))
            ch.link(pool.memset(c.head_block[:, :], 1.0))
            hb = c.head_block[:, :].rearrange("p (h d) -> p h d", d=AD)
            ch.link(pool.affine_select(out=hb, in_=hb, compare_op=ALU.is_ge, fill=0.0,
                                       base=0, pattern=[[-AD, AH], [0, AD]], channel_multiplier=1))
            ch.link(pool.affine_select(out=hb, in_=hb, compare_op=ALU.is_ge, fill=0.0,
                                       base=AD - 1, pattern=[[AD, AH], [0, AD]], channel_multiplier=-1))

        @block.vector
        def _(dve):
            dve.memset(c.zeros[:, :], 0.0).then_inc(zeroed, 1)
            dve.memset(c.zero_bf[:, :], 0.0)
            dve.memset(c.minus_half[:, :], -0.5)
            dve.memset(c.eps[:, :], EPS)
            dve.wait_ge(made, 20)
            dve.tensor_scalar(c.slot_m[:, :], c.slot_i[:, :], CAP - 1, None, ALU.bitwise_and).then_inc(masked, 1)
            dve.wait_ge(masked, 1)
            dve.tensor_scalar(c.empty_row[:, :], c.slot_m[:, :], float(T + 1), None, ALU.add)

    return 16 * len(zeros), 16 * len(ints)


def cast_integers(nc, c, ints_loaded, count):
    with nc.Block() as block:
        @block.vector
        def _(dve):
            dve.wait_ge(ints_loaded, count)
            for q, f in zip(c.q_i, c.q_f):
                dve.tensor_copy(f[:, :, :].rearrange("p a c -> p (a c)"), q[:, :])


def clear_semaphores(nc):
    used = sorted(int(n) for n in nc.released_uncleared_semaphores)
    runs = []
    for n in used:
        if runs and runs[-1][1] == n:
            runs[-1][1] = n + 1
        else:
            runs.append([n, n + 1])
    with nc.Block() as block:
        @block.gpsimd
        def _(pool):
            for first, end in runs:
                pool.sem_clear(range(first, end))


def store(nc, x, out):
    with nc.semaphore("out_written") as written, nc.Block() as block:
        @block.sync
        def _(sp):
            sp.dma_start(out.rearrange("(a p) c -> p a c", p=P), x[:, :, :]).then_inc(written, 16)
            sp.wait_ge(written, 16)


def program(nc, d, out, layers):
    with ExitStack() as ctx:
        def sb(n, shape, dt):
            return ctx.enter_context(nc.sbuf_tensor(n, shape, dt))

        c = Bag()
        x = sb("x", [P, NT, P], F32)
        for n, shape, dt in (
                ("minus_half", [P, TILES], F32), ("eps", [P, 1], F32), ("ident", [P, P], F32), ("ones", [P, P], F32), ("upto", [P, P], F32),
                ("ones_bf", [P, P], BF16), ("before_bf", [P, P], BF16), ("zero_bf", [P, EG * LO], BF16),
                ("earlier_group", [P, GROUPS, GROUPS], F32), ("ramp_i", [P, LO], I32),
                ("lo_digit", [P, LO], BF16), ("hi_digit", [P, HI], BF16), ("part_i", [P, 1], I32),
                ("part1", [P, 1], F32), ("tile_i", [P, NT], I32), ("tile128", [P, NT], F32),
                ("own", [P, EG], F32), ("slot_i", [P, LO], I32), ("slot_m", [P, LO], I32),
                ("empty_row", [P, LO], F32), ("head_block", [P, P], F32),
                ("gate_w", [P, E], F32), ("bias", [P, E], F32), ("shared_g", [P, P], F32),
                ("shared_u", [P, P], F32), ("shared_d", [P, 1, P], F32)):
            c[n] = sb(n, shape, dt)
        c.q_f = [sb(f"q_f{k}", [P, HM, P], F32) for k in range(3)]

        def dram(n, shape, dt=F32):
            return nc.dram_tensor(n, shape, dt, kind="Internal").ap()

        tables = [dram(f"table{k}", (T + CAP, ROW)) for k in range(2)]
        sums = [[dram(f"sums{k}_{j}", (T + CAP, P)) for j in range(CHAINS)] for k in range(2)]
        lists = [dram(f"row_list{k}", (E * CAP,)) for k in range(2)]
        c.zeros = sb("zeros", [P, (T + CAP) // P // 3 * P], F32)
        c.q_i = [sb(f"q_i{k}", [P, HM * P], I32) for k in range(3)]
        cleared = ctx.enter_context(nc.semaphore("cleared"))
        ints_loaded = ctx.enter_context(nc.semaphore("ints_loaded"))
        zeros_done, ints_done = start(nc, c, d, x, tables, [s for pair in sums for s in pair], cleared, ints_loaded)

        gathered, added = ([[ctx.enter_context(nc.semaphore(f"experts{k}_{n}{p}")) for p in range(many)]
                            for k in range(2)] for n, many in (("gathered", 4), ("added", CHAINS)))

        def moe_layer(k):
            with nc.sbuf_tensor(f"moe{k}_logits", [P, NT, E], F32) as logits, \
                    nc.sbuf_tensor(f"moe{k}_rows", [P, E], U32) as rows:
                moe = Bag()
                moe.gathered, moe.added = gathered[k], added[k]
                moe.cleared, moe.zeros_done = cleared, zeros_done
                moe.logits, moe.rows = logits, rows
                moe.gate, moe.bias, moe.table, moe.sums = c.gate_w, c.bias, tables[k], sums[k]
                moe.row_list, moe.w123 = lists[k], d["w123"]
                ffn_layer(nc, f"shared{k}", sb, x, c, (c.shared_g, c.shared_u, c.shared_d), 1, 1.0, 0.5, moe)
                route(nc, f"route{k}", c, moe)
                experts(nc, f"experts{k}", c, moe)
                combine(nc, f"combine{k}", x, moe)

        def quant_layer(k):
            wg, wu, wd = c.q_f
            ffn_layer(nc, f"ffn{k}", sb, x, c, (wg[:, :, :].rearrange("p a c -> p (a c)"),
                      wu[:, :, :].rearrange("p a c -> p (a c)"), wd), HM, QSCALE, 0.5 * QSCALE)

        for what in layers:
            if what == "moe0":
                moe_layer(0)
            if what == "moe1":
                moe_layer(1)
                clear_semaphores(nc)
            if what == "mamba":
                state_space(nc, x, c, d)
            if what == "ffn0":
                cast_integers(nc, c, ints_loaded, ints_done)
                quant_layer(0)
            if what == "attention":
                attention(nc, x, c, d)
            if what == "ffn1":
                quant_layer(1)
        store(nc, x, out)


LAYERS = ("moe0", "mamba", "moe1", "ffn0", "attention", "ffn1")


def kernel(**inputs):
    import numpy as np
    import concourse.bacc as bacc
    from concourse.bass_utils import run_bass_kernel_spmd

    def turned(a):
        return np.ascontiguousarray(np.asarray(a).T)

    w1, w2, w3 = (np.asarray(inputs[f"L0_ffn_{n}"]) for n in ("w1", "w2", "w3"))
    n_pairs = E // 2
    up1, up3 = (w.reshape(n_pairs, P, P).transpose(0, 2, 1) for w in (w1, w3))
    down2 = w2.transpose(0, 2, 1).reshape(n_pairs, P, P)
    arrays = {
        "u": np.ascontiguousarray(np.asarray(inputs["L0_attn_u"]).reshape(T, P)),
        "gate": turned(inputs["L0_ffn_gate_weight"]),
        "bias": np.ascontiguousarray(inputs["L0_ffn_e_bias"]),
        "w123": np.ascontiguousarray(np.concatenate([up1, up3, down2], axis=2)),
        "shared_gate": turned(inputs["L0_ffn_shared_gate"]),
        "shared_up": turned(inputs["L0_ffn_shared_up"]),
        "shared_down": turned(inputs["L0_ffn_shared_down"]),
        "ffn_gate": turned(inputs["L1_ffn_w_gate"]),
        "ffn_up": turned(inputs["L1_ffn_w_up"]),
        "ffn_down": np.ascontiguousarray(
            turned(inputs["L1_ffn_w_down"]).reshape(HM, P, P).transpose(1, 0, 2).reshape(P, HM * P)),
    }
    in_w, conv_b = np.asarray(inputs["L0_attn_in_proj_w"]), np.asarray(inputs["L0_attn_conv_b"])
    arrays |= {
        "in_zdt": turned(np.concatenate([in_w[:D_IN], in_w[D_IN + 4 * P:]])),
        "in_xbc": turned(in_w[D_IN:D_IN + 4 * P]),
        "conv_w": turned(inputs["L0_attn_conv_w"]).reshape(-1),
        "conv_b": np.ascontiguousarray(conv_b),
        "feature_b": turned(conv_b[D_IN:].reshape(2, P)),
        "dt_bias": np.ascontiguousarray(inputs["L0_attn_dt_bias"]),
        "A_log": np.ascontiguousarray(inputs["L0_attn_A_log"]),
        "D": np.ascontiguousarray(inputs["L0_attn_D"]),
        "norm_w": turned(np.asarray(inputs["L0_attn_norm_w"]).reshape(2, P)),
        "out_w": turned(inputs["L0_attn_out_proj_w"]),
        "qkv_w": turned(np.concatenate([np.asarray(inputs[f"L1_attn_W{n}"]) for n in "qkv"])),
        "qkv_b": np.concatenate([np.asarray(inputs[f"L1_attn_b{n}"]) for n in "qkv"]),
        "att_out_w": turned(inputs["L1_attn_Wo"]),
        "att_out_b": np.ascontiguousarray(inputs["L1_attn_bo"]),
    }
    nc = bacc.Bacc("TRN2", target_bir_lowering=False, num_devices=1)
    d = {n: nc.dram_tensor(f"in_{n}", a.shape, mybir.dt.from_np(a.dtype), kind="ExternalInput").ap()
         for n, a in arrays.items()}
    out = nc.dram_tensor("out", (T, P), F32, kind="ExternalOutput").ap()
    program(nc, d, out, LAYERS)
    r = run_bass_kernel_spmd(nc, [{f"in_{n}": a for n, a in arrays.items()}], core_ids=[0])
    return r.results[0]["out"].reshape(SEQS, SEQ, P)
```

```python
from contextlib import ExitStack

import concourse.bass as bass
from concourse import mybir

ALU = mybir.AluOpType
ACT = mybir.ActivationFunctionType
AX_X = mybir.AxisListType.X
F32 = mybir.dt.float32
BF16 = mybir.dt.bfloat16
I32 = mybir.dt.int32
U32 = mybir.dt.uint32

P = 128
SEQS = 8
TILES = 4
NT = SEQS * TILES
T = NT * P
SEQ = TILES * P
EPS = 1e-5

E = 64
CAP = 128
TOPK = 8
GROUPS = 8
TOP_GROUPS = 4
ROW = P + E
HI, LO = 8, 16
EG = P // HI
BATCH = 8
CHAINS = 2

HIDDEN = 384
HM = HIDDEN // P
QSCALE = 1.0 / 127.0

D_IN = 256
HEADS = 4
HD = D_IN // HEADS
ZDT = D_IN + HEADS
TAPS = 4

AH = 16
AD = P // AH


def pairs(eng, n, peel_first=False, by=2):
    if peel_first:
        for p in range(by):
            yield p, p, 0
    with eng.Fori(1 if peel_first else 0, n // by - 1) as i:
        for p in range(by):
            yield i * by + p, p, i
    for p in range(by):
        yield n - by + p, p, n // by - 1


def is_last(b, n):
    return isinstance(b, int) and b == n - 1


def reaches(b, n):
    return not isinstance(b, int) or b >= n


def later(b, n):
    return not isinstance(b, int) or b + n < SEQS


def span(first, n):
    return bass.ds(first, n)


class Chain:

    def __init__(self, eng, sem, per_step=0):
        self.eng, self.sem, self.per_step, self.base, self.n = eng, sem, per_step, 0, 0

    def step(self, b):
        if self.n:
            assert self.n == self.per_step, (self.n, self.per_step)
        self.base, self.n = b * self.per_step, 0

    def link(self, ins):
        self.n += 1
        ins.then_inc(self.sem, 1)
        self.eng.wait_ge(self.sem, self.base + self.n)


NORM_LINKS = 2


def moments(dve, chain, x, b, w):
    for k in range(TILES):
        last = dve.bn_stats(w.stats[:, k, :], x[:, span(b * TILES + k, 1), :].rearrange("p a c -> p (a c)"))
    chain.link(last)
    dve.sem_inc(w.passed, 1)
    for k in range(TILES):
        last = dve.bn_aggr(w.mv[:, k, :], w.stats[:, k, :])
    chain.link(last)
    return dve.tensor_scalar(w.var[:, :], w.mv[:, :, 1], EPS, None, ALU.add)


def inverse_roots(pool, c, w, var_ready, rstd_ready):
    for b, p, i in pairs(pool, SEQS):
        pool.wait_ge(var_ready, b + 1)
        pool.tensor_tensor(w[p].rstd[:, :], w[p].var[:, :], c.minus_half[:, :], ALU.pow).then_inc(rstd_ready, 1)


def normalise(dve, x, b, w, rstd_ready):
    dve.wait_ge(rstd_ready, b + 1)
    for k in range(TILES):
        last = dve.tensor_scalar(w.xn[:, k, :], x[:, span(b * TILES + k, 1), :].rearrange("p a c -> p (a c)"),
                                 w.mv[:, k, 0:1], w.rstd[:, k:k + 1], ALU.subtract, ALU.mult)
    return last


class Bag(dict):

    def __getattr__(self, n):
        return self[n]

    def __setattr__(self, n, v):
        self[n] = v


def norm_buffers(sb, sem, name):
    out = []
    passed = sem(f"{name}_passed")
    for p in range(2):
        w = Bag()
        w.passed = passed
        w.stats = sb(f"{name}_stats{p}", [P, TILES, 6], F32)
        w.mv = sb(f"{name}_mv{p}", [P, TILES, 2], F32)
        w.var = sb(f"{name}_var{p}", [P, TILES], F32)
        w.rstd = sb(f"{name}_rstd{p}", [P, TILES], F32)
        w.xn = sb(f"{name}_xn{p}", [P, TILES, P], F32)
        out.append(w)
    return out


class ExpertSums:

    def __init__(self, sb, sem, moe):
        self.moe = moe
        self.part = [[sb(f"part{p}{k}", [P, TILES, P], F32) for k in range(CHAINS)] for p in range(2)]
        self.landed = [sem(f"part_landed{p}") for p in range(2)]
        self.joined, self.passed = sem("joined"), sem("join_passed")

    def load(self, sp):
        for b, p, i in pairs(sp, SEQS):
            sp.wait_ge(self.joined, 2 * b + 2)
            for k in range(CHAINS):
                sp.dma_start(self.part[p][k][:, :, :], self.moe.sums[k][0:T, :].rearrange("(a p) c -> p a c", p=P)
                             [:, span(b * TILES, TILES), :]).then_inc(self.landed[p], 16)

    def join(self, dve, x, b, p, i):
        dve.wait_ge(self.landed[p], 16 * CHAINS * i + 16 * CHAINS)
        xs = x[:, span(b * TILES, TILES), :]
        for k in range(CHAINS):
            dve.tensor_tensor(xs, xs, self.part[p][k][:, :, :], ALU.add).then_inc(self.joined, 1)
            dve.wait_ge(self.joined, 2 * b + k + 5)
        dve.sem_inc(self.passed, 1)


def ffn_layer(nc, name, sb_, x, c, weights, blocks, gate_scale, out_scale, moe=None,
              before=None, out=None):
    with ExitStack() as ctx:
        def sb(n, shape, dt):
            return ctx.enter_context(nc.sbuf_tensor(f"{name}_{n}", shape, dt))

        def sem(n):
            return ctx.enter_context(nc.semaphore(f"{name}_{n}"))

        def bank(n):
            return ctx.enter_context(nc.psum_tensor(f"{name}_{n}", [P, 512], F32))

        w = norm_buffers(sb, sem, "norm")
        xT = [sb(f"xT{p}", [P, SEQ], F32) for p in range(2)]
        sil = [sb(f"sil{p}", [P, SEQ], F32) for p in range(2)]
        h = [sb(f"h{p}", [P, blocks, SEQ], F32) for p in range(2)]
        turned = bank("turned")
        gate = [bank(f"gate{p}") for p in range(2)]
        up = [bank(f"up{p}") for p in range(2)]
        down = bank("down")
        chain_sem, normed, turned_up, xT_ready = sem("chain"), sem("normed"), sem("turned_up"), sem("xT_ready")
        gate_ready, up_ready, sil_ready, h_ready, down_ready = (
            sem("gate_ready"), sem("up_ready"), sem("sil_ready"), sem("h_ready"), sem("down_ready"))
        var_ready, rstd_ready, table_written = (
            sem("var_ready"), sem("rstd_ready"), [sem(f"table_written{p}") for p in range(2)])
        if moe:
            logits_ready, logits_kept = sem("logits_ready"), sem("logits_kept")
        if out is not None:
            x_done = sem("x_done")
        if moe:
            logits = bank("logits")
        sums = ExpertSums(sb, sem, before) if before else None
        block = ctx.enter_context(nc.Block())
        wg, wu, wd = weights

        @block.gpsimd
        def _(pool):
            inverse_roots(pool, c, w, var_ready, rstd_ready)

        @block.vector
        def _(dve):
            chain = Chain(dve, chain_sem, NORM_LINKS)

            def update(b):
                dve.wait_ge(down_ready, b + 1)
                xs = x[:, span(b * TILES, TILES), :].rearrange("p a c -> p (a c)")
                last = dve.scalar_tensor_tensor(out=xs, in0=down[:, :], scalar=out_scale, in1=xs,
                                                op0=ALU.mult, op1=ALU.add)
                if out is not None:
                    last.then_inc(x_done, 1)

            dve.sem_inc(h_ready, 2)
            if sums:
                dve.sem_inc(sums.joined, 4)
            for b in range(2):
                if sums:
                    sums.join(dve, x, b, b, 0)
                chain.step(b)
                moments(dve, chain, x, b, w[b]).then_inc(var_ready, 1)
                normalise(dve, x, b, w[b], rstd_ready).then_inc(normed, 1)
            if moe:
                dve.wait_ge(moe.x_loaded, 16)
            for b, p, i in pairs(dve, SEQS, peel_first=True):
                if later(b, 2):
                    if sums:
                        sums.join(dve, x, b + 2, p, i + 1)
                    chain.step(b + 2)
                    moments(dve, chain, x, b + 2, w[p]).then_inc(var_ready, 1)
                for m in range(blocks):
                    if m == min(1, blocks - 1) and reaches(b, 1):
                        update(b - 1)
                    dve.wait_ge(sil_ready, b * blocks + m + 1)
                    dve.wait_ge(up_ready, b * blocks + m + 1)
                    q = (blocks * p + m) % 2
                    dve.scalar_tensor_tensor(out=h[p][:, m, :], in0=up[q][:, :], scalar=gate_scale, in1=sil[q][:, :],
                                             op0=ALU.mult, op1=ALU.mult).then_inc(h_ready, 1)
                    if m == blocks - 1 and later(b, 2):
                        if moe:
                            dve.wait_ge(table_written[p], i * 16 + 16)
                        normalise(dve, x, b + 2, w[p], rstd_ready).then_inc(normed, 1)
            update(SEQS - 1)

        @block.tensor
        def _(pe):
            def turn(b, p):
                pe.wait_ge(normed, b + 1)
                for k in range(TILES):
                    last = pe.transpose(turned[:, k * P:(k + 1) * P], w[p].xn[:, k, :], c.ident[:, :])
                last.then_inc(turned_up, 1)

            def multiply_down(b, p):
                pe.wait_ge(h_ready, b * blocks + blocks + 2)
                for k in range(TILES):
                    for m in range(blocks):
                        last = pe.matmul(down[:, k * P:(k + 1) * P], h[p][:, m, k * P:(k + 1) * P], wd[:, m, :],
                                         start=(m == 0), stop=(m == blocks - 1))
                last.then_inc(down_ready, 1)

            turn(0, 0)
            for b, p, i in pairs(pe, SEQS, peel_first=True):
                pe.wait_ge(xT_ready, b + 1)
                if moe:
                    pe.wait_ge(logits_kept, b + 1)
                    for k in range(TILES):
                        last = pe.matmul(logits[:, k * E:(k + 1) * E], xT[p][:, k * P:(k + 1) * P], moe.gate[:, :],
                                         start=True, stop=True)
                    last.then_inc(logits_ready, 1)
                for m in range(blocks):
                    q = (blocks * p + m) % 2
                    pe.wait_ge(h_ready, b * blocks + m + 1)
                    pe.matmul(gate[q][:, :], wg[:, m * P:(m + 1) * P], xT[p][:, :],
                              start=True, stop=True).then_inc(gate_ready, 1)
                    pe.matmul(up[q][:, :], wu[:, m * P:(m + 1) * P], xT[p][:, :],
                              start=True, stop=True).then_inc(up_ready, 1)
                    if m == 0 and reaches(b, 1):
                        multiply_down(b - 1, 1 - p)
                if not is_last(b, SEQS):
                    turn(b + 1, 1 - p)
            multiply_down(SEQS - 1, 1)

        @block.scalar
        def _(act):
            def keep(b, p):
                act.wait_ge(turned_up, b + 1)
                act.activation(xT[p][:, :], turned[:, :], ACT.Copy).then_inc(xT_ready, 1)

            if moe:
                act.sem_inc(logits_kept, 1)
            keep(0, 0)
            for b, p, i in pairs(act, SEQS):
                if moe:
                    act.wait_ge(logits_ready, b + 1)
                    act.activation(moe.logits[:, span(b * TILES, TILES), :].rearrange("p a e -> p (a e)"),
                                   logits[:, 0:TILES * E], ACT.Copy).then_inc(logits_kept, 1)
                for m in range(blocks):
                    q = (blocks * p + m) % 2
                    act.wait_ge(gate_ready, b * blocks + m + 1)
                    act.activation(sil[q][:, :], gate[q][:, :], ACT.Silu, scale=gate_scale).then_inc(sil_ready, 1)
                if not is_last(b, SEQS):
                    keep(b + 1, 1 - p)

        if sums:
            @block.sync
            def _(sp):
                sums.load(sp)

        if out is not None:
            @block.sync
            def _(sp):
                written = table_written[0]
                rows = out.rearrange("(a p) c -> p a c", p=P)
                for b, p, i in pairs(sp, SEQS):
                    sp.wait_ge(x_done, b + 1)
                    now = span(b * TILES, TILES)
                    sp.dma_start(rows[:, now, :], x[:, now, :]).then_inc(written, 16)
                sp.wait_ge(written, 16 * SEQS)

        if moe:
            @block.sync
            def _(sp):
                rows = moe.table[0:T, :].rearrange("(a p) c -> p a c", p=P)
                for b, p, i in pairs(sp, SEQS):
                    sp.wait_ge(normed, b + 1)
                    sp.dma_start(rows[:, span(b * TILES, TILES), 0:P], w[p].xn[:, :, :]).then_inc(table_written[p], 16)
                sp.wait_ge(table_written[0], SEQS // 2 * 16)
                sp.wait_ge(table_written[1], SEQS // 2 * 16)


def route(nc, name, c, moe):
    with ExitStack() as ctx:
        def sb(n, shape, dt):
            return ctx.enter_context(nc.sbuf_tensor(f"{name}_{n}", shape, dt))

        def sem(n):
            return ctx.enter_context(nc.semaphore(f"{name}_{n}"))

        def bank(n):
            return ctx.enter_context(nc.psum_tensor(f"{name}_{n}", [P, 512], F32))

        score = sb("score", [P, NT, E], F32)
        pick = sb("pick", [P, NT, E], BF16)
        ahead = sb("ahead", [P, NT, E], BF16)
        total = sb("total", [P, NT], F32)
        inv = sb("inv", [P, NT], F32)
        inv2 = sb("inv2", [P, NT], F32)
        hi_bf, lo_bf = sb("hi_bf", [P, NT, E], BF16), sb("lo_bf", [P, NT, E], BF16)
        found = sb("found", [P, E // EG, LO], F32)
        empty = sb("empty", [P, E // EG, LO], F32)
        own_part = sb("own_part", [P, LO, EG], F32)
        by_expert = sb("by_expert", [E, CAP], F32)
        with ExitStack() as choosing:
            def early(n, shape, dt):
                return choosing.enter_context(nc.sbuf_tensor(f"{name}_{n}", shape, dt))

            choice = early("choice", [P, NT, E], F32)
            left = early("left", [P, NT, E], F32)
            hi8 = early("hi8", [P, NT, GROUPS, 4], F32)
            lo8 = early("lo8", [P, NT, GROUPS, 4], F32)
            hi4 = early("hi4", [P, NT, GROUPS, 2], F32)
            lo4 = early("lo4", [P, NT, GROUPS, 2], F32)
            lo4b = early("lo4b", [P, NT, GROUPS, 2], F32)
            g1, g2, g3 = (early(f"g{k}", [P, NT, GROUPS], F32) for k in range(3))
            beats = early("beats", [P, NT, GROUPS, GROUPS], BF16)
            ties = early("ties", [P, NT, GROUPS, GROUPS], BF16)
            top = early("top", [P, NT, TOPK], F32)
            place = early("place", [P, NT, E], I32)
            hi = early("hi", [P, NT, E], I32)
            lo = early("lo", [P, NT, E], I32)
        is_hi, part_hi, tile_hi = ([sb(f"{n}{p}", [P, BATCH, E // EG, HI, EG], BF16) for p in range(2)]
                                   for n in ("is_hi", "part_hi", "tile_hi"))
        is_lo = [sb(f"is_lo{p}", [P, LO, BATCH, E], BF16) for p in range(2)]

        counts = [bank(f"counts{k}") for k in range(4)]
        slots = [bank(f"slots{k}") for k in range(4)]
        chain_sem, scored, picked, counted = sem("chain"), sem("scored"), sem("picked"), sem("counted")
        weights_written, weighted_ready, used, rows_found = (
            sem("weights_written"), sem("weighted_ready"), sem("used"), sem("rows_found"))
        rows_written, rows_read, rows_turned = sem("rows_written"), sem("rows_read"), sem("rows_turned")
        weights_ready = sem("weights_ready")
        digits, hi_ready, lo_ready = sem("digits"), sem("hi_ready"), sem("lo_ready")
        block = ctx.enter_context(nc.Block())

        def flat(t):
            return t[:, :, :].rearrange("p a e -> p (a e)")

        def over_groups(t):
            return t[:, :, :].rearrange("p a (g e) -> p a g e", g=GROUPS)

        @block.scalar
        def _(act):
            act.activation(flat(score), flat(moe.logits), ACT.Sigmoid).then_inc(scored, 1)
            act.wait_ge(digits, 1)
            act.activation(flat(hi_bf), flat(hi), ACT.Copy).then_inc(digits, 1)
            for j, p, i in pairs(act, NT // BATCH):
                act.wait_ge(hi_ready, j + 1)
                for t in range(BATCH):
                    act.activation(tile_hi[p][:, t, :, :, :].rearrange("p g h e -> p (g h e)"),
                                   is_hi[p][:, t, :, :, :].rearrange("p g h e -> p (g h e)"), ACT.Copy,
                                   scale=c.tile128[:, span(j * BATCH + t, 1)]).then_inc(weighted_ready, 1)
            act.wait_ge(rows_turned, 1)
            act.activation(moe.rows[:, :], slots[0][:, 0:E], ACT.Copy).then_inc(weighted_ready, 1)

        @block.vector
        def _(dve):
            ch = Chain(dve, chain_sem)
            dve.wait_ge(scored, 1)
            bias = moe.bias[:, :].rearrange("p (a e) -> p a e", a=1).broadcast_to([P, NT, E])
            ch.link(dve.tensor_tensor(choice[:, :, :], score[:, :, :], bias, ALU.add))
            v = over_groups(choice)
            dve.tensor_tensor(hi8[:, :, :, :], v[:, :, :, 0:4], v[:, :, :, 4:8], ALU.max)
            ch.link(dve.tensor_tensor(lo8[:, :, :, :], v[:, :, :, 0:4], v[:, :, :, 4:8], ALU.min))
            dve.tensor_tensor(hi4[:, :, :, :], hi8[:, :, :, 0:2], hi8[:, :, :, 2:4], ALU.max)
            dve.tensor_tensor(lo4[:, :, :, :], hi8[:, :, :, 0:2], hi8[:, :, :, 2:4], ALU.min)
            ch.link(dve.tensor_tensor(lo4b[:, :, :, :], lo8[:, :, :, 0:2], lo8[:, :, :, 2:4], ALU.max))
            ch.link(dve.tensor_tensor(lo4[:, :, :, :], lo4[:, :, :, :], lo4b[:, :, :, :], ALU.max))
            dve.tensor_tensor(g1[:, :, :], hi4[:, :, :, 0], hi4[:, :, :, 1], ALU.max)
            dve.tensor_tensor(g2[:, :, :], hi4[:, :, :, 0], hi4[:, :, :, 1], ALU.min)
            ch.link(dve.tensor_tensor(g3[:, :, :], lo4[:, :, :, 0], lo4[:, :, :, 1], ALU.max))
            ch.link(dve.tensor_tensor(g2[:, :, :], g2[:, :, :], g3[:, :, :], ALU.max))
            ch.link(dve.tensor_tensor(g1[:, :, :], g1[:, :, :], g2[:, :, :], ALU.add))
            shape = [P, NT, GROUPS, GROUPS]
            other = g1[:, :, :].rearrange("p a (o g) -> p a o g", o=1).broadcast_to(shape)
            self_ = g1[:, :, :].rearrange("p a (g o) -> p a g o", o=1).broadcast_to(shape)
            earlier = c.earlier_group[:, :, :].rearrange("p (o g) h -> p o g h", o=1).broadcast_to(shape)
            dve.tensor_tensor(beats[:, :, :, :], other, self_, ALU.is_gt)
            ch.link(dve.tensor_tensor(ties[:, :, :, :], other, self_, ALU.is_equal))
            ch.link(dve.tensor_tensor(ties[:, :, :, :], ties[:, :, :, :], earlier, ALU.mult))
            ch.link(dve.tensor_tensor(beats[:, :, :, :], beats[:, :, :, :], ties[:, :, :, :], ALU.add))
            ch.link(dve.tensor_reduce(g2[:, :, :], beats[:, :, :, :], AX_X, ALU.add))
            ch.link(dve.tensor_scalar(g3[:, :, :], g2[:, :, :], float(TOP_GROUPS), None, ALU.is_lt))
            kept = g3[:, :, :].rearrange("p a (g o) -> p a g o", o=1).broadcast_to([P, NT, GROUPS, E // GROUPS])
            ch.link(dve.tensor_tensor(v, v, kept, ALU.mult))
            for j in range(NT):
                last = dve.max(top[:, j, :], choice[:, j, :])
            ch.link(last)
            for j in range(NT):
                last = dve.match_replace(left[:, j, :], top[:, j, :], choice[:, j, :], -1e30)
            ch.link(last)
            ch.link(dve.tensor_tensor(flat(pick), flat(left), flat(choice), ALU.not_equal))
            ch.link(dve.memset(ahead[:, 0, :], 0.0))
            for j in range(1, NT):
                ch.link(dve.tensor_tensor(ahead[:, j, :], ahead[:, j - 1, :], pick[:, j - 1, :], ALU.add))
            dve.sem_inc(picked, 1)
            ch.link(dve.tensor_tensor(flat(score), flat(score), flat(pick), ALU.mult))
            ch.link(dve.tensor_reduce(total[:, :], score[:, :, :], AX_X, ALU.add))
            ch.link(dve.tensor_scalar(total[:, :], total[:, :], 1e-20, None, ALU.add))
            ch.link(dve.reciprocal(inv[:, :], total[:, :]))
            ch.link(dve.tensor_scalar(inv2[:, :], inv[:, :], 1.25, None, ALU.mult))
            dve.tensor_tensor(score[:, :, :], score[:, :, :],
                              inv2[:, :].rearrange("p (a o) -> p a o", o=1).broadcast_to([P, NT, E]),
                              ALU.mult).then_inc(weights_ready, 1)
            for k in range(4):
                dve.wait_ge(counted, k + 1)
                s = slice(8 * k, 8 * k + 8)
                last = dve.scalar_tensor_tensor(
                    out=place[:, s, :].rearrange("p a e -> p (a e)"),
                    in0=pick[:, s, :].rearrange("p a e -> p (a e)"), scalar=-float(T),
                    in1=counts[k][:, :], op0=ALU.mult, op1=ALU.add)
            ch.link(last)
            dve.tensor_scalar(flat(hi), flat(place), 4, None, ALU.arith_shift_right).then_inc(digits, 1)
            ch.link(dve.tensor_scalar(flat(lo), flat(place), LO - 1, None, ALU.bitwise_and))
            ch.link(dve.tensor_copy(flat(lo_bf), flat(lo)))
            dve.wait_ge(digits, 2)
            for j, p, i in pairs(dve, NT // BATCH):
                dve.wait_ge(used, j + 1)
                hi_digits = hi_bf[:, span(j * BATCH, BATCH), :].rearrange("p a (g e) -> p (a g) e", e=EG)
                lo_digits = lo_bf[:, span(j * BATCH, BATCH), :].rearrange("p a e -> p (a e)")

                def hi_digit(t, h):
                    return t[:, :, :, h, :].rearrange("p a g e -> p (a g) e")

                for h in range(HI):
                    last = dve.tensor_scalar(hi_digit(is_hi[p], h), hi_digits, float(h - T // LO), None, ALU.is_equal)
                last.then_inc(hi_ready, 1)
                for h in range(HI):
                    dve.tensor_scalar(hi_digit(part_hi[p], h), hi_digits, float(h - T // LO), c.part1[:, 0:1],
                                      ALU.is_equal, ALU.mult)
                for l in range(LO):
                    last = dve.tensor_scalar(is_lo[p][:, l, :, :].rearrange("p a e -> p (a e)"), lo_digits, float(l), None, ALU.is_equal)
                last.then_inc(lo_ready, 1)
            dve.wait_ge(used, NT // BATCH + 2)
            for g in range(E // EG):
                ch.link(dve.tensor_tensor(own_part[:, :, :],
                                          slots[g][:, 0:EG * LO].rearrange("p (l e) -> p l e", l=LO),
                                          c.own[:, :].rearrange("p (o e) -> p o e", o=1).broadcast_to([P, LO, EG]),
                                          ALU.mult))
                ch.link(dve.tensor_reduce(found[:, g, :], own_part[:, :, :], AX_X, ALU.add))
            ch.link(dve.tensor_scalar(flat(empty), flat(found), 0.0, None, ALU.is_equal))
            ch.link(dve.tensor_tensor(empty[:, :, :], empty[:, :, :],
                                      c.empty_row[:, :].rearrange("p (o l) -> p o l", o=1)
                                      .broadcast_to([P, E // EG, LO]), ALU.mult))
            dve.scalar_tensor_tensor(out=flat(found), in0=flat(found), scalar=-1.0, in1=flat(empty),
                                     op0=ALU.add, op1=ALU.add).then_inc(rows_found, 1)

        @block.tensor
        def _(pe):
            pe.wait_ge(picked, 1)
            for k in range(4):
                s = slice(8 * k, 8 * k + 8)
                pe.matmul(counts[k][:, :], c.before_bf[:, :], pick[:, s, :].rearrange("p a e -> p (a e)"),
                          start=True, stop=False)
                pe.matmul(counts[k][:, :], c.ones_bf[:, :], ahead[:, s, :].rearrange("p a e -> p (a e)"),
                          start=False, stop=True).then_inc(counted, 1)
            for g in range(E // EG):
                pe.matmul(slots[g][:, 0:EG * LO], c.zero_bf[:, 0:P], c.zero_bf[:, 0:EG * LO], start=True, stop=False,
                          skip_group_check=True)
            pe.sem_inc(used, 2)
            for j, p, i in pairs(pe, NT // BATCH):
                pe.wait_ge(lo_ready, j + 1)
                for t in range(BATCH):
                    pe.wait_ge(weighted_ready, j * BATCH + t + 1)
                    for g in range(E // EG):
                        own = slice(g * EG, (g + 1) * EG)
                        rhs = is_lo[p][:, :, t, own]
                        for lhs in (part_hi, tile_hi):
                            last = pe.matmul(slots[g][:, 0:EG * LO], lhs[p][:, t, g, :, :].rearrange("p h e -> p (h e)"), rhs,
                                             start=False, stop=is_last(j, NT // BATCH) and t == BATCH - 1 and lhs is tile_hi,
                                             skip_group_check=True)
                last.then_inc(used, 1)
            pe.wait_ge(rows_read, 16)
            pe.transpose(slots[0][:, 0:E], by_expert[:, :], c.ident[0:E, 0:E]).then_inc(rows_turned, 1)

        @block.sync
        def _(sp):
            sp.wait_ge(weights_ready, 1)
            sp.dma_start(moe.table[0:T, :].rearrange("(a p) c -> p a c", p=P)[:, :, P:ROW],
                         score[:, :, :]).then_inc(weights_written, 16)
            sp.wait_ge(rows_found, 1)
            for h in range(HI):
                sp.dma_start(moe.row_list.rearrange("(g e h l) -> h e g l", e=EG, h=HI, l=LO)[h],
                             found[h * EG:(h + 1) * EG, :, :]).then_inc(rows_written, 16)
            sp.wait_ge(rows_written, 16 * HI)
            sp.dma_start(by_expert[:, :], moe.row_list.rearrange("(e s) -> e s", s=CAP)).then_inc(rows_read, 16)
            sp.wait_ge(weights_written, 16)


def experts(nc, name, c, moe):
    n_pairs = E // 2
    ring = 4
    ahead = 2
    with ExitStack() as ctx:
        def sb(n, shape, dt):
            return ctx.enter_context(nc.sbuf_tensor(f"{name}_{n}", shape, dt))

        def sem(n):
            return ctx.enter_context(nc.semaphore(f"{name}_{n}"))

        def bank(n):
            return ctx.enter_context(nc.psum_tensor(f"{name}_{n}", [P, 512], F32))

        row = [[sb(f"row{p}{k}", [P, 1], U32) for k in range(2)] for p in range(ring)]
        row_out = [[sb(f"row_out{p}{k}", [P, 1], U32) for k in range(2)] for p in range(2)]
        xg = [[sb(f"xg{p}{k}", [P, ROW], F32) for k in range(2)] for p in range(ring)]
        xgT = [sb(f"xgT{p}", [P, 2 * CAP], F32) for p in range(2)]
        w123 = [sb(f"w123{p}", [P, 3 * P], F32) for p in range(ring)]
        sil = [sb(f"sil{p}", [P, CAP], F32) for p in range(2)]
        h = [sb(f"h{p}", [P, CAP], F32) for p in range(2)]
        y = [[sb(f"y{p}{k}", [P, P], F32) for k in range(2)] for p in range(2)]
        turned = [bank(f"turned{p}") for p in range(2)]
        gate_up = [bank(f"gate_up{p}") for p in range(2)]
        down = [[bank(f"down{p}{k}") for k in range(2)] for p in range(2)]
        row_staged, gathered, loaded = (
            sem("row_staged"), moe.gathered, [sem(f"loaded{p}") for p in range(ring)])
        turned_up, xgT_ready, gate_ready, sil_ready, h_ready, down_ready, y_ready = (
            sem("turned_up"), sem("xgT_ready"), sem("gate_ready"), sem("sil_ready"), sem("h_ready"),
            sem("down_ready"), sem("y_ready"))
        passed = sem("passed")
        added = moe.added
        block = ctx.enter_context(nc.Block())

        @block.gpsimd
        def _(pool):
            def gather(r, p):
                if reaches(r, ring):
                    pool.wait_ge(y_ready, 2 * (r - ring + 1))
                pool.wait_ge(row_staged, r + 1)
                pool.sem_inc(passed, 1)
                for k in range(2):
                    pool.indirect_dma_start(xg[p][k][:, :], None, moe.table[:, :],
                                            bass.IndirectOffsetOnAxis(ap=row[p][k][:, :], axis=0)
                                            ).then_inc(gathered[p], 16)

            pool.wait_ge(moe.cleared, moe.zeros_done)
            for r in range(ahead):
                gather(r, r)
            for r, p, i in pairs(pool, n_pairs, peel_first=True, by=ring):
                if not isinstance(r, int) or r + ahead < n_pairs:
                    gather(r + ahead, (p + ahead) % ring)
                for k in range(2):
                    pool.wait_ge(y_ready, 2 * r + k + 1)
                    if reaches(r, 1):
                        pool.wait_ge(added[k], r * 16)
                        pool.sem_inc(passed, 1)
                    pool.indirect_dma_start(moe.sums[k][:, :],
                                            bass.IndirectOffsetOnAxis(ap=row_out[p % 2][k][:, :], axis=0),
                                            y[p % 2][k][:, :], None, compute_op=ALU.add).then_inc(added[k], 16)
            for k in range(CHAINS):
                pool.wait_ge(added[k], n_pairs * 16)

        @block.sync
        def _(sp):
            for r, p, i in pairs(sp, n_pairs, peel_first=True, by=ring):
                if reaches(r, ring):
                    sp.wait_ge(y_ready, 2 * (r - ring + 1))
                sp.dma_start(w123[p][:, :], moe.w123[span(r, 1), :, :].rearrange("a p c -> (a p) c")
                             ).then_inc(loaded[p], 16)

        @block.tensor
        def _(pe):
            def turn(r, p, i):
                pe.wait_ge(gathered[p], 32 * i + 32)
                for k in range(2):
                    last = pe.transpose(turned[p % 2][:, k * P:(k + 1) * P], xg[p][k][:, 0:P], c.ident[:, :])
                last.then_inc(turned_up, 1)

            turn(0, 0, 0)
            for r, p, i in pairs(pe, n_pairs, by=ring):
                pe.wait_ge(xgT_ready, r + 1)
                pe.wait_ge(loaded[p], 16 * i + 16)
                for m in range(2):
                    for k in range(2):
                        last = pe.matmul(gate_up[p % 2][k * E:(k + 1) * E, m * CAP:(m + 1) * CAP],
                                         w123[p][:, m * P + k * E:m * P + (k + 1) * E],
                                         xgT[p % 2][:, k * CAP:(k + 1) * CAP], start=True, stop=True)
                last.then_inc(gate_ready, 1)
                if not is_last(r, n_pairs):
                    turn(r + 1, (p + 1) % ring, i + (p + 1) // ring)
                pe.wait_ge(h_ready, r + 1)
                for k in range(2):
                    last = pe.matmul(down[p % 2][k][:, 0:P], h[p % 2][k * E:(k + 1) * E, :],
                                     w123[p][k * E:(k + 1) * E, 2 * P:3 * P], start=True, stop=True)
                last.then_inc(down_ready, 1)

        @block.scalar
        def _(act):
            def keep(r, p):
                act.wait_ge(turned_up, r + 1)
                act.activation(xgT[p][:, :], turned[p][:, 0:2 * P], ACT.Copy).then_inc(xgT_ready, 1)

            keep(0, 0)
            for r, p, i in pairs(act, n_pairs):
                act.wait_ge(gate_ready, r + 1)
                act.activation(sil[p][:, :], gate_up[p][:, 0:CAP], ACT.Silu).then_inc(sil_ready, 1)
                if not is_last(r, n_pairs):
                    keep(r + 1, 1 - p)

        @block.vector
        def _(dve):
            def stage(r, p):
                for k in range(2):
                    last = dve.tensor_copy(row[p][k][:, :], moe.rows[:, span(2 * r + k, 1)])
                last.then_inc(row_staged, 1)

            for r in range(ring - 1):
                stage(r, r)
            for r, p, i in pairs(dve, n_pairs, peel_first=True, by=ring):
                dve.wait_ge(sil_ready, r + 1)
                dve.tensor_tensor(h[p % 2][:, :], gate_up[p % 2][:, CAP:2 * CAP], sil[p % 2][:, :],
                                  ALU.mult).then_inc(h_ready, 1)
                if not isinstance(r, int) or r + ring - 1 < n_pairs:
                    stage(r + ring - 1, (p + ring - 1) % ring)
                dve.wait_ge(down_ready, r + 1)
                for k in range(2):
                    if reaches(r, 2):
                        dve.wait_ge(added[k], 16 * (r - 1))
                        dve.sem_inc(passed, 1)
                    dve.tensor_copy(row_out[p % 2][k][:, :], moe.rows[:, span(2 * r + k, 1)])
                    dve.tensor_scalar(y[p % 2][k][:, :], down[p % 2][k][:, 0:P],
                                      xg[p][k][:, span(P + 2 * r + k, 1)], None, ALU.mult).then_inc(y_ready, 1)


DT_LINKS = 15
Y_LINKS = 2 + 3 * TILES


def state_space(nc, x, c, wt, before=None):
    with ExitStack() as ctx:
        def sb(n, shape, dt=F32):
            return ctx.enter_context(nc.sbuf_tensor(f"ssm_{n}", shape, dt))

        def sem(n):
            return ctx.enter_context(nc.semaphore(f"ssm_{n}"))

        def bank(n):
            return ctx.enter_context(nc.psum_tensor(f"ssm_{n}", [P, 512], F32))

        KH = TILES * HEADS
        w = norm_buffers(sb, sem, "norm")
        sums = ExpertSums(sb, sem, before) if before else None
        zdt_w, in_w, tap_b, out_w, norm_col, x_bias, feature_bias, dt_bias, a_log, d_skip = (
            wt[n] for n in ("zdt_w", "in_w", "tap_b", "out_w", "norm_col", "x_bias", "feature_bias", "dt_bias",
                            "a_log", "d_skip"))
        tap_w, a_neg = sb("tap_w", [P, TAPS, 4 * P]), sb("a_neg", [P, HEADS])
        bias_part = [sb(f"bias_part{n}", [P, D_IN], BF16) for n in range(3)]
        bias_left = [sb(f"bias_left{n}", [P, D_IN]) for n in range(2)]
        bias_rows, bias_chain = sb("bias_rows", [P, D_IN], BF16), sem("bias_chain")
        xT = [sb(f"xT{p}", [P, TAPS - 1 + SEQ]) for p in range(2)]
        zx = [sb(f"zx{p}", [P, TILES, 2 * D_IN]) for p in range(2)]
        features = [[sb(f"features{p}{m}", [P, SEQ]) for m in range(2)] for p in range(2)]
        b_tok = [sb(f"b_tok{p}", [P, TILES, P]) for p in range(2)]
        v, u, s, s2, q, a = (sb(n, [P, KH]) for n in ("v", "u", "s", "s2", "q", "a"))
        dt = [sb(f"dt{p}", [P, KH]) for p in range(2)]
        acs, tot, to_end = sb("acs", [P, KH]), sb("tot", [P, KH]), sb("to_end", [P, KH])
        decayed, decay_end, chunk_decay = sb("decayed", [P, KH]), sb("decay_end", [P, KH]), sb("chunk_decay", [P, KH])
        diff = [sb(f"diff{k}", [P, HEADS, P]) for k in range(2)]
        decay = [sb(f"decay{k}", [P, HEADS, P]) for k in range(TILES)]
        cb = [sb(f"cb{k}", [P, P]) for k in range(TILES)]
        score = [sb(f"score{k}", [P, HEADS, P]) for k in range(TILES)]
        xdt, xend, xskip = (sb(n, [P, TILES, D_IN]) for n in ("xdt", "xend", "xskip"))
        state = [sb(f"state{k}", [P, D_IN]) for k in range(TILES + 1)]
        scaled = sb("scaled", [P, D_IN])
        from_state, within, ungated = (sb(n, [P, D_IN]) for n in ("from_state", "within", "ungated"))
        y = [sb(f"y{k}", [P, D_IN]) for k in range(2)]
        square = [sb(f"square{k}", [P, D_IN]) for k in range(TILES)]
        ss, ms, rms = sb("ss", [P, TILES]), sb("ms", [P, TILES]), sb("rms", [P, TILES])
        yT = [sb(f"yT{k}", [P, D_IN]) for k in range(2)]

        turned = bank("turned")
        yT_up = turned[:, 0:D_IN]
        zx_up = [bank(f"zx_up{k}") for k in range(2)]
        feature_up = (turned, zx_up[0])
        small = bank("small")
        dt_up, acs_up, tot_up, cb_up = (small[:, 0:KH], small[:, KH:2 * KH], small[:, 2 * KH:3 * KH],
                                        small[:, P:2 * P])
        rows_up = [bank(f"rows_up{k}") for k in range(2)]
        y_up = bank("y_up")
        mixed = bank("mixed")
        grow_up, out_up = mixed[:, 0:D_IN], mixed[:, D_IN:D_IN + P]

        prepared = sem("prepared")
        chain_sem, var_ready, rstd_ready, normed, turned_up, xT_ready = (
            sem("chain"), sem("var_ready"), sem("rstd_ready"), sem("normed"), sem("turned_up"), sem("xT_ready"))
        zx_multiplied, zx_ready, dt_multiplied = sem("zx_multiplied"), sem("zx_ready"), sem("dt_multiplied")
        feature_multiplied, feature_ready, b_turned, b_ready = (
            sem("feature_multiplied"), sem("feature_ready"), sem("b_turned"), sem("b_ready"))
        v_ready, u_ready, a_ready = sem("v_ready"), sem("u_ready"), sem("a_ready")
        sums_up, sums_ready, decays_ready = sem("sums_up"), sem("sums_ready"), sem("decays_ready")
        rows_ready, diff_ready, decay_ready = sem("rows_ready"), sem("diff_ready"), sem("decay_ready")
        cb_multiplied, cb_ready, score_ready = sem("cb_multiplied"), sem("cb_ready"), sem("score_ready")
        xdt_ready, x_scaled, grown, state_ready, y_multiplied, y_taken = (
            sem("xdt_ready"), sem("x_scaled"), sem("grown"), sem("state_ready"), sem("y_multiplied"),
            sem("y_taken"))
        y_ready, ss_ready, ms_ready, rms_ready = sem("y_ready"), sem("ss_ready"), sem("ms_ready"), sem("rms_ready")
        yT_turned, yT_ready, out_ready, x_done = sem("yT_turned"), sem("yT_ready"), sem("out_ready"), sem("x_done")
        y_chain, dt_chain = sem("y_chain"), sem("dt_chain")

        def heads(t):
            return t.rearrange("p (h e) -> p h e", h=HEADS)

        def per_head(t, k):
            return t[:, k * HEADS:(k + 1) * HEADS].rearrange("p (h o) -> p h o", o=1).broadcast_to([P, HEADS, HD])

        with nc.Block() as block:
            @block.scalar
            def _(act):
                act.wait_ge(wt.loaded, wt.count)
                act.activation(a_log[:, :], a_log[:, :], ACT.Exp).then_inc(prepared, 1)

            @block.vector
            def _(dve):
                for p in range(2):
                    dve.memset(xT[p][:, 0:TAPS - 1], 0.0)
                dve.memset(state[0][:, :], 0.0)
                dve.wait_ge(wt.loaded, wt.count)
                for k in range(TAPS):
                    dve.tensor_tensor(tap_w[:, k, :], in_w[:, :], tap_b[:, k, :], ALU.mult)
                for m in range(2):
                    dve.tensor_scalar(out_w[:, m, :], out_w[:, m, :], norm_col[:, m:m + 1], None, ALU.mult)
                ch = Chain(dve, bias_chain)
                left = x_bias
                for n in range(3):
                    ch.link(dve.tensor_copy(bias_part[n][:, :], left[:, :]))
                    if n < 2:
                        ch.link(dve.tensor_tensor(bias_left[n][:, :], left[:, :], bias_part[n][:, :], ALU.subtract))
                        left = bias_left[n]
                ch.link(dve.tensor_scalar(bias_rows[:, :], bias_part[0][:, :], c.ident[:, 0:1], None, ALU.mult))
                for n in range(1, 3):
                    ch.link(dve.scalar_tensor_tensor(out=bias_rows[:, :], in0=bias_part[n][:, :],
                                                     scalar=c.ident[:, n:n + 1], in1=bias_rows[:, :],
                                                     op0=ALU.mult, op1=ALU.add))
                dve.wait_ge(prepared, 1)
                dve.tensor_scalar(a_neg[:, :], a_log[:, :], -1.0, None, ALU.mult)

        block = ctx.enter_context(nc.Block())

        if sums:
            @block.sync
            def _(sp):
                sums.load(sp)

        @block.gpsimd
        def _(pool):
            def inverse_root(b, p):
                pool.wait_ge(var_ready, b + 1)
                pool.tensor_tensor(w[p].rstd[:, :], w[p].var[:, :], c.minus_half[:, :], ALU.pow
                                   ).then_inc(rstd_ready, 1)

            inverse_root(0, 0)
            inverse_root(1, 1)
            for b, p, i in pairs(pool, SEQS):
                pool.wait_ge(a_ready, b + 1)
                pool.wait_ge(zx_ready, b * TILES + TILES + 2)
                for k in range(TILES):
                    xk = heads(zx[p][:, k, D_IN:])
                    pool.tensor_tensor(heads(xdt[:, k, :]), xk, per_head(dt[p], k), ALU.mult).then_inc(xdt_ready, 1)
                    pool.tensor_tensor(heads(xskip[:, k, :]), xk,
                                       d_skip[:, :].rearrange("p (h o) -> p h o", o=1).broadcast_to([P, HEADS, HD]),
                                       ALU.mult)
                pool.wait_ge(decays_ready, b + 1)
                pool.wait_ge(xdt_ready, b * TILES + TILES)
                for k in range(TILES):
                    pool.tensor_tensor(heads(xend[:, k, :]), heads(xdt[:, k, :]), per_head(decay_end, k),
                                       ALU.mult).then_inc(x_scaled, 1)
                for k in range(TILES):
                    if k == 2 and later(b, 2):
                        inverse_root(b + 2, p)
                    pool.wait_ge(ss_ready, b * TILES + k + 1)
                    pool.tensor_tensor(ms[:, k:k + 1], ss[:, k:k + 1], c.eps[:, :], ALU.add).then_inc(ms_ready, 1)
                    pool.wait_ge(ms_ready, b * TILES + k + 1)
                    pool.tensor_tensor(rms[:, k:k + 1], ms[:, k:k + 1], c.minus_half[:, 0:1], ALU.pow
                                       ).then_inc(rms_ready, 1)

        @block.tensor
        def _(pe):
            def turn(b, p):
                pe.wait_ge(normed, b + 1)
                if reaches(b, 1):
                    pe.wait_ge(b_ready, b)
                for k in range(TILES):
                    last = pe.transpose(turned[:, k * P:(k + 1) * P], w[p].xn[:, k, :], c.ident[:, :])
                last.then_inc(turned_up, 1)

            def project_features(b, p):
                pe.wait_ge(xT_ready, b + 1)
                if reaches(b, 1):
                    pe.wait_ge(cb_ready, b * TILES + 1)
                for k in range(TILES):
                    now = slice(TAPS - 1 + k * P, TAPS - 1 + (k + 1) * P)
                    last = pe.matmul(dt_up[:, k * HEADS:(k + 1) * HEADS], xT[p][:, now], zdt_w[:, D_IN:ZDT],
                                     start=True, stop=True)
                last.then_inc(dt_multiplied, 1)
                for m in range(2):
                    if m == 1:
                        pe.wait_ge(zx_ready, b * TILES + 1)
                    for j in range(TAPS):
                        last = pe.matmul(feature_up[m][:, :], tap_w[:, j, (2 + m) * P:(3 + m) * P], xT[p][:, j:j + SEQ],
                                         start=(j == 0), stop=(j == TAPS - 1))
                    last.then_inc(feature_multiplied, 1)
                pe.wait_ge(feature_ready, 2 * b + 1)
                for k in range(TILES):
                    last = pe.transpose(turned[:, k * P:(k + 1) * P], features[p][0][:, k * P:(k + 1) * P],
                                        c.ident[:, :])
                last.then_inc(b_turned, 1)

            def project_tokens(b, p, k):
                now = slice(TAPS - 1 + k * P, TAPS - 1 + (k + 1) * P)
                pe.wait_ge(zx_ready, b * TILES + k + 1)
                if k == 0:
                    pe.wait_ge(feature_ready, 2 * b + 2)
                pe.matmul(zx_up[k % 2][:, 0:D_IN], xT[p][:, now], zdt_w[:, 0:D_IN], start=True, stop=True)
                for j in range(TAPS):
                    pe.matmul(zx_up[k % 2][:, D_IN:], xT[p][:, k * P + j:k * P + j + P],
                              tap_w[:, j, 0:D_IN], start=(j == 0), stop=False)
                pe.matmul(zx_up[k % 2][:, D_IN:], c.ones_bf[:, :], bias_rows[:, :], start=False, stop=True
                          ).then_inc(zx_multiplied, 1)

            def turn_and_project(k, n, grown_to):
                pe.wait_ge(y_ready, n + 1)
                for m in range(2):
                    last = pe.transpose(yT_up[:, m * P:(m + 1) * P], y[k % 2][:, m * P:(m + 1) * P], c.ident[:, :])
                last.then_inc(yT_turned, 1)
                pe.wait_ge(yT_ready, n + 1)
                pe.wait_ge(state_ready, grown_to)
                pe.wait_ge(x_done, n + 1)
                pe.matmul(out_up, yT[k % 2][:, 0:P], out_w[:, 0, :], start=True, stop=False)
                pe.matmul(out_up, yT[k % 2][:, P:], out_w[:, 1, :], start=False, stop=True).then_inc(out_ready, 1)

            turn(0, 0)
            project_features(0, 0)
            for k in range(TILES):
                project_tokens(0, 0, k)
            for b, p, i in pairs(pe, SEQS):
                pe.wait_ge(a_ready, b + 1)
                pe.matmul(acs_up, c.upto[:, :], a[:, :], start=True, stop=True)
                pe.matmul(tot_up, c.ones[:, :], a[:, :], start=True, stop=True).then_inc(sums_up, 1)
                for k in range(TILES):
                    n = b * TILES + k
                    pe.wait_ge(diff_ready, n + 1)
                    for h in range(HEADS):
                        last = pe.matmul(rows_up[k % 2][:, h * P:(h + 1) * P],
                                         a[:, k * HEADS + h:k * HEADS + h + 1].broadcast_to([P, P]), c.upto[:, :],
                                         start=True, stop=True)
                    last.then_inc(rows_ready, 1)
                    if k == 0:
                        pe.wait_ge(feature_ready, 2 * b + 2)
                        pe.wait_ge(sums_ready, b + 1)
                    pe.wait_ge(cb_ready, n + 1)
                    pe.matmul(cb_up, features[p][0][:, k * P:(k + 1) * P], features[p][1][:, k * P:(k + 1) * P],
                              start=True, stop=True).then_inc(cb_multiplied, 1)
                if later(b, 1):
                    turn(b + 1, 1 - p)
                    project_features(b + 1, 1 - p)
                for k in range(TILES):
                    n = b * TILES + k
                    if k == 0:
                        pe.wait_ge(b_ready, b + 1)
                    else:
                        pe.wait_ge(state_ready, n)
                        pe.wait_ge(x_done, n)
                    pe.wait_ge(x_scaled, n + 1)
                    pe.matmul(grow_up, b_tok[p][:, k, :], xend[:, k, :], start=True, stop=True).then_inc(grown, 1)
                    pe.wait_ge(score_ready, n + 1)
                    pe.wait_ge(y_taken, n + 1)
                    for h in range(HEADS):
                        pe.matmul(y_up[:, h * HD:(h + 1) * HD], score[k][:, h, :], xdt[:, k, h * HD:(h + 1) * HD],
                                  start=True, stop=True)
                    pe.matmul(y_up[:, D_IN:], features[p][1][:, k * P:(k + 1) * P], state[k][:, :],
                              start=True, stop=True).then_inc(y_multiplied, 1)
                    if k == 1 and not is_last(b, SEQS):
                        pe.wait_ge(b_ready, b + 2)
                    if k:
                        turn_and_project(k - 1, n - 1, n + 1)
                    if later(b, 1):
                        project_tokens(b + 1, 1 - p, k)
                turn_and_project(TILES - 1, b * TILES + TILES - 1, b * TILES + TILES)

        @block.scalar
        def _(act):
            def keep(b, p):
                act.wait_ge(turned_up, b + 1)
                act.activation(xT[p][:, TAPS - 1:], turned[:, :], ACT.Copy).then_inc(xT_ready, 1)

            def activate_features(b, p):
                for m in range(2):
                    act.wait_ge(feature_multiplied, 2 * b + m + 1)
                    act.activation(features[p][m][:, :], feature_up[m][:, :], ACT.Silu, bias=feature_bias[:, m:m + 1]
                                   ).then_inc(feature_ready, 1)
                act.wait_ge(b_turned, b + 1)
                act.activation(b_tok[p][:, :, :].rearrange("p a c -> p (a c)"), turned[:, :], ACT.Copy
                               ).then_inc(b_ready, 1)

            def activate_tokens(b, p, k):
                act.wait_ge(zx_multiplied, b * TILES + k + 1)
                act.activation(zx[p][:, k, :], zx_up[k % 2][:, :], ACT.Silu).then_inc(zx_ready, 1)

            def exponential(b):
                act.wait_ge(v_ready, b + 1)
                act.activation(u[:, :], q[:, :], ACT.Exp).then_inc(u_ready, 1)

            act.sem_inc(zx_ready, 2)
            act.sem_inc(decay_ready, 2)
            keep(0, 0)
            exponential(0)
            activate_features(0, 0)
            for k in range(TILES):
                activate_tokens(0, 0, k)
            for b, p, i in pairs(act, SEQS):
                act.wait_ge(sums_ready, b + 1)
                act.activation(decayed[:, :], acs[:, :], ACT.Exp)
                act.activation(decay_end[:, :], to_end[:, :], ACT.Exp)
                act.activation(chunk_decay[:, :], tot[:, :], ACT.Exp).then_inc(decays_ready, 1)
                for k in range(TILES):
                    act.wait_ge(diff_ready, b * TILES + k + 3)
                    act.activation(decay[k][:, :, :], diff[k % 2][:, :, :], ACT.Exp).then_inc(decay_ready, 1)
                if later(b, 1):
                    keep(b + 1, 1 - p)
                    exponential(b + 1)
                    activate_features(b + 1, 1 - p)
                for k in range(TILES):
                    n = b * TILES + k
                    act.wait_ge(y_ready, n + 1)
                    act.activation(square[k][:, :], y[k % 2][:, :], ACT.Square, scale=D_IN ** -0.5,
                                   accum_out=ss[:, k:k + 1]
                                   ).then_inc(ss_ready, 1)
                    act.wait_ge(yT_turned, n + 1)
                    act.activation(yT[k % 2][:, :], yT_up, ACT.Copy).then_inc(yT_ready, 1)
                    if later(b, 1):
                        activate_tokens(b + 1, 1 - p, k)

        @block.vector
        def _(dve):
            chain = Chain(dve, chain_sem, NORM_LINKS)
            dt_links = Chain(dve, dt_chain, DT_LINKS)
            link = dt_links.link

            def spread(t):
                return t[:, :].rearrange("p (o h) -> p o h", o=1).broadcast_to([P, TILES, HEADS])

            def kh(t):
                return t.rearrange("p (k h) -> p k h", h=HEADS)

            def start_time_steps(b):
                dt_links.step(b)
                dve.wait_ge(dt_multiplied, b + 1)
                link(dve.tensor_tensor(kh(v[:, :]), kh(dt_up), spread(dt_bias), ALU.add))
                dve.scalar_tensor_tensor(out=q[:, :], in0=v[:, :], scalar=-1.0, in1=v[:, :],
                                         op0=ALU.mult, op1=ALU.min).then_inc(v_ready, 1)

            def time_steps(b, p):
                dve.wait_ge(u_ready, b + 1)
                link(dve.tensor_scalar(s2[:, :], u[:, :], 2.0, None, ALU.add))
                link(dve.reciprocal(s[:, :], s2[:, :]))
                link(dve.tensor_tensor(s[:, :], s[:, :], u[:, :], ALU.mult))
                link(dve.tensor_tensor(s2[:, :], s[:, :], s[:, :], ALU.mult))
                link(dve.tensor_scalar(q[:, :], s2[:, :], 1.0 / 15.0, None, ALU.mult))
                for n in (13, 11, 9, 7, 5, 3):
                    link(dve.scalar_tensor_tensor(out=q[:, :], in0=q[:, :], scalar=1.0 / n, in1=s2[:, :],
                                                  op0=ALU.add, op1=ALU.mult))
                link(dve.scalar_tensor_tensor(out=q[:, :], in0=q[:, :], scalar=1.0, in1=s[:, :],
                                              op0=ALU.add, op1=ALU.mult))
                link(dve.tensor_scalar(q[:, :], q[:, :], 2.0, None, ALU.mult))
                link(dve.scalar_tensor_tensor(out=dt[p][:, :], in0=v[:, :], scalar=0.0, in1=q[:, :],
                                              op0=ALU.max, op1=ALU.add))
                dve.tensor_tensor(kh(a[:, :]), kh(dt[p][:, :]), spread(a_neg), ALU.mult).then_inc(a_ready, 1)

            def finish(k, n):
                dve.wait_ge(out_ready, n + 1)
                dve.wait_ge(rms_ready, n + 1)
                xs = x[:, span(n, 1), :].rearrange("p a c -> p (a c)")
                dve.scalar_tensor_tensor(out=xs, in0=out_up, scalar=rms[:, k:k + 1], in1=xs,
                                         op0=ALU.mult, op1=ALU.add).then_inc(x_done, 1)

            dve.sem_inc(diff_ready, 2)
            dve.sem_inc(cb_ready, 1)
            dve.sem_inc(x_done, 1)
            dve.sem_inc(y_taken, 1)
            if sums:
                dve.sem_inc(sums.joined, 4)
            for b in range(2):
                if sums:
                    sums.join(dve, x, b, b, 0)
                chain.step(b)
                moments(dve, chain, x, b, w[b]).then_inc(var_ready, 1)
                normalise(dve, x, b, w[b], rstd_ready).then_inc(normed, 1)
            start_time_steps(0)
            time_steps(0, 0)
            for b, p, i in pairs(dve, SEQS):
                dve.wait_ge(sums_up, b + 1)
                dve.tensor_copy(acs[:, :], acs_up).then_inc(y_chain, 1)
                dve.tensor_copy(tot[:, :], tot_up).then_inc(y_chain, 1)
                dve.wait_ge(y_chain, Y_LINKS * b + 2)
                dve.tensor_tensor(to_end[:, :], tot[:, :], acs[:, :], ALU.subtract).then_inc(sums_ready, 1)
                for k in range(TILES):
                    n = b * TILES + k
                    dve.wait_ge(rows_ready, n + 1)
                    dve.wait_ge(decay_ready, n + 1)
                    for h in range(HEADS):
                        last = dve.tensor_scalar(diff[k % 2][:, h, :], rows_up[k % 2][:, h * P:(h + 1) * P],
                                                 acs[:, k * HEADS + h:k * HEADS + h + 1], 0.0,
                                                 ALU.subtract, ALU.min)
                    last.then_inc(diff_ready, 1)
                    dve.wait_ge(cb_multiplied, n + 1)
                    dve.tensor_tensor(cb[k][:, :], cb_up, c.upto[:, :], ALU.mult).then_inc(cb_ready, 1)
                if later(b, 1):
                    start_time_steps(b + 1)
                for k in range(TILES):
                    dve.wait_ge(decay_ready, b * TILES + k + 3)
                    dve.wait_ge(cb_ready, b * TILES + k + 2)
                    dve.tensor_tensor(score[k][:, :, :], decay[k][:, :, :],
                                      cb[k][:, :].rearrange("p (o i) -> p o i", o=1).broadcast_to([P, HEADS, P]),
                                      ALU.mult).then_inc(score_ready, 1)
                if later(b, 1):
                    time_steps(b + 1, 1 - p)
                dve.wait_ge(decays_ready, b + 1)
                for k in range(TILES):
                    n = b * TILES + k
                    done = Y_LINKS * b + 2 + 3 * k
                    dve.tensor_tensor(heads(scaled[:, :]), heads(state[k][:, :]), per_head(chunk_decay, k), ALU.mult
                                      ).then_inc(y_chain, 1)
                    dve.wait_ge(y_chain, done + 1)
                    dve.wait_ge(grown, n + 1)
                    dve.tensor_tensor(state[k + 1][:, :], scaled[:, :], grow_up, ALU.add
                                      ).then_inc(state_ready, 1)
                    dve.wait_ge(y_multiplied, n + 1)
                    dve.tensor_tensor(heads(from_state[:, :]), heads(y_up[:, D_IN:]), per_head(decayed, k), ALU.mult
                                      ).then_inc(y_chain, 1)
                    dve.tensor_tensor(within[:, :], y_up[:, 0:D_IN], xskip[:, k, :], ALU.add).then_inc(y_taken, 1)
                    dve.wait_ge(y_chain, done + 2)
                    dve.wait_ge(y_taken, n + 2)
                    dve.tensor_tensor(ungated[:, :], from_state[:, :], within[:, :], ALU.add).then_inc(y_chain, 1)
                    dve.wait_ge(y_chain, done + 3)
                    dve.tensor_tensor(y[k % 2][:, :], ungated[:, :], zx[p][:, k, 0:D_IN], ALU.mult).then_inc(y_ready, 1)
                    dve.wait_ge(state_ready, n + 1)
                    if k:
                        finish(k - 1, n - 1)
                    if k == 0 and later(b, 2) and sums:
                        sums.join(dve, x, b + 2, p, i + 1)
                    if k == 1 and later(b, 2):
                        chain.step(b + 2)
                        moments(dve, chain, x, b + 2, w[p]).then_inc(var_ready, 1)
                    if k == 2 and later(b, 2):
                        normalise(dve, x, b + 2, w[p], rstd_ready).then_inc(normed, 1)
                finish(TILES - 1, b * TILES + TILES - 1)


def attention(nc, x, c, wt):
    with ExitStack() as ctx:
        def sb(n, shape, dt=F32):
            return ctx.enter_context(nc.sbuf_tensor(f"att_{n}", shape, dt))

        def sem(n):
            return ctx.enter_context(nc.semaphore(f"att_{n}"))

        def bank(n):
            return ctx.enter_context(nc.psum_tensor(f"att_{n}", [P, 512], F32))

        w = norm_buffers(sb, sem, "norm")
        xT = [sb(f"xT{p}", [P, SEQ]) for p in range(2)]
        qT = [sb(f"qT{p}", [P, SEQ]) for p in range(2)]
        qkv = [sb(f"qkv{p}", [P, TILES, 3 * P]) for p in range(2)]
        vk = [sb(f"vk{k}", [P, AH, AD, AD]) for k in range(2)]
        weighted = sb("weighted", [P, AH, AD, AD])
        inside = sb("inside", [P, P])
        state = [sb(f"state{k}", [P, P]) for k in range(TILES)]
        grown = sb("grown", [P, P])
        y = [sb(f"y{k}", [P, P]) for k in range(2)]
        yT = [sb(f"yT{k}", [P, P]) for k in range(2)]

        turned, qkv_up = bank("turned"), bank("qkv_up")
        sums_up = [[bank(f"sums_up{k}{m}") for m in range(2)] for k in range(2)]
        chunk_up, last_up = bank("chunk_up"), bank("last_up")
        grow_up, before_up = chunk_up[:, 0:P], chunk_up[:, P:2 * P]
        yT_up, out_up = last_up[:, 0:P], last_up[:, P:2 * P]

        chain_sem, var_ready, rstd_ready, normed, turned_up, xT_ready = (
            sem("chain"), sem("var_ready"), sem("rstd_ready"), sem("normed"), sem("turned_up"), sem("xT_ready"))
        qkv_multiplied, qkv_kept, qkv_ready, q_multiplied, qT_ready = (
            sem("qkv_multiplied"), sem("qkv_kept"), sem("qkv_ready"), sem("q_multiplied"), sem("qT_ready"))
        vk_ready, summed, weighted_ready, masked, state_ready = (
            sem("vk_ready"), sem("summed"), sem("weighted_ready"), sem("masked"),
            sem("state_ready"))
        inside_ready, before_ready, y_ready, yT_turned, yT_ready, out_ready, x_biased, x_done = (
            sem("inside_ready"), sem("before_ready"), sem("y_ready"), sem("yT_turned"), sem("yT_ready"),
            sem("out_ready"), sem("x_biased"), sem("x_done"))

        block = ctx.enter_context(nc.Block())

        @block.gpsimd
        def _(pool):
            def inverse_root(b, p):
                pool.wait_ge(var_ready, b + 1)
                pool.tensor_tensor(w[p].rstd[:, :], w[p].var[:, :], c.minus_half[:, :], ALU.pow
                                   ).then_inc(rstd_ready, 1)

            def add_bias(b, p, k):
                pool.wait_ge(qkv_kept, b * TILES + k + 1)
                pool.tensor_tensor(qkv[p][:, k, :], qkv[p][:, k, :], wt.qkv_bias[:, :], ALU.add
                                   ).then_inc(qkv_ready, 1)

            def add_out_bias(b):
                pool.wait_ge(normed, b + 1)
                xs = x[:, span(b * TILES, TILES), :]
                bias = wt.out_bias[:, :].rearrange("p (o c) -> p o c", o=1).broadcast_to([P, TILES, P])
                pool.tensor_tensor(xs, xs, bias, ALU.add).then_inc(x_biased, 1)

            def outer(n, p, k):
                pool.wait_ge(qkv_ready, n + 1)
                pool.wait_ge(summed, n + 1)
                shape = [P, AH, AD, AD]
                keys = qkv[p][:, k, P:2 * P].rearrange("p (h o n) -> p h o n", o=1, n=AD).broadcast_to(shape)
                values = qkv[p][:, k, 2 * P:].rearrange("p (h v o) -> p h v o", v=AD, o=1).broadcast_to(shape)
                pool.tensor_tensor(vk[k % 2][:, :, :, :], values, keys, ALU.mult).then_inc(vk_ready, 1)

            inverse_root(0, 0)
            inverse_root(1, 1)
            pool.wait_ge(wt.loaded, wt.count)
            add_bias(0, 0, 0)
            outer(0, 0, 0)
            for k in range(1, TILES):
                add_bias(0, 0, k)
            add_out_bias(0)
            for b, p, i in pairs(pool, SEQS, peel_first=True):
                for k in range(TILES):
                    if k < TILES - 1:
                        outer(b * TILES + k + 1, p, k + 1)
                    elif later(b, 1):
                        outer(b * TILES + TILES, 1 - p, 0)
                    if k == 0 and reaches(b, 1):
                        add_bias(b, p, TILES - 1)
                    if k and later(b, 1):
                        add_bias(b + 1, 1 - p, k - 1)
                    if k == 2 and later(b, 2):
                        inverse_root(b + 2, p)
                    if k == 3 and later(b, 1):
                        add_out_bias(b + 1)

        @block.tensor
        def _(pe):
            def turn_tokens(b, p):
                pe.wait_ge(normed, b + 1)
                if reaches(b, 1):
                    pe.wait_ge(qT_ready, b)
                for k in range(TILES):
                    last = pe.transpose(turned[:, k * P:(k + 1) * P], w[p].xn[:, k, :], c.ident[:, :])
                last.then_inc(turned_up, 1)

            def project_tile(b, p, k):
                if k == 0:
                    pe.wait_ge(xT_ready, b + 1)
                if k or reaches(b, 1):
                    pe.wait_ge(qkv_kept, b * TILES + k)
                pe.matmul(qkv_up[:, 0:3 * P], xT[p][:, k * P:(k + 1) * P], wt.qkv_w[:, :],
                          start=True, stop=True).then_inc(qkv_multiplied, 1)

            def project_q(p):
                pe.matmul(turned[:, :], wt.qkv_w[:, 0:P], xT[p][:, :], start=True, stop=True).then_inc(q_multiplied, 1)

            def running_sums(n, k):
                pe.wait_ge(vk_ready, n + 1)
                pe.wait_ge(weighted_ready, 2 * n + 2)
                flat = vk[k % 2][:, :, :, :].rearrange("p h v n -> p (h v n)")
                for m in range(2):
                    last = pe.matmul(sums_up[k % 2][m][:, :], c.upto[:, :], flat[:, m * 512:(m + 1) * 512],
                                     start=True, stop=True)
                last.then_inc(summed, 1)

            def turn_y(n, k):
                pe.wait_ge(y_ready, n + 1)
                pe.wait_ge(x_done, n + 1)
                pe.transpose(yT_up, y[k % 2][:, :], c.ident[:, :]).then_inc(yT_turned, 1)

            def project_out(n, k):
                pe.wait_ge(yT_ready, n + 1)
                pe.matmul(out_up, yT[k % 2][:, :], wt.out_w[:, :], start=True, stop=True).then_inc(out_ready, 1)

            pe.sem_inc(summed, 2)
            pe.wait_ge(wt.loaded, wt.count)
            turn_tokens(0, 0)
            for k in range(TILES):
                project_tile(0, 0, k)
            project_q(0)
            running_sums(0, 0)
            for b, p, i in pairs(pe, SEQS, peel_first=True):
                for k in range(TILES):
                    n = b * TILES + k
                    if k == 0 and later(b, 1):
                        turn_tokens(b + 1, 1 - p)
                    if k < TILES - 1 or later(b, 1):
                        running_sums(n + 1, k + 1)
                    if k or reaches(b, 1):
                        pe.wait_ge(y_ready, n)
                    if k < TILES - 1:
                        pe.matmul(grow_up, qkv[p][:, k, P:2 * P], qkv[p][:, k, 2 * P:], start=True, stop=True)
                    if k:
                        pe.wait_ge(state_ready, b * (TILES - 1) + k)
                    else:
                        pe.wait_ge(qT_ready, b + 1)
                    pe.matmul(before_up, qT[p][:, k * P:(k + 1) * P], state[k][:, :], start=True, stop=True
                              ).then_inc(before_ready, 1)
                    if k or reaches(b, 1):
                        turn_y(n - 1, k - 1)
                    if later(b, 1):
                        project_tile(b + 1, 1 - p, k)
                    if k or reaches(b, 1):
                        project_out(n - 1, k - 1)
                    if k == TILES - 1 and later(b, 1):
                        project_q(1 - p)
            turn_y(NT - 1, TILES - 1)
            project_out(NT - 1, TILES - 1)

        @block.scalar
        def _(act):
            def keep_features(b, p):
                act.wait_ge(turned_up, b + 1)
                act.activation(xT[p][:, :], turned[:, :], ACT.Copy).then_inc(xT_ready, 1)

            def keep_tile(b, p, k):
                act.wait_ge(qkv_multiplied, b * TILES + k + 1)
                act.activation(qkv[p][:, k, :], qkv_up[:, 0:3 * P], ACT.Copy).then_inc(qkv_kept, 1)

            def keep_q(b, p):
                act.wait_ge(q_multiplied, b + 1)
                act.activation(qT[p][:, :], turned[:, :], ACT.Identity, bias=wt.q_bias[:, 0:1]).then_inc(qT_ready, 1)

            def keep_y(n, k):
                act.wait_ge(yT_turned, n + 1)
                act.activation(yT[k % 2][:, :], yT_up, ACT.Copy).then_inc(yT_ready, 1)

            keep_features(0, 0)
            for k in range(TILES):
                keep_tile(0, 0, k)
            act.wait_ge(wt.loaded, wt.count)
            keep_q(0, 0)
            for b, p, i in pairs(act, SEQS, peel_first=True):
                for k in range(TILES):
                    if k == 0 and later(b, 1):
                        keep_features(b + 1, 1 - p)
                    if k or reaches(b, 1):
                        keep_y(b * TILES + k - 1, k - 1)
                    if later(b, 1):
                        keep_tile(b + 1, 1 - p, k)
                    if k == TILES - 1 and later(b, 1):
                        keep_q(b + 1, 1 - p)
            keep_y(NT - 1, TILES - 1)

        @block.vector
        def _(dve):
            chain = Chain(dve, chain_sem, NORM_LINKS)

            def finish(n):
                dve.wait_ge(out_ready, n + 1)
                xs = x[:, span(n, 1), :].rearrange("p a c -> p (a c)")
                dve.tensor_tensor(xs, xs, out_up, ALU.add).then_inc(x_done, 1)

            dve.sem_inc(weighted_ready, 4)
            dve.sem_inc(x_done, 1)
            dve.memset(state[0][:, :], 0.0)
            for b in range(2):
                chain.step(b)
                moments(dve, chain, x, b, w[b]).then_inc(var_ready, 1)
                normalise(dve, x, b, w[b], rstd_ready).then_inc(normed, 1)
            for b, p, i in pairs(dve, SEQS, peel_first=True):
                for k in range(TILES):
                    n = b * TILES + k
                    dve.wait_ge(summed, n + 3)
                    half = [P, AH // 2, AD, AD]
                    for m in range(2):
                        queries = qkv[p][:, k, m * P // 2:(m + 1) * P // 2].rearrange(
                            "p (h o n) -> p h o n", o=1, n=AD).broadcast_to(half)
                        dve.tensor_tensor(weighted[:, m * AH // 2:(m + 1) * AH // 2, :, :],
                                          sums_up[k % 2][m][:, :].rearrange("p (h v n) -> p h v n", v=AD, n=AD),
                                          queries, ALU.mult).then_inc(weighted_ready, 1)
                    dve.wait_ge(before_ready, n + 1)
                    if k < TILES - 1:
                        g = b * (TILES - 1) + k
                        dve.tensor_tensor(grown[:, :], grow_up, c.head_block[:, :], ALU.mult).then_inc(masked, 1)
                        dve.wait_ge(masked, g + 1)
                        dve.tensor_tensor(state[k + 1][:, :], state[k][:, :], grown[:, :], ALU.add
                                          ).then_inc(state_ready, 1)
                    dve.wait_ge(weighted_ready, 2 * n + 6)
                    dve.tensor_reduce(inside[:, :].rearrange("p (h v) -> p h v", v=AD), weighted[:, :, :, :],
                                      AX_X, ALU.add).then_inc(inside_ready, 1)
                    dve.wait_ge(inside_ready, n + 1)
                    dve.tensor_tensor(y[k % 2][:, :], before_up, inside[:, :], ALU.add).then_inc(y_ready, 1)
                    if k or reaches(b, 1):
                        if k == 1:
                            dve.wait_ge(x_biased, b + 1)
                        finish(n - 1)
                    if k == 0 and later(b, 2):
                        chain.step(b + 2)
                        moments(dve, chain, x, b + 2, w[p]).then_inc(var_ready, 1)
                    if k == 2 and later(b, 2):
                        normalise(dve, x, b + 2, w[p], rstd_ready).then_inc(normed, 1)
            finish(NT - 1)


def start(nc, c, d, x, tables, sums, x_loaded, cleared, ints_loaded, others):
    tokens, early = d["u"].rearrange("(a p) c -> p a c", p=P), 2 * TILES
    first = [(x[:, 0:early, :], tokens[:, 0:early, :]),
             (c.gate_w[:, :], d["gate"]), (c.bias[:, :], d["bias"].rearrange("(o e) -> o e", o=1).broadcast_to([P, E])),
             (c.shared_g[:, :], d["shared_gate"]), (c.shared_u[:, :], d["shared_up"]),
             (c.shared_d[:, 0, :], d["shared_down"])]
    ints = [(c.q_i[0][:, :], d["ffn_gate"]), (c.q_i[1][:, :], d["ffn_up"]), (c.q_i[2][:, :], d["ffn_down"])]
    third = (T + CAP) // P // 3
    zeros = [(t[T:T + CAP, :], c.zeros[:, 0:ROW]) for t in tables] + [
        (s[k * third * P:(k + 1) * third * P, :].rearrange("(p a) c -> p (a c)", p=P), c.zeros[:, 0:third * P])
        for s in sums for k in range(3)]
    with nc.semaphore("start_loaded") as loaded, nc.semaphore("start_zeroed") as zeroed, \
            nc.semaphore("const_made") as made, nc.semaphore("const_masked") as masked, nc.Block() as block:
        @block.sync
        def _(sp):
            for dst, src in first:
                sp.dma_start(dst, src).then_inc(loaded, 16)
            sp.wait_ge(loaded, 16 * len(first))

        @block.scalar
        def _(act):
            act.dma_start(x[:, early:, :], tokens[:, early:, :]).then_inc(x_loaded, 16)
            act.wait_ge(zeroed, 1)
            for dst, src in ints:
                act.dma_start(dst, src).then_inc(ints_loaded, 16)
            for landed, plan in others:
                for dst, src in plan:
                    act.dma_start(dst, src).then_inc(landed, 16)
            for dst, src in zeros:
                act.dma_start(dst, src).then_inc(cleared, 16)

        @block.gpsimd
        def _(pool):
            ch = Chain(pool, made)
            ch.link(pool.memset(c.ident[:, :], 0.0))
            ch.link(pool.affine_select(out=c.ident[:, :], in_=c.ident[:, :], compare_op=ALU.not_equal, fill=1.0,
                                       base=0, pattern=[[-1, P]], channel_multiplier=1))
            ch.link(pool.memset(c.ones[:, :], 1.0))
            ch.link(pool.memset(c.ones_bf[:, :], 1.0))
            ch.link(pool.affine_select(out=c.before_bf[:, :], in_=c.ones_bf[:, :], compare_op=ALU.is_gt, fill=0.0,
                                       base=0, pattern=[[1, P]], channel_multiplier=-1))
            ch.link(pool.affine_select(out=c.upto[:, :], in_=c.ones[:, :], compare_op=ALU.is_ge, fill=0.0,
                                       base=0, pattern=[[1, P]], channel_multiplier=-1))
            ch.link(pool.memset(c.earlier_group[:, :, :], 1.0))
            ch.link(pool.affine_select(out=c.earlier_group[:, :, :], in_=c.earlier_group[:, :, :],
                                       compare_op=ALU.is_gt, fill=0.0, base=0,
                                       pattern=[[1, GROUPS], [-1, GROUPS]], channel_multiplier=0))
            ch.link(pool.iota(c.ramp_i[:, :], pattern=[[1, LO]], base=0, channel_multiplier=0))
            ch.link(pool.tensor_copy(c.lo_digit[:, :], c.ramp_i[:, :]))
            ch.link(pool.iota(c.part_i[:, :], pattern=[[0, 1]], base=1, channel_multiplier=1))
            ch.link(pool.tensor_copy(c.part1[:, :], c.part_i[:, :]))
            ch.link(pool.iota(c.tile_i[:, :], pattern=[[P, NT]], base=0, channel_multiplier=0))
            ch.link(pool.tensor_copy(c.tile128[:, :], c.tile_i[:, :]))
            ch.link(pool.iota(c.slot_i[:, :], pattern=[[0, LO]], base=0, channel_multiplier=1))
            ch.link(pool.memset(c.head_block[:, :], 1.0))
            hb = c.head_block[:, :].rearrange("p (h d) -> p h d", d=AD)
            ch.link(pool.affine_select(out=hb, in_=hb, compare_op=ALU.is_ge, fill=0.0,
                                       base=0, pattern=[[-AD, AH], [0, AD]], channel_multiplier=1))
            ch.link(pool.affine_select(out=hb, in_=hb, compare_op=ALU.is_ge, fill=0.0,
                                       base=AD - 1, pattern=[[AD, AH], [0, AD]], channel_multiplier=-1))

        @block.vector
        def _(dve):
            dve.memset(c.zeros[:, :], 0.0).then_inc(zeroed, 1)
            dve.memset(c.zero_bf[:, :], 0.0)
            dve.memset(c.minus_half[:, :], -0.5)
            dve.memset(c.eps[:, :], EPS)
            dve.wait_ge(made, 15)
            dve.tensor_reduce(c.own[:, :], c.ident[:, :].rearrange("p (h e) -> p e h", e=EG), AX_X, ALU.add)
            dve.tensor_scalar(c.slot_m[:, :], c.slot_i[:, :], P - EG, None, ALU.bitwise_and).then_inc(masked, 1)
            dve.wait_ge(masked, 1)
            dve.scalar_tensor_tensor(out=c.empty_row[:, :], in0=c.slot_m[:, :], scalar=float(T + 1),
                                     in1=c.lo_digit[:, :], op0=ALU.add, op1=ALU.add)

    return 16 * len(zeros), 16 * len(ints)


def cast_integers(nc, c, ints_loaded, count):
    with nc.Block() as block:
        @block.vector
        def _(dve):
            dve.wait_ge(ints_loaded, count)
            for q, f in zip(c.q_i, c.q_f):
                dve.tensor_copy(f[:, :, :].rearrange("p a c -> p (a c)"), q[:, :])


def mamba_weights(sb, sem, d):
    wt = Bag()
    for n, shape in (("zdt_w", [P, ZDT]), ("in_w", [P, 4 * P]), ("tap_b", [P, TAPS, 4 * P]), ("out_w", [P, 2, P]),
                     ("norm_col", [P, 2]), ("x_bias", [P, D_IN]), ("feature_bias", [P, 2]), ("dt_bias", [P, HEADS]),
                     ("a_log", [P, HEADS]), ("d_skip", [P, HEADS])):
        wt[n] = sb(f"ssm_{n}", shape, F32)
    plan = [(wt.zdt_w[:, :], d["in_zdt"]), (wt.in_w[:, :], d["in_xbc"]),
            (wt.tap_b[:, :, :].rearrange("p k c -> p (k c)"),
             d["conv_w"].rearrange("(o c) -> o c", o=1).broadcast_to([P, TAPS * 4 * P])),
            (wt.out_w[:, :, :], d["out_w"].rearrange("(m p) o -> p m o", p=P)),
            (wt.norm_col[:, :], d["norm_w"]),
            (wt.x_bias[:, :], d["conv_b"][0:D_IN].rearrange("(o c) -> o c", o=1).broadcast_to([P, D_IN])),
            (wt.feature_bias[:, :], d["feature_b"])] + [
        (t[:, :], d[n].rearrange("(o h) -> o h", o=1).broadcast_to([P, HEADS]))
        for t, n in ((wt.dt_bias, "dt_bias"), (wt.a_log, "A_log"), (wt.d_skip, "D"))]
    wt.loaded, wt.plan, wt.count = sem("ssm_loaded"), plan, 16 * len(plan)
    return wt


def attention_weights(sb, sem, d):
    wt = Bag()
    for n, shape in (("qkv_w", [P, 3 * P]), ("qkv_bias", [P, 3 * P]), ("q_bias", [P, 1]), ("out_w", [P, P]),
                     ("out_bias", [P, P])):
        wt[n] = sb(f"att_{n}", shape, F32)
    plan = [(wt.qkv_w[:, :], d["qkv_w"]), (wt.q_bias[:, :], d["qkv_b"][0:P].rearrange("(p o) -> p o", o=1)),
            (wt.qkv_bias[:, :], d["qkv_b"].rearrange("(o c) -> o c", o=1).broadcast_to([P, 3 * P])),
            (wt.out_w[:, :], d["att_out_w"]),
            (wt.out_bias[:, :], d["att_out_b"].rearrange("(o c) -> o c", o=1).broadcast_to([P, P]))]
    wt.loaded, wt.plan, wt.count = sem("att_loaded"), plan, 16 * len(plan)
    return wt


def clear_semaphores(nc):
    used = sorted(int(n) for n in nc.released_uncleared_semaphores)
    runs = []
    for n in used:
        if runs and runs[-1][1] == n:
            runs[-1][1] = n + 1
        else:
            runs.append([n, n + 1])
    with nc.Block() as block:
        @block.gpsimd
        def _(pool):
            for first, end in runs:
                pool.sem_clear(range(first, end))


def finish(nc, x, out, background):
    with nc.semaphore("out_written") as written, nc.Block() as block:
        @block.sync
        def _(sp):
            if out is not None:
                sp.dma_start(out.rearrange("(a p) c -> p a c", p=P), x[:, :, :]).then_inc(written, 16)
                sp.wait_ge(written, 16)
            for sem, count in background:
                sp.wait_ge(sem, count)


def program(nc, d, out, layers):
    with ExitStack() as ctx:
        def sb(n, shape, dt):
            return ctx.enter_context(nc.sbuf_tensor(n, shape, dt))

        c = Bag()
        x = sb("x", [P, NT, P], F32)
        for n, shape, dt in (
                ("minus_half", [P, TILES], F32), ("eps", [P, 1], F32), ("ident", [P, P], F32), ("ones", [P, P], F32), ("upto", [P, P], F32),
                ("ones_bf", [P, P], BF16), ("before_bf", [P, P], BF16), ("zero_bf", [P, EG * LO], BF16),
                ("earlier_group", [P, GROUPS, GROUPS], BF16), ("ramp_i", [P, LO], I32),
                ("lo_digit", [P, LO], BF16), ("part_i", [P, 1], I32),
                ("part1", [P, 1], F32), ("tile_i", [P, NT], I32), ("tile128", [P, NT], F32),
                ("own", [P, EG], F32), ("slot_i", [P, LO], I32), ("slot_m", [P, LO], I32),
                ("empty_row", [P, LO], F32), ("head_block", [P, P], F32),
                ("gate_w", [P, E], F32), ("bias", [P, E], F32), ("shared_g", [P, P], F32),
                ("shared_u", [P, P], F32), ("shared_d", [P, 1, P], F32)):
            c[n] = sb(n, shape, dt)
        c.q_f = [sb(f"q_f{k}", [P, HM, P], F32) for k in range(3)]

        def dram(n, shape, dt=F32):
            return nc.dram_tensor(n, shape, dt, kind="Internal").ap()

        tables = [dram(f"table{k}", (T + CAP, ROW)) for k in range(2)]
        sums = [[dram(f"sums{k}_{j}", (T + CAP, P)) for j in range(CHAINS)] for k in range(2)]
        lists = [dram(f"row_list{k}", (E * CAP,)) for k in range(2)]
        c.zeros = sb("zeros", [P, (T + CAP) // P // 3 * P], F32)
        c.q_i = [sb(f"q_i{k}", [P, HM * P], I32) for k in range(3)]
        cleared = ctx.enter_context(nc.semaphore("cleared"))
        ints_loaded = ctx.enter_context(nc.semaphore("ints_loaded"))
        x_loaded = ctx.enter_context(nc.semaphore("x_loaded"))

        def sem(n):
            return ctx.enter_context(nc.semaphore(n))

        mamba, att = mamba_weights(sb, sem, d), attention_weights(sb, sem, d)
        zeros_done, ints_done = start(nc, c, d, x, tables, [s for pair in sums for s in pair], x_loaded, cleared,
                                      ints_loaded,
                                      [(wt.loaded, wt.plan) for wt in (mamba, att)])

        gathered, added = ([[ctx.enter_context(nc.semaphore(f"experts{k}_{n}{p}")) for p in range(many)]
                            for k in range(2)] for n, many in (("gathered", 4), ("added", CHAINS)))

        def moe_layer(k):
            with nc.sbuf_tensor(f"moe{k}_logits", [P, NT, E], F32) as logits, \
                    nc.sbuf_tensor(f"moe{k}_rows", [P, E], U32) as rows:
                moe = Bag()
                moe.gathered, moe.added = gathered[k], added[k]
                moe.cleared, moe.zeros_done, moe.x_loaded = cleared, zeros_done, x_loaded
                moe.logits, moe.rows = logits, rows
                moe.gate, moe.bias, moe.table, moe.sums = c.gate_w, c.bias, tables[k], sums[k]
                moe.row_list, moe.w123 = lists[k], d["w123"]
                ffn_layer(nc, f"shared{k}", sb, x, c, (c.shared_g, c.shared_u, c.shared_d), 1, 1.0, 0.5, moe)
                route(nc, f"route{k}", c, moe)
                experts(nc, f"experts{k}", c, moe)
                return moe

        def quant_layer(k, before, out=None):
            wg, wu, wd = c.q_f
            ffn_layer(nc, f"ffn{k}", sb, x, c, (wg[:, :, :].rearrange("p a c -> p (a c)"),
                      wu[:, :, :].rearrange("p a c -> p (a c)"), wd), HM, QSCALE, 0.5 * QSCALE, before=before,
                      out=out)

        moe = None
        for what in layers:
            if what == "moe0":
                moe = moe_layer(0)
            if what == "mamba":
                state_space(nc, x, c, mamba, moe)
                moe = None
            if what == "moe1":
                moe = moe_layer(1)
                clear_semaphores(nc)
            if what == "ffn0":
                cast_integers(nc, c, ints_loaded, ints_done)
                quant_layer(0, moe)
            if what == "attention":
                attention(nc, x, c, att)
            if what == "ffn1":
                quant_layer(1, None, out)
        finish(nc, x, None if layers[-1] == "ffn1" else out, [(cleared, zeros_done), (ints_loaded, ints_done), (mamba.loaded, mamba.count),
                           (att.loaded, att.count)])


LAYERS = ("moe0", "mamba", "moe1", "ffn0", "attention", "ffn1")


def kernel(**inputs):
    import numpy as np
    import concourse.bacc as bacc
    from concourse.bass_utils import run_bass_kernel_spmd

    def turned(a):
        return np.ascontiguousarray(np.asarray(a).T)

    w1, w2, w3 = (np.asarray(inputs[f"L0_ffn_{n}"]) for n in ("w1", "w2", "w3"))
    n_pairs = E // 2
    up1, up3 = (w.reshape(n_pairs, P, P).transpose(0, 2, 1) for w in (w1, w3))
    down2 = w2.transpose(0, 2, 1).reshape(n_pairs, P, P)
    arrays = {
        "u": np.ascontiguousarray(np.asarray(inputs["L0_attn_u"]).reshape(T, P)),
        "gate": turned(inputs["L0_ffn_gate_weight"]),
        "bias": np.ascontiguousarray(inputs["L0_ffn_e_bias"]),
        "w123": np.ascontiguousarray(np.concatenate([up1, up3, down2], axis=2)),
        "shared_gate": turned(inputs["L0_ffn_shared_gate"]),
        "shared_up": turned(inputs["L0_ffn_shared_up"]),
        "shared_down": turned(inputs["L0_ffn_shared_down"]),
        "ffn_gate": turned(inputs["L1_ffn_w_gate"]),
        "ffn_up": turned(inputs["L1_ffn_w_up"]),
        "ffn_down": np.ascontiguousarray(
            turned(inputs["L1_ffn_w_down"]).reshape(HM, P, P).transpose(1, 0, 2).reshape(P, HM * P)),
    }
    in_w, conv_b = np.asarray(inputs["L0_attn_in_proj_w"]), np.asarray(inputs["L0_attn_conv_b"])
    arrays |= {
        "in_zdt": turned(np.concatenate([in_w[:D_IN], in_w[D_IN + 4 * P:]])),
        "in_xbc": turned(in_w[D_IN:D_IN + 4 * P]),
        "conv_w": turned(inputs["L0_attn_conv_w"]).reshape(-1),
        "conv_b": np.ascontiguousarray(conv_b),
        "feature_b": turned(conv_b[D_IN:].reshape(2, P)),
        "dt_bias": np.ascontiguousarray(inputs["L0_attn_dt_bias"]),
        "A_log": np.ascontiguousarray(inputs["L0_attn_A_log"]),
        "D": np.ascontiguousarray(inputs["L0_attn_D"]),
        "norm_w": turned(np.asarray(inputs["L0_attn_norm_w"]).reshape(2, P)),
        "out_w": turned(inputs["L0_attn_out_proj_w"]),
        "qkv_w": turned(np.concatenate([np.asarray(inputs[f"L1_attn_W{n}"]) for n in "qkv"])),
        "qkv_b": np.concatenate([np.asarray(inputs[f"L1_attn_b{n}"]) for n in "qkv"]),
        "att_out_w": turned(inputs["L1_attn_Wo"]),
        "att_out_b": np.ascontiguousarray(inputs["L1_attn_bo"]),
    }
    nc = bacc.Bacc("TRN2", target_bir_lowering=False, num_devices=1)
    d = {n: nc.dram_tensor(f"in_{n}", a.shape, mybir.dt.from_np(a.dtype), kind="ExternalInput").ap()
         for n, a in arrays.items()}
    out = nc.dram_tensor("out", (T, P), F32, kind="ExternalOutput").ap()
    program(nc, d, out, LAYERS)
    r = run_bass_kernel_spmd(nc, [{f"in_{n}": a for n, a in arrays.items()}], core_ids=[0])
    return r.results[0]["out"].reshape(SEQS, SEQ, P)
```
